# Optimizing a Trainium2 kernel written in Bass

```python
import numpy as np
import jax
import jax.numpy as jnp

def _softmax(x, axis=-1):
    return jax.nn.softmax(x, axis=axis)

def _gelu(x):
    return jax.nn.gelu(x, approximate=True)

def _silu(x):
    return jax.nn.silu(x)

def _sigmoid(x):
    return jax.nn.sigmoid(x)

def _layernorm(x, axis=-1, eps=1e-05):
    m = jnp.mean(x, axis=axis, keepdims=True)
    v = jnp.var(x, axis=axis, keepdims=True)
    return (x - m) / jnp.sqrt(v + eps)

def _scatter_add(tgt, idx, src, axis=0):
    return tgt.at[idx].add(src)

def _segment_sum(src, seg, n):
    return jax.ops.segment_sum(src, seg, n)
kernel_name = 'mk_seq_preln_d2_jaxref_r8_240685'

def setup_inputs(seed: int=0):
    np.random.seed(seed)
    _w = jnp.asarray

    def _L0_attn_setup():
        import jax, jax.numpy as jnp
        import numpy as np
        B, S, D = (2, 256, 512)
        H = 32
        HD = D // H
        THETA = 10000.0

        def _rope_cos_sin(seq_len, head_dim, theta=THETA):
            inv = 1.0 / theta ** (np.arange(0, head_dim, 2)[:head_dim // 2].astype(np.float32) / head_dim)
            t = np.arange(seq_len)
            f = np.outer(t, inv).astype(np.float32)
            return (jnp.asarray(np.cos(f)), jnp.asarray(np.sin(f)))

        def _apply_rotary(x, cos, sin):
            xr = x.astype(jnp.float32).reshape(*x.shape[:-1], HD // 2, 2)
            x0, x1 = (xr[..., 0], xr[..., 1])
            c = cos[None, :, None, :]
            s = sin[None, :, None, :]
            o0 = x0 * c - x1 * s
            o1 = x0 * s + x1 * c
            return jnp.stack((o0, o1), axis=-1).reshape(*x.shape[:-1], HD)
        key = jax.random.key(seed)
        ks = jax.random.split(key, 5)
        std = 0.02
        return {'x': jax.random.normal(ks[0], (B, S, D), dtype=jnp.float32), 'wq': jax.random.normal(ks[1], (D, D), dtype=jnp.float32) * std, 'wk': jax.random.normal(ks[2], (D, D), dtype=jnp.float32) * std, 'wv': jax.random.normal(ks[3], (D, D), dtype=jnp.float32) * std, 'wo': jax.random.normal(ks[4], (D, D), dtype=jnp.float32) * std}
    _L0_attn_in = _L0_attn_setup()

    def _L0_ffn_setup():
        import jax, jax.numpy as jnp
        import numpy as np
        H = 512
        I = 1792
        G = 128

        def dequant(q, s, g=G):
            O, In = q.shape
            return (q.reshape(O, In // g, g).astype(s.dtype) * s[:, :, None]).reshape(O, In)
        key = jax.random.key(seed)
        ks = jax.random.split(key, 7)
        x = jax.random.normal(ks[0], (2, 256, H), dtype=jnp.float32)

        def mk_qlinear(kq, ksc, out_d, in_d):
            q = jax.random.randint(kq, (out_d, in_d), -8, 8, dtype=jnp.int32)
            s = jax.random.uniform(ksc, (out_d, in_d // G), dtype=jnp.float32, minval=0.005, maxval=0.02)
            return (q, s)
        gate_q, gate_s = mk_qlinear(ks[1], ks[2], I, H)
        up_q, up_s = mk_qlinear(ks[3], ks[4], I, H)
        down_q, down_s = mk_qlinear(ks[5], ks[6], H, I)
        return {'x': x, 'gate_q': gate_q, 'gate_s': gate_s, 'up_q': up_q, 'up_s': up_s, 'down_q': down_q, 'down_s': down_s}
    _L0_ffn_in = _L0_ffn_setup()

    def _L1_attn_setup():
        import jax, jax.numpy as jnp
        import numpy as np
        B, T, H, S, F, G = (2, 256, 512, 128, 1248, 6)
        GRAD_ORDER_MIN = 4
        THD = 2.5
        key = jax.random.key(seed)
        ks = jax.random.split(key, 9)
        sc = 0.02
        hidden_states = jax.random.normal(ks[0], (B, T, H), jnp.float32)
        up_w = jax.random.normal(ks[1], (S, H), jnp.float32) * sc
        gate_w = jax.random.normal(ks[2], (S, H), jnp.float32) / np.sqrt(H)
        local_point = jax.random.normal(ks[3], (S,), jnp.float32)
        local_approx_output = jax.random.normal(ks[4], (H, S), jnp.float32) * sc
        fuse_weight = jax.random.normal(ks[5], (H, S, G), jnp.float32) * sc
        discount_factor = jnp.asarray(np.cumsum(np.log(np.arange(1, G + 1, dtype=np.float64))), jnp.float32)
        ffn_gate_w = jax.random.normal(ks[6], (F, H), jnp.float32) * sc
        ffn_up_w = jax.random.normal(ks[7], (F, H), jnp.float32) * sc
        ffn_down_w = jax.random.normal(ks[8], (H, F), jnp.float32) * sc
        return {'hidden_states': hidden_states, 'up_w': up_w, 'gate_w': gate_w, 'local_point': local_point, 'local_approx_output': local_approx_output, 'fuse_weight': fuse_weight, 'discount_factor': discount_factor, 'ffn_gate_w': ffn_gate_w, 'ffn_up_w': ffn_up_w, 'ffn_down_w': ffn_down_w}
    _L1_attn_in = _L1_attn_setup()

    def _L1_ffn_setup():
        import jax, jax.numpy as jnp
        import numpy as np
        B_, S, D = (4, 512, 512)
        E, R, O = (8, 16, 512)
        TOP_K = 2
        SCALING = 8.0 / R
        key = jax.random.key(seed)
        ks = jax.random.split(key, 5)
        x = jax.random.normal(ks[0], (B_, S, D), dtype=jnp.float32)
        router_w = jax.random.normal(ks[1], (E, D), dtype=jnp.float32) * (1.0 / np.sqrt(D))
        router_b = jax.random.normal(ks[2], (E,), dtype=jnp.float32) * 0.01
        A = jax.random.normal(ks[3], (E, R, D), dtype=jnp.float32) * (1.0 / np.sqrt(D))
        Bm = jax.random.normal(ks[4], (E, O, R), dtype=jnp.float32) * 0.02
        return {'x': x, 'router_w': router_w, 'router_b': router_b, 'A': A, 'Bm': Bm}
    _L1_ffn_in = _L1_ffn_setup()
    _d = {'L0_attn_x': _L0_attn_in['x'], 'L0_attn_wq': _L0_attn_in['wq'], 'L0_attn_wk': _L0_attn_in['wk'], 'L0_attn_wv': _L0_attn_in['wv'], 'L0_attn_wo': _L0_attn_in['wo'], 'L0_ffn_gate_q': _L0_ffn_in['gate_q'], 'L0_ffn_gate_s': _L0_ffn_in['gate_s'], 'L0_ffn_up_q': _L0_ffn_in['up_q'], 'L0_ffn_up_s': _L0_ffn_in['up_s'], 'L0_ffn_down_q': _L0_ffn_in['down_q'], 'L0_ffn_down_s': _L0_ffn_in['down_s'], 'L1_attn_up_w': _L1_attn_in['up_w'], 'L1_attn_gate_w': _L1_attn_in['gate_w'], 'L1_attn_local_point': _L1_attn_in['local_point'], 'L1_attn_local_approx_output': _L1_attn_in['local_approx_output'], 'L1_attn_fuse_weight': _L1_attn_in['fuse_weight'], 'L1_attn_discount_factor': _L1_attn_in['discount_factor'], 'L1_attn_ffn_gate_w': _L1_attn_in['ffn_gate_w'], 'L1_attn_ffn_up_w': _L1_attn_in['ffn_up_w'], 'L1_attn_ffn_down_w': _L1_attn_in['ffn_down_w'], 'L1_ffn_router_w': _L1_ffn_in['router_w'], 'L1_ffn_router_b': _L1_ffn_in['router_b'], 'L1_ffn_A': _L1_ffn_in['A'], 'L1_ffn_Bm': _L1_ffn_in['Bm']}
    _x0 = _d['L0_attn_x']
    _d['L0_attn_x'] = jax.random.normal(jax.random.fold_in(jax.random.key(seed), 1), (8, 256, 512), dtype=_x0.dtype)
    del _x0
    return _d

def reference(L0_attn_x, L0_attn_wq, L0_attn_wk, L0_attn_wv, L0_attn_wo, L0_ffn_gate_q, L0_ffn_gate_s, L0_ffn_up_q, L0_ffn_up_s, L0_ffn_down_q, L0_ffn_down_s, L1_attn_up_w, L1_attn_gate_w, L1_attn_local_point, L1_attn_local_approx_output, L1_attn_fuse_weight, L1_attn_discount_factor, L1_attn_ffn_gate_w, L1_attn_ffn_up_w, L1_attn_ffn_down_w, L1_ffn_router_w, L1_ffn_router_b, L1_ffn_A, L1_ffn_Bm):

    def _L0_attn_ref(x, wq, wk, wv, wo):
        import jax, jax.numpy as jnp
        import numpy as np
        B, S, D = (2, 256, 512)
        H = 32
        HD = D // H
        THETA = 10000.0

        def _rope_cos_sin(seq_len, head_dim, theta=THETA):
            inv = 1.0 / theta ** (np.arange(0, head_dim, 2)[:head_dim // 2].astype(np.float32) / head_dim)
            t = np.arange(seq_len)
            f = np.outer(t, inv).astype(np.float32)
            return (jnp.asarray(np.cos(f)), jnp.asarray(np.sin(f)))

        def _apply_rotary(x, cos, sin):
            xr = x.astype(jnp.float32).reshape(*x.shape[:-1], HD // 2, 2)
            x0, x1 = (xr[..., 0], xr[..., 1])
            c = cos[None, :, None, :]
            s = sin[None, :, None, :]
            o0 = x0 * c - x1 * s
            o1 = x0 * s + x1 * c
            return jnp.stack((o0, o1), axis=-1).reshape(*x.shape[:-1], HD)
        b, s, d = x.shape
        q = (x @ wq).reshape(b, s, H, HD)
        k = (x @ wk).reshape(b, s, H, HD)
        v = (x @ wv).reshape(b, s, H, HD)
        cos, sin = _rope_cos_sin(s, HD)
        q = _apply_rotary(q, cos, sin)
        k = _apply_rotary(k, cos, sin)
        scale = 1.0 / jnp.sqrt(jnp.float32(HD))
        scores = jnp.einsum('bqhd,bkhd->bhqk', q, k) * scale
        causal = jnp.tril(jnp.ones((s, s), dtype=bool))
        scores = jnp.where(causal[None, None], scores, jnp.finfo(scores.dtype).min)
        probs = jax.nn.softmax(scores, axis=-1)
        out = jnp.einsum('bhqk,bkhd->bqhd', probs, v).reshape(b, s, d)
        return out @ wo

    def _L0_ffn_ref(x, gate_q, gate_s, up_q, up_s, down_q, down_s):
        import jax, jax.numpy as jnp
        import numpy as np
        H = 512
        I = 1792
        G = 128

        def dequant(q, s, g=G):
            O, In = q.shape
            return (q.reshape(O, In // g, g).astype(s.dtype) * s[:, :, None]).reshape(O, In)
        Wg = dequant(gate_q, gate_s)
        Wu = dequant(up_q, up_s)
        Wd = dequant(down_q, down_s)
        gate_score = jax.nn.silu(jnp.einsum('bsh,ih->bsi', x, Wg))
        intermediate = gate_score * jnp.einsum('bsh,ih->bsi', x, Wu)
        return jnp.einsum('bsi,hi->bsh', intermediate, Wd)

    def _L1_attn_ref(hidden_states, up_w, gate_w, local_point, local_approx_output, fuse_weight, discount_factor, ffn_gate_w, ffn_up_w, ffn_down_w):
        import jax, jax.numpy as jnp
        import numpy as np
        B, T, H, S, F, G = (2, 256, 512, 128, 1248, 6)
        GRAD_ORDER_MIN = 4
        THD = 2.5
        approx_up = hidden_states @ up_w.T
        gate_pre = hidden_states @ gate_w.T
        delta = gate_pre - local_point
        neg_factor = jnp.where(delta > 0, 1.0, -1.0).astype(hidden_states.dtype)
        delta_abs = jnp.abs(delta)
        log_delta = jnp.log(delta_abs)
        keep = (delta_abs <= THD).astype(hidden_states.dtype)
        approx_out = approx_up @ local_approx_output.T
        for idx in range(G):
            m = idx + 1
            dterm = jnp.exp(log_delta * m - discount_factor[idx])
            if m % 2 == 1:
                dterm = dterm * neg_factor
            tmp = dterm * approx_up
            if m > GRAD_ORDER_MIN:
                tmp = tmp * keep
            approx_out = approx_out + tmp @ fuse_weight[:, :, idx].T
        ffn_out = jax.nn.silu(hidden_states @ ffn_gate_w.T) * (hidden_states @ ffn_up_w.T) @ ffn_down_w.T
        return approx_out + ffn_out

    def _L1_ffn_ref(x, router_w, router_b, A, Bm):
        import jax, jax.numpy as jnp
        import numpy as np
        B_, S, D = (4, 512, 512)
        E, R, O = (8, 16, 512)
        TOP_K = 2
        SCALING = 8.0 / R
        flat = x.reshape(-1, x.shape[-1])
        N = flat.shape[0]
        logits = flat @ router_w.T + router_b
        probs = jax.nn.softmax(logits, axis=-1)
        topv, topi = jax.lax.top_k(probs, TOP_K)
        gates = topv / jnp.sum(topv, axis=-1, keepdims=True)
        w = jnp.zeros((N, E), dtype=flat.dtype).at[jnp.arange(N)[:, None], topi].add(gates)
        h = jnp.einsum('nd,erd->ner', flat, A)
        hw = h * w[:, :, None]
        out = jnp.einsum('ner,eor->no', hw, Bm) * SCALING
        return out.reshape(*x.shape[:-1], O)
    x = L0_attn_x
    x = x + _L0_attn_ref(_layernorm(x, axis=-1), L0_attn_wq, L0_attn_wk, L0_attn_wv, L0_attn_wo)
    x = x + _L0_ffn_ref(_layernorm(x, axis=-1), L0_ffn_gate_q, L0_ffn_gate_s, L0_ffn_up_q, L0_ffn_up_s, L0_ffn_down_q, L0_ffn_down_s)
    x = x + _L1_attn_ref(_layernorm(x, axis=-1), L1_attn_up_w, L1_attn_gate_w, L1_attn_local_point, L1_attn_local_approx_output, L1_attn_fuse_weight, L1_attn_discount_factor, L1_attn_ffn_gate_w, L1_attn_ffn_up_w, L1_attn_ffn_down_w)
    x = x + _L1_ffn_ref(_layernorm(x, axis=-1), L1_ffn_router_w, L1_ffn_router_b, L1_ffn_A, L1_ffn_Bm)
    return x

_drawn_inputs = setup_inputs


def setup_inputs(seed=0):
    import zlib

    import numpy as np

    out = dict(_drawn_inputs(seed))
    spreads = {}
    factors = {'L0_attn_wq': 6.939,
     'L0_attn_wk': 6.931,
     'L1_ffn_router_w': 7.108,
     'L1_ffn_router_b': 42.66,
     'L1_ffn_A': 6.194,
     'L1_ffn_Bm': 6.187}
    for name, (base, spread) in spreads.items():
        noise = np.random.default_rng([zlib.crc32(name.encode()), seed]).standard_normal(out[name].shape)
        drawn = base * np.exp(spread * noise) if base else spread * noise
        out[name] = jnp.asarray(drawn.astype(out[name].dtype))
    for name, factor in factors.items():
        out[name] = (out[name] * factor).astype(out[name].dtype)
    return out
```

```python
from contextlib import ExitStack

import concourse.bass as bass
from concourse import mybir

F32 = mybir.dt.float32
F32R = mybir.dt.float32r
BF16 = mybir.dt.bfloat16
I32 = mybir.dt.int32
U32 = mybir.dt.uint32
ALU = mybir.AluOpType
ACT = mybir.ActivationFunctionType
AXX = mybir.AxisListType.X

P = 128
D = 512
KT = D // P
B, S = 8, 256
TOK = B * S
NT = TOK // P
TPB = S // P
H, HD = 32, 16
NPAIR = H // 2
UNITS = H // 4
F0 = 1792
F1 = 1280
G = 6
E8, R16 = 8, 16
EPS = 1e-5
THD = 2.5
NEG = -3.0e38


class Chain:

    def __init__(self, eng, sem, base, tick=None):
        self.eng, self.sem, self.base, self.tick, self.n = eng, sem, base, tick, 0

    def __call__(self, ins, alone=False):
        self.n += 1
        ins.then_inc(self.sem, 1)
        self.eng.wait_ge(self.sem, self.base + self.n)
        if alone:
            self.eng.sem_inc(self.tick, 1)


def wait_alone(eng, sem, value, tick):
    eng.wait_ge(sem, value)
    eng.sem_inc(tick, 1)


def three_pass(nc, out, lhs, rhs, first, last):
    nc.tensor.matmul(out, lhs[0], rhs[0], start=first, stop=False)
    nc.tensor.matmul(out, lhs[0], rhs[1], start=False, stop=False)
    return nc.tensor.matmul(out, lhs[1], rhs[0], start=False, stop=last)


def alloc(nc, ctx):
    def sb(name, shape, dt=F32):
        return ctx.enter_context(nc.sbuf_tensor(name, shape, dt))

    def sem(name):
        return ctx.enter_context(nc.semaphore(name))

    return sb, sem


def attention_phase(nc, X, PB, ident, x_in, wqkvo, rope_in, mask_in, ident_in):
    with ExitStack() as ctx:
        sb, sem = alloc(nc, ctx)
        WH = sb("WH", [P, 4, KT, D], F32R)
        WL = sb("WL", [P, 4, KT, D], F32R)
        XTH = sb("aXTH", [P, KT, S], F32R)
        XTL = sb("aXTL", [P, KT, S], F32R)
        V = sb("V", [P, TPB, H, 32])
        XN = sb("XN", [P, TPB, D])
        RA = sb("RA", [P, D])
        RB = sb("RB", [P, D])
        STK = sb("STK", [P, 2, 16, 4, HD], F32R)
        QT = sb("QT", [P, NPAIR, S], F32R)
        KTT = sb("KTT", [P, NPAIR, 2, S], F32R)
        PR = sb("PR", [P, 3, D])
        PT = sb("PT", [P, 2, 4, 384])
        OT = sb("OT", [P, 2, S])
        AO = sb("AO", [P, TPB, D])
        rope = sb("rope", [P, 4, TPB, HD])
        maskf = sb("maskf", [P, P])
        maskb = sb("maskb", [P, P], BF16)
        identb = sb("identb", [P, P], BF16)
        ident_r = sb("ident_r", [P, P], F32R)
        st = sb("st", [P, TPB, 6])
        mv = sb("mv", [P, TPB, 2])
        ve = sb("ve", [P, TPB])
        half = sb("half", [P, TPB])
        rstd = sb("rstd", [P, TPB])
        mx = sb("mx", [P, 3, 4])
        nmx = sb("nmx", [P, 3, 4])
        rden = sb("rden", [P, 2, TPB, 4])
        WRAW = [X[:, 4 * w + 4:4 * w + 8, :] for w in range(3)]
        WRAW.append(V[:, :, :, :].rearrange("p t h d -> p (t h d)").rearrange("p (k n) -> p k n", k=KT))

        s_cst, s_w, s_x = sem("s_cst"), sem("s_w"), sem("s_x")
        s_whi, s_wlo, s_zero, s_cd = sem("s_whi"), sem("s_wlo"), sem("s_zero"), sem("s_cd")
        s_chain, s_tick, s_sptick = sem("s_chain"), sem("s_tick"), sem("s_sptick")
        s_ve, s_pow = sem("s_ve"), sem("s_pow")
        s_xn = sem("s_xn")
        mm_full = [sem(f"mm_full{i}") for i in range(2)]
        mm_free = [sem(f"mm_free{i}") for i in range(2)]
        sc_full = [sem(f"sc_full{i}") for i in range(3)]
        sc_free = [sem(f"sc_free{i}") for i in range(3)]
        pt_full = [sem(f"pt_full{i}") for i in range(3)]
        pt_free = [sem(f"pt_free{i}") for i in range(3)]
        s_mx = sem("s_mx")
        s_xth = sem("s_xth")
        s_qkv, s_rb, s_rr = sem("s_qkv"), sem("s_rb"), sem("s_rr")
        s_hi, s_lo = sem("s_hi"), sem("s_lo")
        s_ka, s_ath = sem("s_ka"), sem("s_ath")

        USES = {}
        for t in range(TPB):
            USES["xt", t] = len(USES)
        for t in range(TPB):
            for w in range(2):
                for g in range(4):
                    USES["stk", t, w, g] = len(USES)
        for u in range(UNITS):
            USES["pv", u] = len(USES)
            USES["otT", u] = len(USES)
        for t in range(TPB):
            USES["at", t] = len(USES)
        for t in range(TPB):
            USES["o", t] = len(USES)
        NU = len(USES) // 2
        assert len(USES) % 2 == 0

        def mm_bank(*key):
            return PB[USES[key] % 2]

        def wait_mm(eng, i, *key):
            eng.wait_ge(mm_full[USES[key] % 2], i * NU + (USES[key] // 2 + 1))

        def wait_freed(eng, i, *key):
            eng.wait_ge(mm_free[USES[key] % 2], i * NU + (USES[key] // 2 + 2))

        def free_mm(ins, *key):
            return ins.then_inc(mm_free[USES[key] % 2], 1)

        block = ctx.enter_context(nc.Block())

        @block.sync
        def _(sp):
            sp.dma_start(ident[:, :], ident_in).then_inc(s_cst, 16)
            sp.dma_start(maskf[:, :], mask_in).then_inc(s_cst, 16)
            sp.dma_start(rope[:, :, :, :], rope_in).then_inc(s_cst, 16)
            sp.dma_start(X[:, 0:TPB, :], x_in[0]).then_inc(s_x, 16)
            for w in range(4):
                sp.dma_start(WRAW[w], wqkvo[w]).then_inc(s_w, 16)
            sp.wait_ge(s_x, 16)
            sp.wait_ge(s_wlo, 4)
            with sp.Fori(1, B) as i:
                sp.dma_start(X[:, bass.ds(i * TPB, TPB), :],
                             x_in[bass.ds(i, 1)].rearrange("a p t n -> p (a t) n")).then_inc(s_x, 16)
                wait_alone(sp, s_x, i * 16 + 16, s_sptick)

        @block.gpsimd
        def _(pool):
            nc.gpsimd.memset(half[:, :], -0.5).then_inc(s_cd, 1)
            pool.wait_ge(s_cd, 1)
            pool.wait_ge(s_wlo, 4)
            nc.gpsimd.memset(V[:, :, :, HD:32], 1.0).then_inc(s_zero, 1)
            with pool.Fori(0, B) as i:
                pool.wait_ge(s_ve, i + 1)
                nc.gpsimd.tensor_tensor(rstd[:, :], ve[:, :], half[:, :], ALU.pow).then_inc(s_pow, 1)
                for n in range(2 * TPB):
                    pool.wait_ge(s_rb, i * 4 + n + 1)
                    nc.gpsimd.tensor_tensor(RA[:, :], RA[:, :], RB[:, :], ALU.add).then_inc(s_rr, 1)

        @block.scalar
        def _(act):
            act.wait_ge(s_w, 64)
            for w in range(4):
                nc.scalar.copy(WH[:, w, :, :], WRAW[w]).then_inc(s_whi, 1)
            act.wait_ge(s_cst, 48)
            nc.scalar.copy(identb[:, :], ident[:, :]).then_inc(s_zero, 1)
            nc.scalar.copy(ident_r[:, :], ident[:, :]).then_inc(s_zero, 1)
            nc.scalar.copy(maskb[:, :], maskf[:, :]).then_inc(s_zero, 1)
            with act.Fori(0, B) as i:
                for t in range(TPB):
                    wait_mm(act, i, "xt", t)
                    nc.scalar.copy(XTH[:, :, t * P:(t + 1) * P],
                                   mm_bank("xt", t)[:, :].rearrange("p (k n) -> p k n", k=KT)).then_inc(s_xth, 1)
                def evacuate(n):
                    t, w = n // 4, n // 2 % 2
                    for g in (2 * (n % 2), 2 * (n % 2) + 1):
                        wait_mm(act, i, "stk", t, w, g)
                        bank = mm_bank("stk", t, w, g)
                        if w == 0:
                            free_mm(nc.scalar.copy(
                                QT[:, 4 * g:4 * g + 4, t * P:(t + 1) * P],
                                bank[:, :].rearrange("p (a n) -> p a n", a=4)), "stk", t, w, g)
                        else:
                            nc.scalar.copy(
                                KTT[0:64, 4 * g:4 * g + 4, 0, t * P:(t + 1) * P],
                                bank[0:64, :].rearrange("p (a n) -> p a n", a=4)).then_inc(s_ka, 1)

                for n in range(8):
                    t, w, hh = n // 4, n // 2 % 2, n % 2
                    if hh == 0:
                        act.wait_ge(s_rr, i * 4 + n // 2 + 1)
                    if n >= 2:
                        m = n - 2
                        wait_mm(act, i, "stk", m // 4, m // 2 % 2, 2 * (m % 2) + 1)
                    src = RA[:, hh * 256:(hh + 1) * 256].rearrange("p (h a d) -> p h a d", a=1, d=HD)
                    dst = STK[:, n % 2, :, 0:2, :] if w == 0 else STK[:, n % 2, :, 0:4:2, :]
                    nc.scalar.copy(dst, src.to_broadcast([P, 16, 2, HD])).then_inc(s_hi, 1)
                    if n:
                        evacuate(n - 1)
                    if w == 1 and hh == 1:
                        act.wait_ge(s_qkv, i * 6 + t * 3 + 3)
                        nc.scalar.copy(V[:, t, :, 0:HD], PB[4 + 3 * t][:, :].rearrange("p (h d) -> p h d", h=H))
                evacuate(7)

                def exp_job(n):
                    u, j = n // 3, n % 3
                    act.wait_ge(s_mx, i * 24 + n + 1)
                    act.wait_ge(pt_full[j], i * 8 + u + 1)
                    heads = 4 if j == 0 else 2
                    w = D // heads
                    for h in range(heads):
                        ins = nc.scalar.activation(PR[:, j, h * w:(h + 1) * w], PB[2 + j][:, h * w:(h + 1) * w],
                                                   ACT.Exp, bias=nmx[:, j, h:h + 1])
                    ins.then_inc(sc_free[j], 1)

                for n in range(3):
                    exp_job(n)
                for n in range(3 * UNITS + 1):
                    if n + 3 < 3 * UNITS:
                        exp_job(n + 3)
                    if n % 3 == 0 and n:
                        u = n // 3 - 1
                        wait_mm(act, i, "pv", u)
                        free_mm(nc.scalar.copy(OT[:, u % 2, :], mm_bank("pv", u)[:, 0:S]), "pv", u)
                for t in range(TPB):
                    wait_mm(act, i, "at", t)
                    nc.scalar.copy(XTH[:, :, t * P:(t + 1) * P],
                                   mm_bank("at", t)[:, :].rearrange("p (k n) -> p k n", k=KT)).then_inc(s_ath, 1)

        @block.vector
        def _(dve):
            for w in range(4):
                dve.wait_ge(s_whi, w + 1)
                nc.vector.tensor_tensor(WL[:, w, :, :], WRAW[w], WH[:, w, :, :].bitcast(F32),
                                        ALU.subtract).then_inc(s_wlo, 1)
            dve.wait_ge(s_wlo, 4)
            nc.vector.memset(KTT[:, :, :, :].bitcast(U32), 0).then_inc(s_wlo, 1)
            dve.wait_ge(s_wlo, 5)
            dve.wait_ge(s_cst, 48)
            with dve.Fori(0, B) as i:
                link = Chain(dve, s_chain, i * 10, s_tick)
                dve.wait_ge(s_x, i * 16 + 16)
                for t in range(TPB):
                    ins = nc.vector.bn_stats(st[:, t, :], X[:, bass.ds(i * TPB + t, 1), :].rearrange("p a n -> p (a n)"))
                link(ins, alone=True)
                for t in range(TPB):
                    ins = nc.vector.bn_aggr(mv[:, t, :], st[:, t, :])
                link(ins)
                nc.vector.tensor_scalar(ve[:, :], mv[:, :, 1], EPS, None, ALU.add).then_inc(s_ve, 1)
                dve.wait_ge(s_pow, i + 1)
                for t in range(TPB):
                    nc.vector.tensor_scalar(XN[:, t, :], X[:, bass.ds(i * TPB + t, 1), :].rearrange("p a n -> p (a n)"),
                                            mv[:, t, 0:1], rstd[:, t:t + 1],
                                            ALU.subtract, ALU.mult).then_inc(s_xn, 1)
                for t in range(TPB):
                    dve.wait_ge(s_xth, i * 2 + t + 1)
                    free_mm(nc.vector.tensor_tensor(
                        XTL[:, :, t * P:(t + 1) * P],
                        mm_bank("xt", t)[:, :].rearrange("p (k n) -> p k n", k=KT),
                        XTH[:, :, t * P:(t + 1) * P].bitcast(F32), ALU.subtract), "xt", t)
                def upper_keys(n):
                    t = n // 4
                    if n // 2 % 2 == 1:
                        for g in (2 * (n % 2), 2 * (n % 2) + 1):
                            dve.wait_ge(s_ka, i * 8 + t * 4 + g + 1)
                            free_mm(nc.vector.tensor_copy(
                                KTT[64:P, 4 * g:4 * g + 4, 1, t * P:(t + 1) * P],
                                mm_bank("stk", t, 1, g)[64:P, :].rearrange("p (a n) -> p a n", a=4)),
                                "stk", t, 1, g)

                for t in range(TPB):
                    for w in range(2):
                        c = t * 2 + w
                        dve.wait_ge(s_qkv, i * 6 + t * 3 + w + 1)
                        bank = PB[2 + 3 * t + w]
                        cos = rope[:, 2 * w, t:t + 1, :].to_broadcast([P, H, HD])
                        sin = rope[:, 2 * w + 1, t, :].rearrange("p (a k e) -> p a k e", a=1, e=2)
                        q4 = bank[:, :].rearrange("p (h k e) -> p h k e", h=H, e=2)
                        b4 = RB[:, :].rearrange("p (h k e) -> p h k e", h=H, e=2)
                        if c:
                            dve.wait_ge(s_lo, i * 8 + c * 2)
                        nc.vector.tensor_tensor(RA[:, :].rearrange("p (h d) -> p h d", h=H),
                                                bank[:, :].rearrange("p (h d) -> p h d", h=H), cos, ALU.mult)
                        nc.vector.tensor_tensor(b4[:, :, :, 0], q4[:, :, :, 1],
                                                sin[:, :, :, 0].to_broadcast([P, H, 8]), ALU.mult)
                        nc.vector.tensor_tensor(b4[:, :, :, 1], q4[:, :, :, 0],
                                                sin[:, :, :, 1].to_broadcast([P, H, 8]), ALU.mult).then_inc(s_rb, 1)
                        for hh in range(2):
                            n = c * 2 + hh
                            dve.wait_ge(s_hi, i * 8 + n + 1)
                            src = RA[:, hh * 256:(hh + 1) * 256].rearrange("p (h a d) -> p h a d", a=1, d=HD)
                            hi = STK[:, n % 2, :, 0:1, :].bitcast(F32)
                            dst = STK[:, n % 2, :, 2:4, :] if w == 0 else STK[:, n % 2, :, 1:4:2, :]
                            nc.vector.tensor_tensor(dst, src.to_broadcast([P, 16, 2, HD]),
                                                    hi.to_broadcast([P, 16, 2, HD]), ALU.subtract).then_inc(s_lo, 1)
                            if n:
                                upper_keys(n - 1)
                upper_keys(7)

                def max_job(n):
                    u, j = n // 3, n % 3
                    heads = 4 if j == 0 else 2
                    dve.wait_ge(sc_full[j], i * 8 + u + 1)
                    dve.wait_ge(sc_free[j], i * 8 + u + 1)
                    nc.vector.tensor_reduce(nmx[:, j, 0:heads], PB[2 + j][:, :].rearrange("p (h n) -> p h n", h=heads),
                                            axis=AXX, op=ALU.max, negate=True).then_inc(s_mx, 1)

                def probs_job(n):
                    u, j = n // 3, n % 3
                    dve.wait_ge(pt_full[j], i * 8 + u + 2)
                    if u >= 2 and j == 0:
                        wait_mm(dve, i, "pv", u - 2)
                    if j == 0:
                        dst = PT[:, u % 2, :, 0:P]
                        src = PB[5][:, :].rearrange("p (h n) -> p h n", h=4)
                    else:
                        dst = PT[:, u % 2, 2 * j - 2:2 * j, P:384]
                        src = PB[5 + j][:, :].rearrange("p (h n) -> p h n", h=2)
                    nc.vector.tensor_copy(dst, src).then_inc(pt_free[j], 1)

                for n in range(3):
                    max_job(n)
                for n in range(3 * UNITS + 2):
                    if n < 3 * UNITS:
                        probs_job(n)
                    if n + 3 < 3 * UNITS:
                        max_job(n + 3)
                    if n % 3 == 1 and n > 1:
                        u = n // 3 - 1
                        wait_mm(dve, i, "otT", u)
                        v = mm_bank("otT", u)[:, 0:S].rearrange("p (t h d) -> p t h d", t=TPB, h=4)
                        link(nc.vector.reciprocal(rden[:, u % 2, :, :], v[:, :, :, HD]))
                        free_mm(nc.vector.tensor_tensor(
                            AO[:, :, u * 64:(u + 1) * 64].rearrange("p t (h d) -> p t h d", h=4), v[:, :, :, 0:HD],
                            rden[:, u % 2, :, :].unsqueeze(3).to_broadcast([P, TPB, 4, HD]), ALU.mult),
                            "otT", u)
                for t in range(TPB):
                    dve.wait_ge(s_ath, i * 2 + t + 1)
                    free_mm(nc.vector.tensor_tensor(
                        XTL[:, :, t * P:(t + 1) * P],
                        mm_bank("at", t)[:, :].rearrange("p (k n) -> p k n", k=KT),
                        XTH[:, :, t * P:(t + 1) * P].bitcast(F32), ALU.subtract), "at", t)
                for t in range(TPB):
                    wait_mm(dve, i, "o", t)
                    x = X[:, bass.ds(i * TPB + t, 1), :].rearrange("p a n -> p (a n)")
                    free_mm(nc.vector.tensor_tensor(x, x, mm_bank("o", t)[:, :], ALU.add), "o", t)

        @block.tensor
        def _(pe):
            for s in mm_free:
                pe.sem_inc(s, 1)
            for s in sc_free + pt_free + pt_full:
                pe.sem_inc(s, 1)
            pe.wait_ge(s_wlo, 5)
            pe.wait_ge(s_zero, 4)
            with pe.Fori(0, B) as i:
                def take_mm(*key):
                    pe.wait_ge(mm_free[USES[key] % 2], i * NU + (USES[key] // 2 + 1))
                    return mm_bank(*key)

                def give_mm(ins, *key):
                    return ins.then_inc(mm_full[USES[key] % 2], 1)

                for t in range(TPB):
                    pe.wait_ge(s_xn, i * 2 + t + 1)
                    bank = take_mm("xt", t)
                    for k in range(KT):
                        ins = nc.tensor.transpose(bank[:, k * P:(k + 1) * P], XN[:, t, k * P:(k + 1) * P], ident[:, :])
                    give_mm(ins, "xt", t)
                for t in range(TPB):
                    wait_freed(pe, i, "xt", t)
                    for w in range(3):
                        bank = PB[2 + 3 * t + w]
                        for k in range(KT):
                            ins = three_pass(nc, bank[:, :],
                                             (XTH[:, k, t * P:(t + 1) * P], XTL[:, k, t * P:(t + 1) * P]),
                                             (WH[:, w, k, :], WL[:, w, k, :]), k == 0, k == KT - 1)
                        ins.then_inc(s_qkv, 1)
                for t in range(TPB):
                    for w in range(2):
                        for g in range(4):
                            n = (t * 2 + w) * 2 + g // 2
                            pe.wait_ge(s_lo, i * 8 + n + 1)
                            bank = take_mm("stk", t, w, g)
                            for a in range(4):
                                c = (g % 2) * 8 + 2 * a
                                ins = nc.tensor.transpose(
                                    bank[:, a * P:(a + 1) * P].bitcast(F32R),
                                    STK[:, n % 2, c:c + 2, :, :].rearrange("p h a d -> p (h a d)"), ident_r[:, :])
                            give_mm(ins, "stk", t, w, g)

                def score_job(n):
                    u, j = n // 3, n % 3
                    bank = PB[2 + j]
                    pe.wait_ge(sc_free[j], i * 8 + u + 1)
                    if j == 0:
                        nc.tensor.matmul(bank[:, :].rearrange("p (h n) -> p h n", h=4), identb[:, :],
                                         maskb[:, :].unsqueeze(1).to_broadcast([P, 4, P]), start=True, stop=False)
                        for a in range(2):
                            ins = nc.tensor.matmul(
                                bank[:, a * 256:(a + 1) * 256].rearrange("p (h n) -> p h n", h=2),
                                QT[:, 2 * u + a, 0:P], KTT[:, 2 * u + a, :, 0:P], start=False, stop=a == 1)
                    else:
                        p = 2 * u + j - 1
                        nc.tensor.matmul(bank[:, :].rearrange("p (h n) -> p h n", h=2),
                                         QT[:, p, P:S], KTT[:, p, :, :], start=True, stop=False)
                        ins = nc.tensor.matmul(
                            bank[:, :].rearrange("p (h n) -> p h n", h=2)[:, :, P:S], identb[:, :],
                            maskb[:, :].unsqueeze(1).to_broadcast([P, 2, P]), start=False, stop=True)
                    ins.then_inc(sc_full[j], 1)

                def turn_job(n):
                    u, j = n // 3, n % 3
                    pe.wait_ge(sc_free[j], i * 8 + u + 2)
                    pe.wait_ge(pt_free[j], i * 8 + u + 1)
                    for a in range(4):
                        ins = nc.tensor.transpose(PB[5 + j][:, a * P:(a + 1) * P], PR[:, j, a * P:(a + 1) * P], ident[:, :])
                    ins.then_inc(pt_full[j], 1)

                for w in range(2):
                    for g in (2, 3):
                        wait_freed(pe, i, "stk", 1, w, g)
                for n in range(3):
                    score_job(n)
                for n in range(3 * UNITS + 2):
                    if n < 3 * UNITS:
                        turn_job(n)
                    if n + 3 < 3 * UNITS:
                        score_job(n + 3)
                    if n % 3 == 0 and n:
                        u = n // 3 - 1
                        for j in range(3):
                            pe.wait_ge(pt_free[j], i * 8 + u + 2)
                        bank = take_mm("pv", u)
                        for h in range(4):
                            o = bank[32 * h:32 * h + 32, 0:S]
                            nc.tensor.matmul(o, V[:, 0, 4 * u + h, :], PT[:, u % 2, h, 0:S], start=True, stop=False,
                                             tile_position=(0, 32 * h))
                        for h in range(4):
                            ins = nc.tensor.matmul(bank[32 * h:32 * h + 32, P:S], V[:, 1, 4 * u + h, :],
                                                   PT[:, u % 2, h, S:384], start=False, stop=True,
                                                   tile_position=(0, 32 * h))
                        give_mm(ins, "pv", u)
                    if n % 3 == 1 and n > 1:
                        u = n // 3 - 1
                        wait_freed(pe, i, "pv", u)
                        bank = take_mm("otT", u)
                        for t in range(TPB):
                            ins = nc.tensor.transpose(bank[:, t * P:(t + 1) * P], OT[:, u % 2, t * P:(t + 1) * P], ident[:, :])
                        give_mm(ins, "otT", u)
                wait_freed(pe, i, "otT", UNITS - 1)
                for t in range(TPB):
                    bank = take_mm("at", t)
                    for k in range(KT):
                        ins = nc.tensor.transpose(bank[:, k * P:(k + 1) * P], AO[:, t, k * P:(k + 1) * P], ident[:, :])
                    give_mm(ins, "at", t)
                for t in range(TPB):
                    wait_freed(pe, i, "at", t)
                    bank = take_mm("o", t)
                    for k in range(KT):
                        ins = three_pass(nc, bank[:, :],
                                         (XTH[:, k, t * P:(t + 1) * P], XTL[:, k, t * P:(t + 1) * P]),
                                         (WH[:, 3, k, :], WL[:, 3, k, :]), k == 0, k == KT - 1)
                    give_mm(ins, "o", t)


def norm_phase(nc, X, PB, ident, XTH, XTL, tag):
    with ExitStack() as ctx:
        sb, sem = alloc(nc, ctx)
        XN = sb(f"nXN{tag}", [P, 4, D])
        st = sb(f"nst{tag}", [P, 4, 6])
        mv = sb(f"nmv{tag}", [P, 4, 2])
        ve = sb(f"nve{tag}", [P, 4])
        half = sb(f"nhalf{tag}", [P, 4])
        rstd = sb(f"nrstd{tag}", [P, 4])
        s_half, s_chain, s_tick, s_ve, s_pow = (sem(f"n{x}{tag}") for x in ("half", "chain", "tick", "ve", "pow"))
        s_xn, s_xp, s_hi, s_lo = (sem(f"n{x}{tag}") for x in ("xn", "xp", "hi", "lo"))
        block = ctx.enter_context(nc.Block())

        @block.gpsimd
        def _(pool):
            nc.gpsimd.memset(half[:, :], -0.5).then_inc(s_half, 1)
            pool.wait_ge(s_half, 1)
            with pool.Fori(0, NT // 4) as i:
                pool.wait_ge(s_ve, i + 1)
                nc.gpsimd.tensor_tensor(rstd[:, :], ve[:, :], half[:, :], ALU.pow).then_inc(s_pow, 1)

        @block.vector
        def _(dve):
            with dve.Fori(0, NT // 4) as i:
                link = Chain(dve, s_chain, i * 2, s_tick)
                x = X[:, bass.ds(i * 4, 4), :]
                for t in range(4):
                    ins = nc.vector.bn_stats(st[:, t, :], x[:, t, :])
                link(ins, alone=True)
                for t in range(4):
                    ins = nc.vector.bn_aggr(mv[:, t, :], st[:, t, :])
                link(ins)
                nc.vector.tensor_scalar(ve[:, :], mv[:, :, 1], EPS, None, ALU.add).then_inc(s_ve, 1)
                dve.wait_ge(s_pow, i + 1)
                for t in range(4):
                    nc.vector.tensor_scalar(XN[:, t, :], x[:, t, :], mv[:, t, 0:1], rstd[:, t:t + 1],
                                            ALU.subtract, ALU.mult).then_inc(s_xn, 1)
                for t in range(4):
                    dve.wait_ge(s_hi, i * 4 + t + 1)
                    cols = bass.ds(i * 512 + t * P, P)
                    nc.vector.tensor_tensor(XTL[:, :, cols], PB[t][:, :].rearrange("p (k n) -> p k n", k=KT),
                                            XTH[:, :, cols].bitcast(F32), ALU.subtract).then_inc(s_lo, 1)

        @block.scalar
        def _(act):
            with act.Fori(0, NT // 4) as i:
                for t in range(4):
                    act.wait_ge(s_xp, i * 4 + t + 1)
                    nc.scalar.copy(XTH[:, :, bass.ds(i * 512 + t * P, P)],
                                   PB[t][:, :].rearrange("p (k n) -> p k n", k=KT)).then_inc(s_hi, 1)

        @block.tensor
        def _(pe):
            with pe.Fori(0, NT // 4) as i:
                for t in range(4):
                    pe.wait_ge(s_xn, i * 4 + t + 1)
                    for k in range(KT):
                        ins = nc.tensor.transpose(PB[t][:, k * P:(k + 1) * P], XN[:, t, k * P:(k + 1) * P], ident[:, :])
                    ins.then_inc(s_xp, 1)


def swiglu_phase(nc, X, PB, XTH, XTL, F, gu_in, d_in, gu_scale, d_scale, tag):
    quant = gu_scale is not None
    C = F // 256
    with ExitStack() as ctx:
        sb, sem = alloc(nc, ctx)
        GUH = sb(f"GUH{tag}", [P, 2, 2, KT, P], F32R)
        GUL = sb(f"GUL{tag}", [P, 2, 2, KT, P], F32R)
        DH = sb(f"DH{tag}", [P, 2, D], F32R)
        DL = sb(f"DL{tag}", [P, 2, D], F32R)
        raw = sb(f"raw{tag}", [P, 3, 1024], I32 if quant else F32)
        w32 = sb(f"w32{tag}", [P, 1024]) if quant else None
        scl = sb(f"scl{tag}", [P, 3, 1024]) if quant else None
        HH = sb(f"HH{tag}", [P, 6, D], F32R)
        HL = sb(f"HL{tag}", [P, 6, D], F32R)
        SG = sb(f"SG{tag}", [P, 2, D])
        HF = sb(f"HF{tag}", [P, 2, D])
        s_raw = [sem(f"raw{n}{tag}") for n in range(3)]
        s_cvt, s_mul, s_whi = sem(f"cvt{tag}"), sem(f"mul{tag}"), sem(f"whi{tag}")
        s_w = sem(f"w{tag}")
        s_gu, s_silu, s_h, s_hhi, s_hlo = (sem(f"{x}{tag}") for x in ("gu", "silu", "h", "hhi", "hlo"))
        s_dn, s_xadd, s_sptick = sem(f"dn{tag}"), sem(f"xadd{tag}"), sem(f"sptick{tag}")
        block = ctx.enter_context(nc.Block())
        ORDER = [("gu", 0, 0), ("gu", 0, 1), ("gu", 0, 2), ("gu", 0, 3), ("gu", 1, 0), ("gu", 1, 1), ("dn", 0),
                 ("gu", 1, 2), ("dn", 1), ("gu", 1, 3), ("dn", 2), ("dn", 3)]

        def looped(eng, body):
            with eng.Fori(0, C - 1) as i:
                body(i, True)
            body(C - 1, False)

        def fetch(sp, c, slot):
            one = bass.ds(c, 1)
            if slot < 2:
                src = gu_in[one, slot].rearrange("a p n -> (a p) n")
            else:
                src = d_in[one].rearrange("a p n -> (a p) n")
            sp.dma_start(raw[:, slot, :], src).then_inc(s_raw[slot], 16)
            if quant:
                s = (gu_scale[one, slot] if slot < 2 else d_scale[one]).to_broadcast([P, 1024])
                sp.dma_start(scl[:, slot, :], s).then_inc(s_raw[slot], 16)

        per = 32 if quant else 16

        @block.sync
        def _(sp):
            for slot in (0, 1, 2):
                fetch(sp, 0, slot)
            with sp.Fori(0, C - 1) as i:
                for slot in (0, 1, 2):
                    wait_alone(sp, s_w, i * 3 + slot + 1, s_sptick)
                    fetch(sp, i + 1, slot)

        @block.gpsimd
        def _(pool):
            def body(i, _):
                for slot in range(3):
                    hi = GUH[:, slot] if slot < 2 else DH[:, :, :]
                    lo = GUL[:, slot] if slot < 2 else DL[:, :, :]
                    pat = "p a k n -> p (a k n)" if slot < 2 else "p k n -> p (k n)"
                    src = raw[:, slot, :]
                    if quant:
                        pool.wait_ge(s_cvt, i * 3 + slot + 1)
                        nc.gpsimd.tensor_tensor(w32[:, :], w32[:, :], scl[:, slot, :], ALU.mult).then_inc(s_mul, 1)
                        src = w32[:, :]
                    pool.wait_ge(s_whi, i * 3 + slot + 1)
                    nc.gpsimd.tensor_tensor(lo.rearrange(pat), src, hi.rearrange(pat).bitcast(F32),
                                            ALU.subtract).then_inc(s_w, 1)
            looped(pool, body)

        @block.scalar
        def _(act):
            def to_float(c, slot, first=False):
                if quant:
                    act.wait_ge(s_raw[slot], (c + 1) * per)
                    if not first or slot:
                        act.wait_ge(s_w, c * 3 + slot)
                    nc.scalar.copy(w32[:, :], raw[:, slot, :]).then_inc(s_cvt, 1)

            def to_hi(c, slot, first=False):
                hi = GUH[:, slot].rearrange("p a k n -> p (a k n)") if slot < 2 else \
                    DH[:, :, :].rearrange("p k n -> p (k n)")
                if slot == 2 and not first:
                    act.wait_ge(s_dn, c * 16 + 16)
                if quant:
                    act.wait_ge(s_mul, c * 3 + slot + 1)
                    nc.scalar.copy(hi, w32[:, :]).then_inc(s_whi, 1)
                else:
                    act.wait_ge(s_raw[slot], (c + 1) * per)
                    nc.scalar.copy(hi, raw[:, slot, :]).then_inc(s_whi, 1)

            for slot in range(3):
                to_float(0, slot, True)
                to_hi(0, slot, True)

            def body(i, more):
                for s in range(8):
                    slot, t = s // 4, s % 4
                    act.wait_ge(s_gu, i * 8 + s + 1)
                    nc.scalar.activation(SG[:, s % 2, :], PB[2 * (s % 2)][:, :], ACT.Silu).then_inc(s_silu, 1)
                    h = t if slot == 0 else 4 + t % 2
                    act.wait_ge(s_h, i * 8 + s + 3)
                    act.wait_ge(s_dn, i * 16 + 4 * t + (4 if slot == 0 else 12))
                    nc.scalar.copy(HH[:, h, :], HF[:, s % 2, :]).then_inc(s_hhi, 1)
                    if more and s == 4:
                        to_float(i + 1, 0)
                    if more and s == 5:
                        to_hi(i + 1, 0)
                if more:
                    for slot in (1, 2):
                        to_float(i + 1, slot)
                        to_hi(i + 1, slot)
            looped(act, body)

        @block.vector
        def _(dve):
            def body(i, _):
                s = 0
                for step in ORDER:
                    if step[0] == "gu":
                        slot, t = step[1:]
                        h = t if slot == 0 else 4 + t % 2
                        dve.wait_ge(s_silu, i * 8 + s + 1)
                        nc.vector.tensor_tensor(HF[:, s % 2, :], PB[2 * (s % 2) + 1][:, :], SG[:, s % 2, :],
                                                ALU.mult).then_inc(s_h, 1)
                        dve.wait_ge(s_hhi, i * 8 + s + 1)
                        nc.vector.tensor_tensor(HL[:, h, :], HF[:, s % 2, :], HH[:, h, :].bitcast(F32),
                                                ALU.subtract).then_inc(s_hlo, 1)
                        s += 1
                    else:
                        t = step[1]
                        for j in range(4):
                            dve.wait_ge(s_dn, i * 16 + t * 4 + j + 17)
                            x = X[:, 4 * t + j, :]
                            nc.vector.tensor_tensor(x, x, PB[4 + j][:, :], ALU.add).then_inc(s_xadd, 1)
            looped(dve, body)

        @block.tensor
        def _(pe):
            pe.sem_inc(s_h, 2)
            pe.sem_inc(s_dn, 16)
            pe.sem_inc(s_xadd, 4)

            def body(i, _):
                s = 0
                for step in ORDER:
                    if step[0] == "gu":
                        slot, t = step[1:]
                        if t == 0:
                            pe.wait_ge(s_w, i * 3 + slot + 1)
                        pe.wait_ge(s_h, i * 8 + s + 1)
                        tok = slice(t * 512, (t + 1) * 512)
                        for a in range(2):
                            for k in range(KT):
                                ins = three_pass(nc, PB[2 * (s % 2) + a][:, :],
                                                 (GUH[:, slot, a, k, :], GUL[:, slot, a, k, :]),
                                                 (XTH[:, k, tok], XTL[:, k, tok]), k == 0, k == KT - 1)
                        ins.then_inc(s_gu, 1)
                        s += 1
                    else:
                        t = step[1]
                        if t == 0:
                            pe.wait_ge(s_w, i * 3 + 3)
                        pe.wait_ge(s_hlo, i * 8 + 4 + t + 1)
                        for j in range(4):
                            pe.wait_ge(s_xadd, i * 16 + t * 4 + j + 1)
                            for f in range(2):
                                h = t if f == 0 else 4 + t % 2
                                c = slice(j * P, (j + 1) * P)
                                ins = three_pass(nc, PB[4 + j][:, :], (HH[:, h, c], HL[:, h, c]),
                                                 (DH[:, f, :], DL[:, f, :]), f == 0, f == 1)
                            ins.then_inc(s_dn, 1)
            looped(pe, body)


def taylor_phase(nc, X, PB, XTH, XTL, ug_in, point_in, fuse_in, disc_in):
    with ExitStack() as ctx:
        sb, sem = alloc(nc, ctx)
        UGH = sb("UGH", [P, 2, KT, P], F32R)
        UGL = sb("UGL", [P, 2, KT, P], F32R)
        FH = sb("FH", [P, G + 1, D], F32R)
        FL = sb("FL", [P, G + 1, D], F32R)
        rawf = sb("rawf", [P, D * 3])
        point = sb("point", [P, 1])
        disc = sb("disc", [P, G])
        cdis = sb("cdis", [P, G])
        DEL = sb("DEL", [P, D])
        KEEP = sb("KEEP", [P, D])
        A = sb("A", [P, 2, D])
        AH = sb("AH", [P, G + 1, D], F32R)
        AL = sb("AL", [P, G + 1, D], F32R)
        s_in, s_raw, s_free, s_c, s_wm, s_whi, s_wlo = (
            sem(f"t{x}") for x in ("in", "raw", "free", "c", "wm", "whi", "wlo"))
        s_ug, s_a, s_ahi, s_alo, s_out, s_xadd, s_ch, s_af = (
            sem(f"t{x}") for x in ("ug", "a", "ahi", "alo", "out", "xadd", "ch", "af"))
        block = ctx.enter_context(nc.Block())
        NW = 2 + G + 1

        def split_of(w, part):
            if w < 2:
                return (UGH, UGL)[part][:, w].rearrange("p k n -> p (k n)")
            return (FH, FL)[part][:, w - 2, :]

        @block.sync
        def _(sp):
            sp.dma_start(point[:, :], point_in).then_inc(s_in, 16)
            sp.dma_start(disc[:, :], disc_in.to_broadcast([P, G])).then_inc(s_in, 16)
            for w in range(NW):
                if w >= 3:
                    sp.wait_ge(s_wlo, w - 2)
                src = ug_in[w] if w < 2 else fuse_in[w - 2]
                sp.dma_start(rawf[:, (w % 3) * D:(w % 3 + 1) * D], src).then_inc(s_raw, 16)
                sp.wait_ge(s_raw, 16 * (w + 1))

        @block.scalar
        def _(act):
            act.wait_ge(s_in, 32)
            nc.scalar.activation(cdis[:, :], disc[:, :], ACT.Exp, scale=-1.0).then_inc(s_c, 1)
            for w in range(NW):
                act.wait_ge(s_raw, 16 * (w + 1))
                r = rawf[:, (w % 3) * D:(w % 3 + 1) * D]
                if w >= 3:
                    act.wait_ge(s_c, w - 2)
                    nc.scalar.mul(r, r, cdis[:, w - 3:w - 2]).then_inc(s_c, 1)
                    act.wait_ge(s_c, w - 1)
                nc.scalar.copy(split_of(w, 0), r).then_inc(s_whi, 1)
            with act.Fori(0, 4) as i:
                for m in range(G + 1):
                    act.wait_ge(s_a, i * 7 + m + 1)
                    if m < G:
                        act.wait_ge(s_af, i * G + m + 1)
                    nc.scalar.copy(AH[:, m, :], A[:, m % 2, :]).then_inc(s_ahi, 1)

        @block.vector
        def _(dve):
            for w in range(NW):
                dve.wait_ge(s_whi, w + 1)
                nc.vector.tensor_tensor(split_of(w, 1), rawf[:, (w % 3) * D:(w % 3 + 1) * D],
                                        split_of(w, 0).bitcast(F32), ALU.subtract).then_inc(s_wlo, 1)
            with dve.Fori(0, 4) as i:
                link = Chain(dve, s_ch, i * 3)
                dve.wait_ge(s_ug, i + 1)
                nc.vector.tensor_copy(A[:, 0, :], PB[0][:, :]).then_inc(s_a, 1)
                link(nc.vector.tensor_scalar(DEL[:, :], PB[1][:, :], point[:, 0:1], None, ALU.subtract))
                link(nc.vector.scalar_tensor_tensor(KEEP[:, :], DEL[:, :], -THD, DEL[:, :], ALU.is_ge, ALU.mult))
                link(nc.vector.scalar_tensor_tensor(KEEP[:, :], DEL[:, :], THD, KEEP[:, :], ALU.is_le, ALU.mult))
                for m in range(G + 1):
                    if m < G:
                        dve.wait_ge(s_a, i * 7 + m + 1)
                        dve.wait_ge(s_alo, i * 7 + m)
                        nc.vector.tensor_tensor(A[:, (m + 1) % 2, :], A[:, m % 2, :],
                                                (KEEP if m + 1 == 5 else DEL)[:, :], ALU.mult).then_inc(s_a, 1)
                    dve.wait_ge(s_ahi, i * 7 + m + 1)
                    nc.vector.tensor_tensor(AL[:, m, :], A[:, m % 2, :], AH[:, m, :].bitcast(F32),
                                            ALU.subtract).then_inc(s_alo, 1)
                for j in range(4):
                    dve.wait_ge(s_out, i * 4 + j + 1)
                    x = X[:, bass.ds(i * 4 + j, 1), :].rearrange("p a n -> p (a n)")
                    nc.vector.tensor_tensor(x, x, PB[4 + j][:, :], ALU.add).then_inc(s_xadd, 1)

        @block.tensor
        def _(pe):
            pe.sem_inc(s_af, G)
            pe.wait_ge(s_wlo, NW)
            with pe.Fori(0, 4) as i:
                tok = bass.ds(i * 512, 512)
                for a in range(2):
                    for k in range(KT):
                        ins = three_pass(nc, PB[a][:, :], (UGH[:, a, k, :], UGL[:, a, k, :]),
                                         (XTH[:, k, tok], XTL[:, k, tok]), k == 0, k == KT - 1)
                ins.then_inc(s_ug, 1)
                for m in range(G + 1):
                    pe.wait_ge(s_alo, i * 7 + m + 1)
                    for j in range(4):
                        c = slice(j * P, (j + 1) * P)
                        ins = three_pass(nc, PB[4 + j][:, :], (AH[:, m, c], AL[:, m, c]),
                                         (FH[:, m, :], FL[:, m, :]), m == 0, m == G)
                        if m == G:
                            ins.then_inc(s_out, 1)
                    if m < G:
                        ins.then_inc(s_af, 1)
                pe.wait_ge(s_xadd, i * 4 + 4)


def expert_phase(nc, X, PB, ident, ra_in, rb_in, bm_in, iota_in, out):
    NA = E8 * R16
    with ExitStack() as ctx:
        sb, sem = alloc(nc, ctx)
        RA = sb("eRA", [P, KT, NA + E8])
        rb = sb("erb", [P, E8])
        bmr = sb("ebmr", [P, D])
        BH = sb("eBH", [P, D], F32R)
        BL = sb("eBL", [P, D], F32R)
        iota = sb("eiota", [P, E8])
        XN = sb("eXN", [P, 4, D])
        XT = sb("eXT", [P, 4, D])
        st = sb("est", [P, 4, 6])
        mv = sb("emv", [P, 4, 2])
        ve = sb("eve", [P, 4])
        half = sb("ehalf", [P, 4])
        rstd = sb("erstd", [P, 4])
        LG = sb("eLG", [P, 4, E8])
        nm = sb("enm", [P, 4])
        EX = sb("eEX", [P, 4, E8])
        sm = sb("esm", [P, 4])
        top = sb("etop", [P, 4, 8])
        idx = sb("eidx", [P, 4, 8], U32)
        idf = sb("eidf", [P, 4, 8])
        gs = sb("egs", [P, 4])
        gt = sb("egt", [P, 4, 2])
        w1 = sb("ew1", [P, 4, E8])
        w2 = sb("ew2", [P, 4, E8])
        HW = sb("eHW", [P, 4, NA])
        HTH = sb("eHTH", [P, 4, NA], F32R)
        HTL = sb("eHTL", [P, 4, NA], F32R)
        Y = sb("eY", [P, 4, D])
        names = ("in", "half", "chain", "ve", "pow", "xn", "xp", "xt", "h", "lg", "ex", "hw", "hp", "hh", "hl",
                 "o", "y", "st", "bh", "bl", "tick", "sptick")
        s = {n: sem(f"e{n}") for n in names}
        block = ctx.enter_context(nc.Block())
        turns = NT // 4

        @block.sync
        def _(sp):
            sp.dma_start(RA[:, :, :], ra_in).then_inc(s["in"], 16)
            sp.dma_start(rb[:, :], rb_in.to_broadcast([P, E8])).then_inc(s["in"], 16)
            sp.dma_start(bmr[:, :], bm_in).then_inc(s["in"], 16)
            sp.dma_start(iota[:, :], iota_in).then_inc(s["in"], 16)
            with sp.Fori(0, turns) as i:
                for t in range(4):
                    wait_alone(sp, s["y"], i * 4 + t + 1, s["sptick"])
                    sp.dma_start(out[bass.ds(i * 4 + t, 1)].rearrange("a p n -> (a p) n"), Y[:, t, :]).then_inc(s["st"], 16)
                wait_alone(sp, s["st"], i * 64 + 80, s["sptick"])
            sp.wait_ge(s["st"], turns * 64 + 16)

        @block.gpsimd
        def _(pool):
            nc.gpsimd.memset(half[:, :], -0.5).then_inc(s["half"], 1)
            pool.wait_ge(s["half"], 1)
            with pool.Fori(0, turns) as i:
                pool.wait_ge(s["ve"], i + 1)
                nc.gpsimd.tensor_tensor(rstd[:, :], ve[:, :], half[:, :], ALU.pow).then_inc(s["pow"], 1)

        @block.scalar
        def _(act):
            act.wait_ge(s["in"], 64)
            nc.scalar.copy(BH[:, :], bmr[:, :]).then_inc(s["bh"], 1)
            with act.Fori(0, turns) as i:
                for t in range(4):
                    act.wait_ge(s["xp"], i * 4 + t + 1)
                    nc.scalar.copy(XT[:, t, :], PB[t][:, :]).then_inc(s["xt"], 1)
                act.wait_ge(s["lg"], i + 1)
                nc.scalar.activation(EX[:, :, :], LG[:, :, :], ACT.Exp).then_inc(s["ex"], 1)
                for t in range(4):
                    act.wait_ge(s["hp"], i * 4 + t + 1)
                    nc.scalar.copy(HTH[:, t, :], PB[t][:, 0:NA]).then_inc(s["hh"], 1)

        @block.vector
        def _(dve):
            dve.wait_ge(s["bh"], 1)
            nc.vector.tensor_tensor(BL[:, :], bmr[:, :], BH[:, :].bitcast(F32), ALU.subtract).then_inc(s["bl"], 1)
            dve.sem_inc(s["st"], 16)
            with dve.Fori(0, turns) as i:
                link = Chain(dve, s["chain"], i * 17, s["tick"])
                x = X[:, bass.ds(i * 4, 4), :]
                for t in range(4):
                    ins = nc.vector.bn_stats(st[:, t, :], x[:, t, :])
                link(ins, alone=True)
                for t in range(4):
                    ins = nc.vector.bn_aggr(mv[:, t, :], st[:, t, :])
                link(ins)
                nc.vector.tensor_scalar(ve[:, :], mv[:, :, 1], EPS, None, ALU.add).then_inc(s["ve"], 1)
                dve.wait_ge(s["pow"], i + 1)
                for t in range(4):
                    nc.vector.tensor_scalar(XN[:, t, :], x[:, t, :], mv[:, t, 0:1], rstd[:, t:t + 1],
                                            ALU.subtract, ALU.mult).then_inc(s["xn"], 1)
                for t in range(4):
                    dve.wait_ge(s["h"], i * 4 + t + 1)
                    ins = nc.vector.tensor_tensor(LG[:, t, :], PB[4 + t][:, NA:NA + E8], rb[:, :], ALU.add)
                link(ins)
                link(nc.vector.tensor_reduce(nm[:, :], LG[:, :, :], axis=AXX, op=ALU.max))
                nc.vector.tensor_tensor(LG[:, :, :], LG[:, :, :], nm[:, :].unsqueeze(2).to_broadcast([P, 4, E8]),
                                        ALU.subtract).then_inc(s["lg"], 1)
                dve.wait_ge(s["ex"], i + 1)
                link(nc.vector.tensor_reduce(sm[:, :], EX[:, :, :], axis=AXX, op=ALU.add))
                link(nc.vector.reciprocal(sm[:, :], sm[:, :]))
                link(nc.vector.tensor_tensor(EX[:, :, :], EX[:, :, :], sm[:, :].unsqueeze(2).to_broadcast([P, 4, E8]),
                                             ALU.mult), alone=True)
                for t in range(4):
                    ins = nc.vector.max(top[:, t, :], EX[:, t, :])
                link(ins, alone=True)
                for t in range(4):
                    ins = nc.vector.max_index(idx[:, t, :], top[:, t, :], EX[:, t, :])
                link(ins)
                link(nc.vector.tensor_tensor(gs[:, :], top[:, :, 0], top[:, :, 1], ALU.add))
                link(nc.vector.tensor_copy(idf[:, :, :], idx[:, :, :]))
                link(nc.vector.reciprocal(gs[:, :], gs[:, :]))
                link(nc.vector.tensor_tensor(gt[:, :, :], top[:, :, 0:2], gs[:, :].unsqueeze(2).to_broadcast([P, 4, 2]),
                                             ALU.mult))
                link(nc.vector.tensor_scalar(gt[:, :, :], gt[:, :, :], 0.5, None, ALU.mult))
                for w, c in ((w1, 0), (w2, 1)):
                    ins = nc.vector.tensor_tensor(w[:, :, :], iota[:, :].unsqueeze(1).to_broadcast([P, 4, E8]),
                                                  idf[:, :, c:c + 1].to_broadcast([P, 4, E8]), ALU.is_equal)
                link(ins)
                for w, c in ((w1, 0), (w2, 1)):
                    ins = nc.vector.tensor_tensor(w[:, :, :], w[:, :, :], gt[:, :, c:c + 1].to_broadcast([P, 4, E8]),
                                                  ALU.mult)
                link(ins)
                link(nc.vector.tensor_tensor(w1[:, :, :], w1[:, :, :], w2[:, :, :], ALU.add))
                for t in range(4):
                    nc.vector.tensor_tensor(HW[:, t, :].rearrange("p (e r) -> p e r", e=E8),
                                            PB[4 + t][:, 0:NA].rearrange("p (e r) -> p e r", e=E8),
                                            w1[:, t, :].unsqueeze(2).to_broadcast([P, E8, R16]),
                                            ALU.mult).then_inc(s["hw"], 1)
                for t in range(4):
                    dve.wait_ge(s["hh"], i * 4 + t + 1)
                    nc.vector.tensor_tensor(HTL[:, t, :], PB[t][:, 0:NA], HTH[:, t, :].bitcast(F32),
                                            ALU.subtract).then_inc(s["hl"], 1)
                for t in range(4):
                    dve.wait_ge(s["o"], i * 4 + t + 1)
                    if t == 0:
                        dve.wait_ge(s["st"], i * 64 + 16)
                    nc.vector.tensor_tensor(Y[:, t, :], PB[4 + t][:, :], x[:, t, :], ALU.add).then_inc(s["y"], 1)

        @block.tensor
        def _(pe):
            pe.wait_ge(s["in"], 64)
            pe.wait_ge(s["bl"], 1)
            with pe.Fori(0, turns) as i:
                for t in range(4):
                    pe.wait_ge(s["xn"], i * 4 + t + 1)
                    for k in range(KT):
                        ins = nc.tensor.transpose(PB[t][:, k * P:(k + 1) * P], XN[:, t, k * P:(k + 1) * P], ident[:, :])
                    ins.then_inc(s["xp"], 1)
                for t in range(4):
                    pe.wait_ge(s["xt"], i * 4 + t + 1)
                    for k in range(KT):
                        ins = nc.tensor.matmul(PB[4 + t][:, 0:NA + E8], XT[:, t, k * P:(k + 1) * P], RA[:, k, :],
                                               start=k == 0, stop=k == KT - 1)
                    ins.then_inc(s["h"], 1)
                for t in range(4):
                    pe.wait_ge(s["hw"], i * 4 + t + 1)
                    nc.tensor.transpose(PB[t][:, 0:NA], HW[:, t, :], ident[:, :]).then_inc(s["hp"], 1)
                for t in range(4):
                    pe.wait_ge(s["hl"], i * 4 + t + 1)
                    three_pass(nc, PB[4 + t][:, :], (HTH[:, t, :], HTL[:, t, :]), (BH[:, :], BL[:, :]),
                               True, True).then_inc(s["o"], 1)
                pe.wait_ge(s["y"], i * 4 + 4)


def dump_phase(nc, X, out):
    with nc.semaphore("dump") as s, nc.Block() as block:
        @block.sync
        def _(sp):
            for j in range(NT):
                sp.dma_start(out[j], X[:, j, :]).then_inc(s, 16)
            sp.wait_ge(s, 16 * NT)


def build(nc, d, out, stop=9):
    with ExitStack() as ctx:
        X = ctx.enter_context(nc.sbuf_tensor("X", [P, NT, D], F32))
        ident = ctx.enter_context(nc.sbuf_tensor("ident", [P, P], F32))
        PB = [ctx.enter_context(nc.psum_tensor(f"PB{i}", [P, D], F32)) for i in range(8)]
        attention_phase(nc, X, PB, ident, d["x"], d["wqkvo"], d["rope"], d["mask"], d["ident"])
        if stop == 0:
            return dump_phase(nc, X, out)
        with ExitStack() as c2:
            XTH = c2.enter_context(nc.sbuf_tensor("XTH", [P, KT, TOK], F32R))
            XTL = c2.enter_context(nc.sbuf_tensor("XTL", [P, KT, TOK], F32R))
            norm_phase(nc, X, PB, ident, XTH, XTL, "a")
            swiglu_phase(nc, X, PB, XTH, XTL, F0, d["gu0"], d["d0"], d["sgu0"], d["sd0"], "a")
            if stop == 1:
                return dump_phase(nc, X, out)
            norm_phase(nc, X, PB, ident, XTH, XTL, "b")
            taylor_phase(nc, X, PB, XTH, XTL, d["ug"], d["point"], d["fuse"], d["disc"])
            swiglu_phase(nc, X, PB, XTH, XTL, F1, d["gu1"], d["d1"], None, None, "b")
            if stop == 2:
                return dump_phase(nc, X, out)
        expert_phase(nc, X, PB, ident, d["ra"], d["rb"], d["bm"], d["iota"], out)


def layouts(np, a):
    c = np.ascontiguousarray

    def rows(w):
        return c(w.reshape(KT, P, -1).transpose(1, 0, 2))

    def gate_up(g, u, F):
        def one(w):
            w = np.concatenate([w, np.zeros((F - w.shape[0], D), w.dtype)]) if w.shape[0] < F else w
            return w.T.reshape(KT, P, F // 256, 2, P).transpose(2, 3, 1, 0, 4)
        return c(np.stack([one(g), one(u)], axis=3)).reshape(F // 256, 2, P, 2 * KT * P)

    def down(w, F):
        w = w.T
        w = np.concatenate([w, np.zeros((F - w.shape[0], D), w.dtype)]) if w.shape[0] < F else w
        return c(w.reshape(F // 256, 2, P, D).transpose(0, 2, 1, 3)).reshape(F // 256, P, 2 * D)

    def scale_gu(g, u):
        def one(s):
            return s.reshape(F0 // 256, 2, P, KT).transpose(0, 1, 3, 2)
        return c(np.stack([one(g), one(u)], axis=2)).reshape(F0 // 256, 2, 2 * KT * P)

    inv = (1.0 / 10000.0 ** (np.arange(0, HD, 2)[:HD // 2].astype(np.float32) / HD))
    f = np.outer(np.arange(S), inv).astype(np.float32)
    cos, sin = np.cos(f).astype(np.float32), np.sin(f).astype(np.float32)
    cos2 = np.repeat(cos, 2, axis=1)
    sin2 = np.stack([-sin, sin], axis=-1).reshape(S, HD)
    q = np.float32(HD ** -0.5)
    rope = np.stack([cos2 * q, sin2 * q, cos2, sin2]).astype(np.float32).reshape(4, TPB, P, HD)
    mask = np.where(np.arange(P)[None, :] > np.arange(P)[:, None], np.float32(NEG), np.float32(0))
    fuse = a["L1_attn_fuse_weight"]
    return {
        "x": c(a["L0_attn_x"].reshape(B, TPB, P, D).transpose(0, 2, 1, 3)),
        "wqkvo": np.stack([rows(a[f"L0_attn_w{n}"]) for n in "qkvo"]),
        "rope": c(rope.transpose(2, 0, 1, 3)),
        "mask": mask.astype(np.float32),
        "ident": np.eye(P, dtype=np.float32),
        "gu0": gate_up(a["L0_ffn_gate_q"], a["L0_ffn_up_q"], F0),
        "d0": down(a["L0_ffn_down_q"], F0),
        "sgu0": scale_gu(a["L0_ffn_gate_s"], a["L0_ffn_up_s"]),
        "sd0": c(a["L0_ffn_down_s"].T).reshape(F0 // 256, 2 * D),
        "ug": np.stack([rows(a["L1_attn_up_w"].T).reshape(P, -1), rows(a["L1_attn_gate_w"].T).reshape(P, -1)]),
        "point": c(a["L1_attn_local_point"].reshape(P, 1)),
        "fuse": np.stack([c(a["L1_attn_local_approx_output"].T)] + [c(fuse[:, :, m].T) for m in range(G)]),
        "disc": c(a["L1_attn_discount_factor"].reshape(1, G)),
        "gu1": gate_up(a["L1_attn_ffn_gate_w"], a["L1_attn_ffn_up_w"], F1),
        "d1": down(a["L1_attn_ffn_down_w"], F1),
        "ra": np.concatenate([rows(a["L1_ffn_A"].reshape(E8 * R16, D).T), rows(a["L1_ffn_router_w"].T)], axis=2),
        "rb": c(a["L1_ffn_router_b"].reshape(1, E8)),
        "bm": c(a["L1_ffn_Bm"].transpose(0, 2, 1)).reshape(E8 * R16, D),
        "iota": np.tile(np.arange(E8, dtype=np.float32), (P, 1)),
    }


def program(nc, arrays, stop=9):
    d = {n: nc.dram_tensor(f"in_{n}", v.shape, mybir.dt.from_np(v.dtype), kind="ExternalInput").ap()
         for n, v in arrays.items()}
    out = nc.dram_tensor("out_0", (NT, P, D), F32, kind="ExternalOutput").ap()
    build(nc, d, out, stop)


def kernel(**inputs):
    import numpy as np
    import concourse.bacc as bacc
    from concourse.bass_utils import run_bass_kernel_spmd

    arrays = layouts(np, {n: np.asarray(v) for n, v in inputs.items()})
    nc = bacc.Bacc("TRN2", target_bir_lowering=False, num_devices=1)
    program(nc, arrays)
    r = run_bass_kernel_spmd(nc, [{f"in_{n}": v for n, v in arrays.items()}], core_ids=[0])
    return r.results[0]["out_0"].reshape(B, S, D)
```

```python
from contextlib import ExitStack

import concourse.bass as bass
from concourse import mybir

F32 = mybir.dt.float32
F32R = mybir.dt.float32r
BF16 = mybir.dt.bfloat16
I32 = mybir.dt.int32
U32 = mybir.dt.uint32
ALU = mybir.AluOpType
ACT = mybir.ActivationFunctionType
AXX = mybir.AxisListType.X

P = 128
D = 512
KT = D // P
B, S = 8, 256
TOK = B * S
NT = TOK // P
TPB = S // P
H, HD = 32, 16
NPAIR = H // 2
UNITS = H // 4
F0 = 1792
F1 = 1280
G = 6
E8, R16 = 8, 16
EPS = 1e-5
THD = 2.5
NEG = -3.0e38


class Chain:

    def __init__(self, eng, sem, base, tick=None):
        self.eng, self.sem, self.base, self.tick, self.n = eng, sem, base, tick, 0

    def __call__(self, ins, alone=False):
        self.n += 1
        ins.then_inc(self.sem, 1)
        self.eng.wait_ge(self.sem, self.base + self.n)
        if alone:
            self.eng.sem_inc(self.tick, 1)


def wait_alone(eng, sem, value, tick):
    eng.wait_ge(sem, value)
    eng.sem_inc(tick, 1)


def three_pass(nc, out, lhs, rhs, first, last):
    nc.tensor.matmul(out, lhs[0], rhs[0], start=first, stop=False)
    nc.tensor.matmul(out, lhs[0], rhs[1], start=False, stop=False)
    return nc.tensor.matmul(out, lhs[1], rhs[0], start=False, stop=last)


def steps(text):
    out = []
    for word in text.split():
        early = word.startswith("next-")
        kind, *args = word[5 if early else 0:].split(".")
        out.append((("early",) if early else ()) + (kind, *(int(v) for v in args)))
    return out


def alloc(nc, ctx):
    def sb(name, shape, dt=F32):
        return ctx.enter_context(nc.sbuf_tensor(name, shape, dt))

    def sem(name):
        return ctx.enter_context(nc.semaphore(name))

    return sb, sem


def attention_phase(nc, X, PB, ident, x_in, wqkvo, rope_in, mask_in, ident_in):
    HH = H // 2
    NJ = 3 * UNITS
    with ExitStack() as ctx:
        sb, sem = alloc(nc, ctx)
        WH = sb("WH", [P, 4, KT, D], F32R)
        WL = sb("WL", [P, 4, KT, D], F32R)
        XTH = sb("aXTH", [P, KT, S], F32R)
        XTL = sb("aXTL", [P, KT, S], F32R)
        ATH = sb("ATH", [P, KT, P], F32R)
        ATL = sb("ATL", [P, KT, P], F32R)
        V = sb("V", [P, 2, TPB, HH, 32])
        XN = sb("XN", [P, TPB, D])
        RA = sb("RA", [P, TPB, HH, HD])
        RB = sb("RB", [P, TPB, HH, HD])
        STK = sb("STK", [P, TPB, HH, 4, HD], F32R)
        QT = sb("QT", [P, 2, HH // 2, S], F32R)
        KTT = sb("KTT", [P, 2, HH // 2, 2, S], F32R)
        PR = sb("PR", [P, 3, D])
        PT = sb("PT", [P, 2, 4, 384])
        OT = sb("OT", [P, 2, S])
        AO = sb("AO", [P, TPB, D])
        rope = sb("rope", [P, 4, TPB, HD])
        maskf = sb("maskf", [P, P])
        maskb = sb("maskb", [P, P], BF16)
        identb = sb("identb", [P, P], BF16)
        ident_r = sb("ident_r", [P, P], F32R)
        st = sb("st", [P, TPB, 6])
        mv = sb("mv", [P, TPB, 2])
        ve = sb("ve", [P, TPB])
        half = sb("half", [P, TPB])
        rstd = sb("rstd", [P, TPB])
        nmx = sb("nmx", [P, 3, 4])
        rden = sb("rden", [P, 2, TPB, 4])
        WRAW = [X[:, 4 * w + 4:4 * w + 8, :] for w in range(3)]
        WRAW.append(V[:, :, :, :, :].rearrange("p a t h d -> p (a t h d)").rearrange("p (k n) -> p k n", k=KT))

        s_cst, s_x, s_w = sem("s_cst"), sem("s_x"), [sem(f"s_w{w}") for w in range(4)]
        s_whi, s_wlo, s_zero, s_cd, s_half = sem("s_whi"), sem("s_wlo"), sem("s_zero"), sem("s_cd"), sem("s_half")
        s_chain, s_tick, s_sptick = sem("s_chain"), sem("s_tick"), sem("s_sptick")
        s_ve, s_pow, s_xn, s_xth = sem("s_ve"), sem("s_pow"), sem("s_xn"), sem("s_xth")
        fr_full = [sem(f"fr_full{i}") for i in range(2)]
        fr_free = [sem(f"fr_free{i}") for i in range(2)]
        sc_full = [sem(f"sc_full{i}") for i in range(3)]
        sc_free = [sem(f"sc_free{i}") for i in range(3)]
        tp_full = [sem(f"tp_full{i}") for i in range(2)]
        tp_free = [sem(f"tp_free{i}") for i in range(2)]
        ou_full, ou_free = sem("ou_full"), sem("ou_free")
        tl_full, tl_free = sem("tl_full"), sem("tl_free")
        s_mx, s_rden, s_rr, s_hi, s_lo = sem("s_mx"), sem("s_rden"), sem("s_rr"), sem("s_hi"), sem("s_lo")
        s_ka, s_ath = sem("s_ka"), sem("s_ath")
        SC, TP, FR, OU = PB[0:3], PB[3:5], PB[5:7], PB[7]

        TENSOR_STEPS = steps("""
            score.0 at.0 flip.0 score.1 score.2 turn.0.0.0.0 proj.0.1.0 score.3 o.0.0 flip.1 flip.2 score.4
            score.5 turn.0.0.0.1 flip.3 score.6 proj.0.1.1 o.0.1 flip.4 at.1 turn.0.0.1.0 flip.5 turn.0.0.1.1
            o.1.0 turn.0.1.0.0 o.1.1 score.7 pv.0 score.8 out.0 turn.0.1.0.1 turn.0.1.1.0 flip.6 pv.1 flip.7
            turn.0.1.1.1 score.9 score.10 out.1 flip.8 proj.0.2.0 flip.9 score.11 score.12 pv.2 flip.10
            proj.0.2.1 score.13 flip.11 out.2 flip.12 score.14 flip.13 pv.3 xt.0 score.15 score.16 out.3
            flip.14 xt.1 score.17 proj.1.0.0 flip.15 score.18 proj.1.0.1 pv.4 flip.16 score.19 flip.17
            proj.1.1.0 out.4 proj.1.1.1 score.20 flip.18 turn.1.0.0.0 score.21 flip.19 pv.5 turn.1.0.0.1
            turn.1.0.1.0 score.22 flip.20 score.23 out.5 turn.1.0.1.1 flip.21 pv.6 turn.1.1.0.0 turn.1.1.0.1
            out.6 flip.22 proj.1.2.0 turn.1.1.1.0 proj.1.2.1 flip.23 next-proj.0.0.0 turn.1.1.1.1
            next-proj.0.0.1 pv.7 out.7
        """)
        VECTOR_STEPS = steps("""
            score.0 stack.0.0.0 at.0 stack.0.0.1 score.1 score.2 score.3 flip.1 flip.2 score.4 score.5 score.6
            rope.0.1 o.0.1 flip.4 at.1 flip.5 stack.0.1.0 stack.0.1.1 turn.0.1.0.0 o.1.1 score.7 score.8 out.0
            turn.0.1.0.1 turn.0.1.1.0 flip.7 turn.0.1.1.1 score.9 score.10 out.1 flip.8 score.11 score.12
            stats flip.10 score.13 flip.11 out.2 score.14 norm flip.13 xt.0 score.15 score.16 out.3 flip.14
            xt.1 score.17 score.18 rope.1.0 flip.16 score.19 flip.17 out.4 stack.1.0.0 stack.1.0.1 score.20
            rope.1.1 score.21 flip.19 score.22 flip.20 score.23 out.5 stack.1.1.0 turn.1.1.0.0 turn.1.1.0.1
            stack.1.1.1 out.6 flip.22 turn.1.1.1.0 flip.23 turn.1.1.1.1 next-rope.0.0 out.7
        """)
        SCALAR_STEPS = steps("""
            score.0 stack.0.0.0 at.0 stack.0.0.1 flip.0 score.1 score.2 turn.0.0.0.0 score.3 score.4 score.5
            turn.0.0.0.1 flip.3 score.6 at.1 turn.0.0.1.0 stack.0.1.0 turn.0.0.1.1 stack.0.1.1 turn.0.1.0.0
            score.7 pv.0 score.8 turn.0.1.0.1 turn.0.1.1.0 flip.6 pv.1 turn.0.1.1.1 score.9 score.10 flip.9
            score.11 score.12 pv.2 score.13 vals.0 flip.12 score.14 pv.3 xt.0 score.15 score.16 xt.1 score.17
            flip.15 score.18 pv.4 score.19 stack.1.0.0 stack.1.0.1 score.20 flip.18 turn.1.0.0.0 score.21 pv.5
            turn.1.0.0.1 turn.1.0.1.0 score.22 score.23 stack.1.1.0 turn.1.0.1.1 flip.21 pv.6 turn.1.1.0.0
            turn.1.1.0.1 stack.1.1.1 turn.1.1.1.0 vals.1 turn.1.1.1.1 pv.7
        """)
        GPSIMD_STEPS = steps("""
            rope.0.1 stats rope.1.0 rope.1.1 next-rope.0.0
        """)

        def ahead(step):
            return step[0] in ("stats", "norm", "xt", "early") or \
                step[0] in ("proj", "rope", "stack", "turn", "vals") and step[1] == 1

        USES = {("proj", 0, 0): -1}
        for step in TENSOR_STEPS:
            if step[0] == "proj" and step[3] == 0:
                USES[step[:3]] = len(USES) - 1
            elif step[0] in ("turn", "xt"):
                USES[step] = len(USES) - 1
        NU = len(USES)
        assert NU == 24

        def fr(use):
            return (14 + USES[use]) % 2

        def fr_wait_full(eng, b, use):
            eng.wait_ge(fr_full[fr(use)], b * 12 + ((14 + USES[use]) // 2 + 1))

        def fr_wait_turn(eng, b, use):
            eng.wait_ge(fr_free[fr(use)], b * 12 + ((14 + USES[use]) // 2 + 1))

        def fr_wait_read(eng, b, use):
            eng.wait_ge(fr_free[fr(use)], b * 12 + ((14 + USES[use]) // 2 + 2))

        def follow(do, b, steps):
            for step in steps:
                if step[0] == "early":
                    do(b + 1, *step[1:])
                else:
                    do(b, *step)

        def run(eng, order, do):
            follow(do, -1, [s for s in order if ahead(s)])
            follow(do, 0, [s for s in order if s[0] not in ("at", "o")])
            with eng.Fori(1, B - 1) as i:
                follow(do, i, order)
            follow(do, B - 1, [s for s in order if not ahead(s)])
            follow(do, B, [s for s in order if s[0] in ("at", "o")])

        block = ctx.enter_context(nc.Block())

        @block.sync
        def _(sp):
            sp.dma_start(X[:, 0:TPB, :], x_in[0]).then_inc(s_x, 16)
            sp.dma_start(WRAW[0], wqkvo[0]).then_inc(s_w[0], 16)
            sp.dma_start(ident[:, :], ident_in).then_inc(s_cst, 16)
            sp.dma_start(maskf[:, :], mask_in).then_inc(s_cst, 16)
            sp.dma_start(rope[:, :, :, :], rope_in).then_inc(s_cst, 16)
            for w in range(1, 4):
                sp.dma_start(WRAW[w], wqkvo[w]).then_inc(s_w[w], 16)
            sp.wait_ge(s_x, 16)
            sp.wait_ge(s_wlo, 4)
            with sp.Fori(1, B) as i:
                sp.dma_start(X[:, bass.ds(i * TPB, TPB), :],
                             x_in[bass.ds(i, 1)].rearrange("a p t n -> p (a t) n")).then_inc(s_x, 16)
                wait_alone(sp, s_x, i * 16 + 16, s_sptick)

        @block.gpsimd
        def _(pool):
            nc.gpsimd.memset(half[:, :], -0.5).then_inc(s_half, 1)
            pool.wait_ge(s_half, 1)

            def do(b, kind, *a):
                if kind == "stats":
                    pool.wait_ge(s_ve, b + 2)
                    nc.gpsimd.tensor_tensor(rstd[:, :], ve[:, :], half[:, :], ALU.pow).then_inc(s_pow, 1)
                    if isinstance(b, int) and b == -1:
                        nc.gpsimd.memset(KTT[:, :, :, :, :].bitcast(U32), 0).then_inc(s_zero, 1)
                        pool.wait_ge(s_wlo, 4)
                        nc.gpsimd.memset(V[:, :, :, :, HD:32], 1.0).then_inc(s_zero, 1)
                elif kind == "rope":
                    fr_wait_read(pool, b, ("proj", *a))
                    nc.gpsimd.tensor_tensor(RA[:, :, :, :], RA[:, :, :, :], RB[:, :, :, :], ALU.add).then_inc(s_rr, 1)

            run(pool, GPSIMD_STEPS, do)

        @block.scalar
        def _(act):
            act.wait_ge(s_cst, 48)
            nc.scalar.copy(ident_r[:, :], ident[:, :]).then_inc(s_cd, 1)
            nc.scalar.copy(identb[:, :], ident[:, :]).then_inc(s_cd, 1)
            nc.scalar.copy(maskb[:, :], maskf[:, :]).then_inc(s_cd, 1)
            for w in range(4):
                act.wait_ge(s_w[w], 16)
                nc.scalar.copy(WH[:, w, :, :], WRAW[w]).then_inc(s_whi, 1)

            def do(b, kind, *a):
                if kind == "xt":
                    t, = a
                    fr_wait_full(act, b, ("xt", t))
                    nc.scalar.copy(XTH[:, :, t * P:(t + 1) * P],
                                   FR[fr(("xt", t))][:, :].rearrange("p (k n) -> p k n", k=KT)).then_inc(s_xth, 1)
                elif kind == "stack":
                    f, w, t = a
                    act.wait_ge(s_rr, b * 4 + (2 * f + w + 3))
                    dst = STK[:, t, :, 0:2, :] if w == 0 else STK[:, t, :, 0:4:2, :]
                    nc.scalar.copy(dst, RA[:, t, :, :].unsqueeze(2).to_broadcast([P, HH, 2, HD])).then_inc(s_hi, 1)
                elif kind == "turn":
                    f, w, t, g = a
                    use = ("turn", *a)
                    fr_wait_full(act, b, use)
                    bank = FR[fr(use)]
                    cols = slice(t * P, (t + 1) * P)
                    if w == 0:
                        nc.scalar.copy(QT[:, 1 - f, 4 * g:4 * g + 4, cols],
                                       bank[:, :].rearrange("p (a n) -> p a n", a=4)).then_inc(fr_free[fr(use)], 1)
                    else:
                        nc.scalar.copy(KTT[0:64, 1 - f, 4 * g:4 * g + 4, 0, cols],
                                       bank[0:64, :].rearrange("p (a n) -> p a n", a=4)).then_inc(s_ka, 1)
                elif kind == "vals":
                    use = ("proj", a[0], 2)
                    fr_wait_full(act, b, use)
                    if isinstance(b, int) and b == -1:
                        act.wait_ge(s_zero, 2)
                    nc.scalar.copy(V[:, 1 - a[0], :, :, 0:HD],
                                   FR[fr(use)][:, :].rearrange("p (t h d) -> p t h d", t=TPB, h=HH)
                                   ).then_inc(fr_free[fr(use)], 1)
                elif kind == "score":
                    n, = a
                    u, j = n // 3, n % 3
                    act.wait_ge(s_mx, b * NJ + (n + 1))
                    heads = 4 if j == 0 else 2
                    w = D // heads
                    for h in range(heads):
                        ins = nc.scalar.activation(PR[:, j, h * w:(h + 1) * w], SC[j][:, h * w:(h + 1) * w],
                                                   ACT.Exp, bias=nmx[:, j, h:h + 1])
                    ins.then_inc(sc_free[j], 1)
                elif kind == "flip" and a[0] % 3 == 0:
                    n, = a
                    act.wait_ge(tp_full[n % 2], b * 12 + (n // 2 + 1))
                    nc.scalar.copy(PT[:, n // 3 % 2, :, 0:P],
                                   TP[n % 2][:, :].rearrange("p (h n) -> p h n", h=4)).then_inc(tp_free[n % 2], 1)
                elif kind == "pv":
                    u, = a
                    act.wait_ge(ou_full, b * 16 + (2 * u + 1))
                    nc.scalar.copy(OT[:, u % 2, :], OU[:, 0:S]).then_inc(ou_free, 1)
                elif kind == "at":
                    t, = a
                    act.wait_ge(tl_full, b * 4 + (2 * t - 3))
                    nc.scalar.copy(ATH[:, :, :], OU[:, :].rearrange("p (k n) -> p k n", k=KT)).then_inc(s_ath, 1)

            run(act, SCALAR_STEPS, do)

        @block.vector
        def _(dve):
            def do(b, kind, *a):
                xs = [X[:, 2 * b + 2 + t, :] if isinstance(b, int) else
                      X[:, bass.ds(b * TPB + (TPB + t), 1), :].rearrange("p a n -> p (a n)") for t in range(TPB)
                      ] if kind in ("stats", "norm") else None
                if kind == "stats":
                    dve.wait_ge(s_x, b * 16 + 32)
                    for t in range(TPB):
                        ins = nc.vector.bn_stats(st[:, t, :], xs[t])
                    norm_link(b, ins, 0)
                    for t in range(TPB):
                        ins = nc.vector.bn_aggr(mv[:, t, :], st[:, t, :])
                    norm_link(b, ins, 1)
                    nc.vector.tensor_scalar(ve[:, :], mv[:, :, 1], EPS, None, ALU.add).then_inc(s_ve, 1)
                elif kind == "norm":
                    dve.wait_ge(s_pow, b + 2)
                    for t in range(TPB):
                        nc.vector.tensor_scalar(XN[:, t, :], xs[t], mv[:, t, 0:1], rstd[:, t:t + 1],
                                                ALU.subtract, ALU.mult).then_inc(s_xn, 1)
                    if isinstance(b, int) and b == -1:
                        split_weight(0)
                elif kind == "xt":
                    t, = a
                    use = ("xt", t)
                    dve.wait_ge(s_xth, b * 2 + (t + 3))
                    nc.vector.tensor_tensor(XTL[:, :, t * P:(t + 1) * P],
                                            FR[fr(use)][:, :].rearrange("p (k n) -> p k n", k=KT),
                                            XTH[:, :, t * P:(t + 1) * P].bitcast(F32),
                                            ALU.subtract).then_inc(fr_free[fr(use)], 1)
                    if isinstance(b, int) and b == -1 and t == 1:
                        for w in range(1, 4):
                            split_weight(w)
                elif kind == "rope":
                    f, w = a
                    use = ("proj", f, w)
                    fr_wait_full(dve, b, use)
                    bank = FR[fr(use)]
                    cos = rope[:, 2 * w, :, :].unsqueeze(2).to_broadcast([P, TPB, HH, HD])
                    sin = rope[:, 2 * w + 1, :, :].rearrange("p t (k e) -> p t k e", e=2)
                    q4 = bank[:, :].rearrange("p (t h k e) -> p t h k e", t=TPB, h=HH, e=2)
                    b4 = RB[:, :, :, :].rearrange("p t h (k e) -> p t h k e", e=2)
                    if not (isinstance(b, int) and b == -1 and w == 0):
                        dve.wait_ge(s_lo, b * 8 + (4 * f + 2 * w + 4))
                    nc.vector.tensor_tensor(RA[:, :, :, :], bank[:, :].rearrange("p (t h d) -> p t h d", t=TPB, h=HH),
                                            cos, ALU.mult)
                    for e in range(2):
                        ins = nc.vector.tensor_tensor(b4[:, :, :, :, e], q4[:, :, :, :, 1 - e],
                                                      sin[:, :, :, e].unsqueeze(2).to_broadcast([P, TPB, HH, HD // 2]),
                                                      ALU.mult)
                    ins.then_inc(fr_free[fr(use)], 1)
                elif kind == "stack":
                    f, w, t = a
                    dve.wait_ge(s_hi, b * 8 + (4 * f + 2 * w + t + 5))
                    dst = STK[:, t, :, 2:4, :] if w == 0 else STK[:, t, :, 1:4:2, :]
                    nc.vector.tensor_tensor(dst, RA[:, t, :, :].unsqueeze(2).to_broadcast([P, HH, 2, HD]),
                                            STK[:, t, :, 0:1, :].bitcast(F32).to_broadcast([P, HH, 2, HD]),
                                            ALU.subtract).then_inc(s_lo, 1)
                elif kind == "turn" and a[1] == 1:
                    f, w, t, g = a
                    use = ("turn", *a)
                    dve.wait_ge(s_ka, b * 8 + (4 * f + 2 * t + g + 5))
                    nc.vector.tensor_copy(KTT[64:P, 1 - f, 4 * g:4 * g + 4, 1, t * P:(t + 1) * P],
                                          FR[fr(use)][64:P, :].rearrange("p (a n) -> p a n", a=4)
                                          ).then_inc(fr_free[fr(use)], 1)
                elif kind == "score":
                    n, = a
                    u, j = n // 3, n % 3
                    heads = 4 if j == 0 else 2
                    dve.wait_ge(sc_full[j], b * 8 + (u + 1))
                    nc.vector.tensor_reduce(nmx[:, j, 0:heads], SC[j][:, :].rearrange("p (h n) -> p h n", h=heads),
                                            axis=AXX, op=ALU.max, negate=True).then_inc(s_mx, 1)
                elif kind == "flip" and a[0] % 3:
                    n, = a
                    u, j = n // 3, n % 3
                    dve.wait_ge(tp_full[n % 2], b * 12 + (n // 2 + 1))
                    nc.vector.tensor_copy(PT[:, u % 2, 2 * j - 2:2 * j, P:384],
                                          TP[n % 2][:, :].rearrange("p (h n) -> p h n", h=2)
                                          ).then_inc(tp_free[n % 2], 1)
                elif kind == "out":
                    u, = a
                    dve.wait_ge(ou_full, b * 16 + (2 * u + 2))
                    v = OU[:, 0:S].rearrange("p (t h d) -> p t h d", t=TPB, h=4)
                    nc.vector.reciprocal(rden[:, u % 2, :, :], v[:, :, :, HD]).then_inc(s_rden, 1)
                    dve.wait_ge(s_rden, b * 8 + (u + 1))
                    nc.vector.tensor_tensor(
                        AO[:, :, u * 64:(u + 1) * 64].rearrange("p t (h d) -> p t h d", h=4), v[:, :, :, 0:HD],
                        rden[:, u % 2, :, :].unsqueeze(3).to_broadcast([P, TPB, 4, HD]), ALU.mult).then_inc(ou_free, 1)
                elif kind == "at":
                    t, = a
                    dve.wait_ge(s_ath, b * 2 + (t - 1))
                    nc.vector.tensor_tensor(ATL[:, :, :], OU[:, :].rearrange("p (k n) -> p k n", k=KT),
                                            ATH[:, :, :].bitcast(F32), ALU.subtract).then_inc(tl_free, 1)
                elif kind == "o" and a[1] == 1:
                    t = a[0]
                    dve.wait_ge(tl_full, b * 4 + (2 * t - 2))
                    x = X[:, 2 * b - 2 + t, :] if isinstance(b, int) else \
                        X[:, bass.ds(b * TPB + (t - TPB), 1), :].rearrange("p a n -> p (a n)")
                    nc.vector.tensor_tensor(x, x, OU[:, :], ALU.add).then_inc(tl_free, 1)

            def norm_link(b, ins, n):
                ins.then_inc(s_chain, 1)
                dve.wait_ge(s_chain, b * 2 + (n + 3))
                dve.sem_inc(s_tick, 1)

            def split_weight(w):
                dve.wait_ge(s_whi, w + 1)
                nc.vector.tensor_tensor(WL[:, w, :, :], WRAW[w], WH[:, w, :, :].bitcast(F32),
                                        ALU.subtract).then_inc(s_wlo, 1)

            run(dve, VECTOR_STEPS, do)

        @block.tensor
        def _(pe):
            for s in fr_free + sc_free + tp_free + [ou_free]:
                pe.sem_inc(s, 1)
            pe.wait_ge(s_cst, 48)
            pe.wait_ge(s_cd, 3)

            def do(b, kind, *a):
                first = isinstance(b, int) and b == -1
                if kind == "xt":
                    t, = a
                    use = ("xt", t)
                    pe.wait_ge(s_xn, b * 2 + (t + 3))
                    fr_wait_turn(pe, b, use)
                    for k in range(KT):
                        ins = nc.tensor.transpose(FR[fr(use)][:, k * P:(k + 1) * P],
                                                  XN[:, t, k * P:(k + 1) * P], ident[:, :])
                    ins.then_inc(fr_full[fr(use)], 1)
                elif kind == "proj":
                    f, w, t = a
                    use = ("proj", f, w)
                    if f == 1 and w == 0:
                        fr_wait_read(pe, b, ("xt", t))
                    if t == 0:
                        if first:
                            pe.wait_ge(s_wlo, w + 1)
                        fr_wait_turn(pe, b, use)
                    cols = slice((1 - f) * 256, (2 - f) * 256)
                    for k in range(KT):
                        ins = three_pass(nc, FR[fr(use)][:, t * 256:(t + 1) * 256],
                                         (XTH[:, k, t * P:(t + 1) * P], XTL[:, k, t * P:(t + 1) * P]),
                                         (WH[:, w, k, cols], WL[:, w, k, cols]), k == 0, k == KT - 1)
                    if t == 1:
                        ins.then_inc(fr_full[fr(use)], 1)
                elif kind == "turn":
                    f, w, t, g = a
                    use = ("turn", *a)
                    pe.wait_ge(s_lo, b * 8 + (4 * f + 2 * w + t + 5))
                    fr_wait_turn(pe, b, use)
                    for p in range(4):
                        c = g * 8 + 2 * p
                        ins = nc.tensor.transpose(
                            FR[fr(use)][:, p * P:(p + 1) * P].bitcast(F32R),
                            STK[:, t, c:c + 2, :, :].rearrange("p h a d -> p (h a d)"), ident_r[:, :])
                    ins.then_inc(fr_full[fr(use)], 1)
                elif kind == "score":
                    n, = a
                    u, j = n // 3, n % 3
                    hf = u // 4
                    bank = SC[j]
                    if n % 12 == 0:
                        for g in range(2):
                            fr_wait_read(pe, b if hf else b - 1, ("turn", 1 - hf, 1, 1, g))
                        if isinstance(b, int) and b == 0 and n == 0:
                            pe.wait_ge(s_zero, 2)
                    pe.wait_ge(sc_free[j], b * 8 + (u + 1))
                    if j == 0:
                        nc.tensor.matmul(bank[:, :].rearrange("p (h n) -> p h n", h=4), identb[:, :],
                                         maskb[:, :].unsqueeze(1).to_broadcast([P, 4, P]), start=True, stop=False)
                        for c in range(2):
                            pr = 2 * (u % 4) + c
                            ins = nc.tensor.matmul(
                                bank[:, c * 256:(c + 1) * 256].rearrange("p (h n) -> p h n", h=2),
                                QT[:, hf, pr, 0:P], KTT[:, hf, pr, :, 0:P], start=False, stop=c == 1)
                    else:
                        pr = 2 * (u % 4) + j - 1
                        nc.tensor.matmul(bank[:, :].rearrange("p (h n) -> p h n", h=2),
                                         QT[:, hf, pr, P:S], KTT[:, hf, pr, :, :], start=True, stop=False)
                        ins = nc.tensor.matmul(
                            bank[:, :].rearrange("p (h n) -> p h n", h=2)[:, :, P:S], identb[:, :],
                            maskb[:, :].unsqueeze(1).to_broadcast([P, 2, P]), start=False, stop=True)
                    ins.then_inc(sc_full[j], 1)
                elif kind == "flip":
                    n, = a
                    u, j = n // 3, n % 3
                    pe.wait_ge(sc_free[j], b * 8 + (u + 2))
                    pe.wait_ge(tp_free[n % 2], b * 12 + (n // 2 + 1))
                    for c in range(4):
                        ins = nc.tensor.transpose(TP[n % 2][:, c * P:(c + 1) * P], PR[:, j, c * P:(c + 1) * P],
                                                  ident[:, :])
                    ins.then_inc(tp_full[n % 2], 1)
                elif kind == "pv":
                    u, = a
                    hf = u // 4
                    if u % 4 == 0:
                        v = (b if hf else b - 1, ("proj", 1 - hf, 2))
                        fr_wait_read(pe, *v)
                    if u == 0 and not (isinstance(b, int) and b == 0):
                        pe.wait_ge(tl_free, b * 4)
                    for n in (3 * u + 1, 3 * u + 2):
                        pe.wait_ge(tp_free[n % 2], b * 12 + (n // 2 + 2))
                    pe.wait_ge(ou_free, b * 16 + (2 * u + 1))
                    for h in range(4):
                        nc.tensor.matmul(OU[32 * h:32 * h + 32, 0:S], V[:, hf, 0, 4 * (u % 4) + h, :],
                                         PT[:, u % 2, h, 0:S], start=True, stop=False, tile_position=(0, 32 * h))
                    for h in range(4):
                        ins = nc.tensor.matmul(OU[32 * h:32 * h + 32, P:S], V[:, hf, 1, 4 * (u % 4) + h, :],
                                               PT[:, u % 2, h, S:384], start=False, stop=True,
                                               tile_position=(0, 32 * h))
                    ins.then_inc(ou_full, 1)
                elif kind == "out":
                    u, = a
                    pe.wait_ge(ou_free, b * 16 + (2 * u + 2))
                    for t in range(TPB):
                        ins = nc.tensor.transpose(OU[:, t * P:(t + 1) * P], OT[:, u % 2, t * P:(t + 1) * P],
                                                  ident[:, :])
                    ins.then_inc(ou_full, 1)
                elif kind == "at":
                    t, = a
                    if t == 0:
                        pe.wait_ge(ou_free, b * 16 + 1)
                    else:
                        pe.wait_ge(tl_free, b * 4 - 2)
                    for k in range(KT):
                        ins = nc.tensor.transpose(OU[:, k * P:(k + 1) * P], AO[:, t, k * P:(k + 1) * P], ident[:, :])
                    ins.then_inc(tl_full, 1)
                elif kind == "o":
                    t, part = a
                    if part == 0:
                        pe.wait_ge(tl_free, b * 4 + (2 * t - 3))
                    for k in (2 * part, 2 * part + 1):
                        ins = three_pass(nc, OU[:, :], (ATH[:, k, :], ATL[:, k, :]),
                                         (WH[:, 3, k, :], WL[:, 3, k, :]), k == 0, k == KT - 1)
                    if part == 1:
                        ins.then_inc(tl_full, 1)

            run(pe, TENSOR_STEPS, do)


def norm_phase(nc, X, PB, ident, XTH, XTL, tag):
    with ExitStack() as ctx:
        sb, sem = alloc(nc, ctx)
        XN = sb(f"nXN{tag}", [P, 4, D])
        st = sb(f"nst{tag}", [P, 4, 6])
        mv = sb(f"nmv{tag}", [P, 4, 2])
        ve = sb(f"nve{tag}", [P, 4])
        half = sb(f"nhalf{tag}", [P, 4])
        rstd = sb(f"nrstd{tag}", [P, 4])
        s_half, s_chain, s_tick, s_ve, s_pow = (sem(f"n{x}{tag}") for x in ("half", "chain", "tick", "ve", "pow"))
        s_xn, s_xp, s_hi, s_lo = (sem(f"n{x}{tag}") for x in ("xn", "xp", "hi", "lo"))
        block = ctx.enter_context(nc.Block())

        @block.gpsimd
        def _(pool):
            nc.gpsimd.memset(half[:, :], -0.5).then_inc(s_half, 1)
            pool.wait_ge(s_half, 1)
            with pool.Fori(0, NT // 4) as i:
                pool.wait_ge(s_ve, i + 1)
                nc.gpsimd.tensor_tensor(rstd[:, :], ve[:, :], half[:, :], ALU.pow).then_inc(s_pow, 1)

        @block.vector
        def _(dve):
            with dve.Fori(0, NT // 4) as i:
                link = Chain(dve, s_chain, i * 2, s_tick)
                x = X[:, bass.ds(i * 4, 4), :]
                for t in range(4):
                    ins = nc.vector.bn_stats(st[:, t, :], x[:, t, :])
                link(ins, alone=True)
                for t in range(4):
                    ins = nc.vector.bn_aggr(mv[:, t, :], st[:, t, :])
                link(ins)
                nc.vector.tensor_scalar(ve[:, :], mv[:, :, 1], EPS, None, ALU.add).then_inc(s_ve, 1)
                dve.wait_ge(s_pow, i + 1)
                for t in range(4):
                    nc.vector.tensor_scalar(XN[:, t, :], x[:, t, :], mv[:, t, 0:1], rstd[:, t:t + 1],
                                            ALU.subtract, ALU.mult).then_inc(s_xn, 1)
                for t in range(4):
                    dve.wait_ge(s_hi, i * 4 + t + 1)
                    cols = bass.ds(i * 512 + t * P, P)
                    nc.vector.tensor_tensor(XTL[:, :, cols], PB[t][:, :].rearrange("p (k n) -> p k n", k=KT),
                                            XTH[:, :, cols].bitcast(F32), ALU.subtract).then_inc(s_lo, 1)

        @block.scalar
        def _(act):
            with act.Fori(0, NT // 4) as i:
                for t in range(4):
                    act.wait_ge(s_xp, i * 4 + t + 1)
                    nc.scalar.copy(XTH[:, :, bass.ds(i * 512 + t * P, P)],
                                   PB[t][:, :].rearrange("p (k n) -> p k n", k=KT)).then_inc(s_hi, 1)

        @block.tensor
        def _(pe):
            with pe.Fori(0, NT // 4) as i:
                for t in range(4):
                    pe.wait_ge(s_xn, i * 4 + t + 1)
                    for k in range(KT):
                        ins = nc.tensor.transpose(PB[t][:, k * P:(k + 1) * P], XN[:, t, k * P:(k + 1) * P], ident[:, :])
                    ins.then_inc(s_xp, 1)


def swiglu_phase(nc, X, PB, XTH, XTL, F, gu_in, d_in, gu_scale, d_scale, tag):
    quant = gu_scale is not None
    C = F // 256
    with ExitStack() as ctx:
        sb, sem = alloc(nc, ctx)
        GUH = sb(f"GUH{tag}", [P, 2, 2, KT, P], F32R)
        GUL = sb(f"GUL{tag}", [P, 2, 2, KT, P], F32R)
        DH = sb(f"DH{tag}", [P, 2, D], F32R)
        DL = sb(f"DL{tag}", [P, 2, D], F32R)
        raw = sb(f"raw{tag}", [P, 3, 1024], I32 if quant else F32)
        w32 = sb(f"w32{tag}", [P, 1024]) if quant else None
        scl = sb(f"scl{tag}", [P, 3, 1024]) if quant else None
        HH = sb(f"HH{tag}", [P, 6, D], F32R)
        HL = sb(f"HL{tag}", [P, 6, D], F32R)
        SG = sb(f"SG{tag}", [P, 2, D])
        HF = sb(f"HF{tag}", [P, 2, D])
        s_raw = [sem(f"raw{n}{tag}") for n in range(3)]
        s_cvt, s_mul, s_whi = sem(f"cvt{tag}"), sem(f"mul{tag}"), sem(f"whi{tag}")
        s_w = sem(f"w{tag}")
        s_gu, s_silu, s_h, s_hhi, s_hlo = (sem(f"{x}{tag}") for x in ("gu", "silu", "h", "hhi", "hlo"))
        s_dn, s_xadd, s_sptick = sem(f"dn{tag}"), sem(f"xadd{tag}"), sem(f"sptick{tag}")
        block = ctx.enter_context(nc.Block())
        ORDER = [("gu", 0, 0), ("gu", 0, 1), ("gu", 0, 2), ("gu", 0, 3), ("gu", 1, 0), ("gu", 1, 1), ("dn", 0),
                 ("gu", 1, 2), ("dn", 1), ("gu", 1, 3), ("dn", 2), ("dn", 3)]

        def looped(eng, body):
            with eng.Fori(0, C - 1) as i:
                body(i, True)
            body(C - 1, False)

        def fetch(sp, c, slot):
            one = bass.ds(c, 1)
            if slot < 2:
                src = gu_in[one, slot].rearrange("a p n -> (a p) n")
            else:
                src = d_in[one].rearrange("a p n -> (a p) n")
            sp.dma_start(raw[:, slot, :], src).then_inc(s_raw[slot], 16)
            if quant:
                s = (gu_scale[one, slot] if slot < 2 else d_scale[one]).to_broadcast([P, 1024])
                sp.dma_start(scl[:, slot, :], s).then_inc(s_raw[slot], 16)

        per = 32 if quant else 16

        @block.sync
        def _(sp):
            for slot in (0, 1, 2):
                fetch(sp, 0, slot)
            with sp.Fori(0, C - 1) as i:
                for slot in (0, 1, 2):
                    wait_alone(sp, s_w, i * 3 + slot + 1, s_sptick)
                    fetch(sp, i + 1, slot)

        @block.gpsimd
        def _(pool):
            def body(i, _):
                for slot in range(3):
                    hi = GUH[:, slot] if slot < 2 else DH[:, :, :]
                    lo = GUL[:, slot] if slot < 2 else DL[:, :, :]
                    pat = "p a k n -> p (a k n)" if slot < 2 else "p k n -> p (k n)"
                    src = raw[:, slot, :]
                    if quant:
                        pool.wait_ge(s_cvt, i * 3 + slot + 1)
                        nc.gpsimd.tensor_tensor(w32[:, :], w32[:, :], scl[:, slot, :], ALU.mult).then_inc(s_mul, 1)
                        src = w32[:, :]
                    pool.wait_ge(s_whi, i * 3 + slot + 1)
                    nc.gpsimd.tensor_tensor(lo.rearrange(pat), src, hi.rearrange(pat).bitcast(F32),
                                            ALU.subtract).then_inc(s_w, 1)
            looped(pool, body)

        @block.scalar
        def _(act):
            def to_float(c, slot, first=False):
                if quant:
                    act.wait_ge(s_raw[slot], (c + 1) * per)
                    if not first or slot:
                        act.wait_ge(s_w, c * 3 + slot)
                    nc.scalar.copy(w32[:, :], raw[:, slot, :]).then_inc(s_cvt, 1)

            def to_hi(c, slot, first=False):
                hi = GUH[:, slot].rearrange("p a k n -> p (a k n)") if slot < 2 else \
                    DH[:, :, :].rearrange("p k n -> p (k n)")
                if slot == 2 and not first:
                    act.wait_ge(s_dn, c * 16 + 16)
                if quant:
                    act.wait_ge(s_mul, c * 3 + slot + 1)
                    nc.scalar.copy(hi, w32[:, :]).then_inc(s_whi, 1)
                else:
                    act.wait_ge(s_raw[slot], (c + 1) * per)
                    nc.scalar.copy(hi, raw[:, slot, :]).then_inc(s_whi, 1)

            for slot in range(3):
                to_float(0, slot, True)
                to_hi(0, slot, True)

            def body(i, more):
                for s in range(8):
                    slot, t = s // 4, s % 4
                    act.wait_ge(s_gu, i * 8 + s + 1)
                    nc.scalar.activation(SG[:, s % 2, :], PB[2 * (s % 2)][:, :], ACT.Silu).then_inc(s_silu, 1)
                    h = t if slot == 0 else 4 + t % 2
                    act.wait_ge(s_h, i * 8 + s + 3)
                    act.wait_ge(s_dn, i * 16 + 4 * t + (4 if slot == 0 else 12))
                    nc.scalar.copy(HH[:, h, :], HF[:, s % 2, :]).then_inc(s_hhi, 1)
                    if more and s == 4:
                        to_float(i + 1, 0)
                    if more and s == 5:
                        to_hi(i + 1, 0)
                if more:
                    for slot in (1, 2):
                        to_float(i + 1, slot)
                        to_hi(i + 1, slot)
            looped(act, body)

        @block.vector
        def _(dve):
            def body(i, _):
                s = 0
                for step in ORDER:
                    if step[0] == "gu":
                        slot, t = step[1:]
                        h = t if slot == 0 else 4 + t % 2
                        dve.wait_ge(s_silu, i * 8 + s + 1)
                        nc.vector.tensor_tensor(HF[:, s % 2, :], PB[2 * (s % 2) + 1][:, :], SG[:, s % 2, :],
                                                ALU.mult).then_inc(s_h, 1)
                        dve.wait_ge(s_hhi, i * 8 + s + 1)
                        nc.vector.tensor_tensor(HL[:, h, :], HF[:, s % 2, :], HH[:, h, :].bitcast(F32),
                                                ALU.subtract).then_inc(s_hlo, 1)
                        s += 1
                    else:
                        t = step[1]
                        for j in range(4):
                            dve.wait_ge(s_dn, i * 16 + t * 4 + j + 17)
                            x = X[:, 4 * t + j, :]
                            nc.vector.tensor_tensor(x, x, PB[4 + j][:, :], ALU.add).then_inc(s_xadd, 1)
            looped(dve, body)

        @block.tensor
        def _(pe):
            pe.sem_inc(s_h, 2)
            pe.sem_inc(s_dn, 16)
            pe.sem_inc(s_xadd, 4)

            def body(i, _):
                s = 0
                for step in ORDER:
                    if step[0] == "gu":
                        slot, t = step[1:]
                        if t == 0:
                            pe.wait_ge(s_w, i * 3 + slot + 1)
                        pe.wait_ge(s_h, i * 8 + s + 1)
                        tok = slice(t * 512, (t + 1) * 512)
                        for a in range(2):
                            for k in range(KT):
                                ins = three_pass(nc, PB[2 * (s % 2) + a][:, :],
                                                 (GUH[:, slot, a, k, :], GUL[:, slot, a, k, :]),
                                                 (XTH[:, k, tok], XTL[:, k, tok]), k == 0, k == KT - 1)
                        ins.then_inc(s_gu, 1)
                        s += 1
                    else:
                        t = step[1]
                        if t == 0:
                            pe.wait_ge(s_w, i * 3 + 3)
                        pe.wait_ge(s_hlo, i * 8 + 4 + t + 1)
                        for j in range(4):
                            pe.wait_ge(s_xadd, i * 16 + t * 4 + j + 1)
                            for f in range(2):
                                h = t if f == 0 else 4 + t % 2
                                c = slice(j * P, (j + 1) * P)
                                ins = three_pass(nc, PB[4 + j][:, :], (HH[:, h, c], HL[:, h, c]),
                                                 (DH[:, f, :], DL[:, f, :]), f == 0, f == 1)
                            ins.then_inc(s_dn, 1)
            looped(pe, body)


def taylor_phase(nc, X, PB, XTH, XTL, ug_in, point_in, fuse_in, disc_in):
    with ExitStack() as ctx:
        sb, sem = alloc(nc, ctx)
        UGH = sb("UGH", [P, 2, KT, P], F32R)
        UGL = sb("UGL", [P, 2, KT, P], F32R)
        FH = sb("FH", [P, G + 1, D], F32R)
        FL = sb("FL", [P, G + 1, D], F32R)
        rawf = sb("rawf", [P, D * 3])
        point = sb("point", [P, 1])
        disc = sb("disc", [P, G])
        cdis = sb("cdis", [P, G])
        DEL = sb("DEL", [P, D])
        KEEP = sb("KEEP", [P, D])
        A = sb("A", [P, 2, D])
        AH = sb("AH", [P, G + 1, D], F32R)
        AL = sb("AL", [P, G + 1, D], F32R)
        s_in, s_raw, s_free, s_c, s_wm, s_whi, s_wlo = (
            sem(f"t{x}") for x in ("in", "raw", "free", "c", "wm", "whi", "wlo"))
        s_ug, s_a, s_ahi, s_alo, s_out, s_xadd, s_ch, s_af = (
            sem(f"t{x}") for x in ("ug", "a", "ahi", "alo", "out", "xadd", "ch", "af"))
        block = ctx.enter_context(nc.Block())
        NW = 2 + G + 1

        def split_of(w, part):
            if w < 2:
                return (UGH, UGL)[part][:, w].rearrange("p k n -> p (k n)")
            return (FH, FL)[part][:, w - 2, :]

        @block.sync
        def _(sp):
            sp.dma_start(point[:, :], point_in).then_inc(s_in, 16)
            sp.dma_start(disc[:, :], disc_in.to_broadcast([P, G])).then_inc(s_in, 16)
            for w in range(NW):
                if w >= 3:
                    sp.wait_ge(s_wlo, w - 2)
                src = ug_in[w] if w < 2 else fuse_in[w - 2]
                sp.dma_start(rawf[:, (w % 3) * D:(w % 3 + 1) * D], src).then_inc(s_raw, 16)
                sp.wait_ge(s_raw, 16 * (w + 1))

        @block.scalar
        def _(act):
            act.wait_ge(s_in, 32)
            nc.scalar.activation(cdis[:, :], disc[:, :], ACT.Exp, scale=-1.0).then_inc(s_c, 1)
            for w in range(NW):
                act.wait_ge(s_raw, 16 * (w + 1))
                r = rawf[:, (w % 3) * D:(w % 3 + 1) * D]
                if w >= 3:
                    act.wait_ge(s_c, w - 2)
                    nc.scalar.mul(r, r, cdis[:, w - 3:w - 2]).then_inc(s_c, 1)
                    act.wait_ge(s_c, w - 1)
                nc.scalar.copy(split_of(w, 0), r).then_inc(s_whi, 1)
            with act.Fori(0, 4) as i:
                for m in range(G + 1):
                    act.wait_ge(s_a, i * 7 + m + 1)
                    if m < G:
                        act.wait_ge(s_af, i * G + m + 1)
                    nc.scalar.copy(AH[:, m, :], A[:, m % 2, :]).then_inc(s_ahi, 1)

        @block.vector
        def _(dve):
            for w in range(NW):
                dve.wait_ge(s_whi, w + 1)
                nc.vector.tensor_tensor(split_of(w, 1), rawf[:, (w % 3) * D:(w % 3 + 1) * D],
                                        split_of(w, 0).bitcast(F32), ALU.subtract).then_inc(s_wlo, 1)
            with dve.Fori(0, 4) as i:
                link = Chain(dve, s_ch, i * 3)
                dve.wait_ge(s_ug, i + 1)
                nc.vector.tensor_copy(A[:, 0, :], PB[0][:, :]).then_inc(s_a, 1)
                link(nc.vector.tensor_scalar(DEL[:, :], PB[1][:, :], point[:, 0:1], None, ALU.subtract))
                link(nc.vector.scalar_tensor_tensor(KEEP[:, :], DEL[:, :], -THD, DEL[:, :], ALU.is_ge, ALU.mult))
                link(nc.vector.scalar_tensor_tensor(KEEP[:, :], DEL[:, :], THD, KEEP[:, :], ALU.is_le, ALU.mult))
                for m in range(G + 1):
                    if m < G:
                        dve.wait_ge(s_a, i * 7 + m + 1)
                        dve.wait_ge(s_alo, i * 7 + m)
                        nc.vector.tensor_tensor(A[:, (m + 1) % 2, :], A[:, m % 2, :],
                                                (KEEP if m + 1 == 5 else DEL)[:, :], ALU.mult).then_inc(s_a, 1)
                    dve.wait_ge(s_ahi, i * 7 + m + 1)
                    nc.vector.tensor_tensor(AL[:, m, :], A[:, m % 2, :], AH[:, m, :].bitcast(F32),
                                            ALU.subtract).then_inc(s_alo, 1)
                for j in range(4):
                    dve.wait_ge(s_out, i * 4 + j + 1)
                    x = X[:, bass.ds(i * 4 + j, 1), :].rearrange("p a n -> p (a n)")
                    nc.vector.tensor_tensor(x, x, PB[4 + j][:, :], ALU.add).then_inc(s_xadd, 1)

        @block.tensor
        def _(pe):
            pe.sem_inc(s_af, G)
            pe.wait_ge(s_wlo, NW)
            with pe.Fori(0, 4) as i:
                tok = bass.ds(i * 512, 512)
                for a in range(2):
                    for k in range(KT):
                        ins = three_pass(nc, PB[a][:, :], (UGH[:, a, k, :], UGL[:, a, k, :]),
                                         (XTH[:, k, tok], XTL[:, k, tok]), k == 0, k == KT - 1)
                ins.then_inc(s_ug, 1)
                for m in range(G + 1):
                    pe.wait_ge(s_alo, i * 7 + m + 1)
                    for j in range(4):
                        c = slice(j * P, (j + 1) * P)
                        ins = three_pass(nc, PB[4 + j][:, :], (AH[:, m, c], AL[:, m, c]),
                                         (FH[:, m, :], FL[:, m, :]), m == 0, m == G)
                        if m == G:
                            ins.then_inc(s_out, 1)
                    if m < G:
                        ins.then_inc(s_af, 1)
                pe.wait_ge(s_xadd, i * 4 + 4)


def expert_phase(nc, X, PB, ident, ra_in, rb_in, bm_in, iota_in, out):
    NA = E8 * R16
    with ExitStack() as ctx:
        sb, sem = alloc(nc, ctx)
        RA = sb("eRA", [P, KT, NA + E8])
        rb = sb("erb", [P, E8])
        bmr = sb("ebmr", [P, D])
        BH = sb("eBH", [P, D], F32R)
        BL = sb("eBL", [P, D], F32R)
        iota = sb("eiota", [P, E8])
        XN = sb("eXN", [P, 4, D])
        XT = sb("eXT", [P, 4, D])
        st = sb("est", [P, 4, 6])
        mv = sb("emv", [P, 4, 2])
        ve = sb("eve", [P, 4])
        half = sb("ehalf", [P, 4])
        rstd = sb("erstd", [P, 4])
        LG = sb("eLG", [P, 4, E8])
        nm = sb("enm", [P, 4])
        EX = sb("eEX", [P, 4, E8])
        sm = sb("esm", [P, 4])
        top = sb("etop", [P, 4, 8])
        idx = sb("eidx", [P, 4, 8], U32)
        idf = sb("eidf", [P, 4, 8])
        gs = sb("egs", [P, 4])
        gt = sb("egt", [P, 4, 2])
        w1 = sb("ew1", [P, 4, E8])
        w2 = sb("ew2", [P, 4, E8])
        HW = sb("eHW", [P, 4, NA])
        HTH = sb("eHTH", [P, 4, NA], F32R)
        HTL = sb("eHTL", [P, 4, NA], F32R)
        Y = sb("eY", [P, 4, D])
        names = ("in", "half", "chain", "ve", "pow", "xn", "xp", "xt", "h", "lg", "ex", "hw", "hp", "hh", "hl",
                 "o", "y", "st", "bh", "bl", "tick", "sptick")
        s = {n: sem(f"e{n}") for n in names}
        block = ctx.enter_context(nc.Block())
        turns = NT // 4

        @block.sync
        def _(sp):
            sp.dma_start(RA[:, :, :], ra_in).then_inc(s["in"], 16)
            sp.dma_start(rb[:, :], rb_in.to_broadcast([P, E8])).then_inc(s["in"], 16)
            sp.dma_start(bmr[:, :], bm_in).then_inc(s["in"], 16)
            sp.dma_start(iota[:, :], iota_in).then_inc(s["in"], 16)
            with sp.Fori(0, turns) as i:
                for t in range(4):
                    wait_alone(sp, s["y"], i * 4 + t + 1, s["sptick"])
                    sp.dma_start(out[bass.ds(i * 4 + t, 1)].rearrange("a p n -> (a p) n"), Y[:, t, :]).then_inc(s["st"], 16)
                wait_alone(sp, s["st"], i * 64 + 80, s["sptick"])
            sp.wait_ge(s["st"], turns * 64 + 16)

        @block.gpsimd
        def _(pool):
            nc.gpsimd.memset(half[:, :], -0.5).then_inc(s["half"], 1)
            pool.wait_ge(s["half"], 1)
            with pool.Fori(0, turns) as i:
                pool.wait_ge(s["ve"], i + 1)
                nc.gpsimd.tensor_tensor(rstd[:, :], ve[:, :], half[:, :], ALU.pow).then_inc(s["pow"], 1)

        @block.scalar
        def _(act):
            act.wait_ge(s["in"], 64)
            nc.scalar.copy(BH[:, :], bmr[:, :]).then_inc(s["bh"], 1)
            with act.Fori(0, turns) as i:
                for t in range(4):
                    act.wait_ge(s["xp"], i * 4 + t + 1)
                    nc.scalar.copy(XT[:, t, :], PB[t][:, :]).then_inc(s["xt"], 1)
                act.wait_ge(s["lg"], i + 1)
                nc.scalar.activation(EX[:, :, :], LG[:, :, :], ACT.Exp).then_inc(s["ex"], 1)
                for t in range(4):
                    act.wait_ge(s["hp"], i * 4 + t + 1)
                    nc.scalar.copy(HTH[:, t, :], PB[t][:, 0:NA]).then_inc(s["hh"], 1)

        @block.vector
        def _(dve):
            dve.wait_ge(s["bh"], 1)
            nc.vector.tensor_tensor(BL[:, :], bmr[:, :], BH[:, :].bitcast(F32), ALU.subtract).then_inc(s["bl"], 1)
            dve.sem_inc(s["st"], 16)
            with dve.Fori(0, turns) as i:
                link = Chain(dve, s["chain"], i * 17, s["tick"])
                x = X[:, bass.ds(i * 4, 4), :]
                for t in range(4):
                    ins = nc.vector.bn_stats(st[:, t, :], x[:, t, :])
                link(ins, alone=True)
                for t in range(4):
                    ins = nc.vector.bn_aggr(mv[:, t, :], st[:, t, :])
                link(ins)
                nc.vector.tensor_scalar(ve[:, :], mv[:, :, 1], EPS, None, ALU.add).then_inc(s["ve"], 1)
                dve.wait_ge(s["pow"], i + 1)
                for t in range(4):
                    nc.vector.tensor_scalar(XN[:, t, :], x[:, t, :], mv[:, t, 0:1], rstd[:, t:t + 1],
                                            ALU.subtract, ALU.mult).then_inc(s["xn"], 1)
                for t in range(4):
                    dve.wait_ge(s["h"], i * 4 + t + 1)
                    ins = nc.vector.tensor_tensor(LG[:, t, :], PB[4 + t][:, NA:NA + E8], rb[:, :], ALU.add)
                link(ins)
                link(nc.vector.tensor_reduce(nm[:, :], LG[:, :, :], axis=AXX, op=ALU.max))
                nc.vector.tensor_tensor(LG[:, :, :], LG[:, :, :], nm[:, :].unsqueeze(2).to_broadcast([P, 4, E8]),
                                        ALU.subtract).then_inc(s["lg"], 1)
                dve.wait_ge(s["ex"], i + 1)
                link(nc.vector.tensor_reduce(sm[:, :], EX[:, :, :], axis=AXX, op=ALU.add))
                link(nc.vector.reciprocal(sm[:, :], sm[:, :]))
                link(nc.vector.tensor_tensor(EX[:, :, :], EX[:, :, :], sm[:, :].unsqueeze(2).to_broadcast([P, 4, E8]),
                                             ALU.mult), alone=True)
                for t in range(4):
                    ins = nc.vector.max(top[:, t, :], EX[:, t, :])
                link(ins, alone=True)
                for t in range(4):
                    ins = nc.vector.max_index(idx[:, t, :], top[:, t, :], EX[:, t, :])
                link(ins)
                link(nc.vector.tensor_tensor(gs[:, :], top[:, :, 0], top[:, :, 1], ALU.add))
                link(nc.vector.tensor_copy(idf[:, :, :], idx[:, :, :]))
                link(nc.vector.reciprocal(gs[:, :], gs[:, :]))
                link(nc.vector.tensor_tensor(gt[:, :, :], top[:, :, 0:2], gs[:, :].unsqueeze(2).to_broadcast([P, 4, 2]),
                                             ALU.mult))
                link(nc.vector.tensor_scalar(gt[:, :, :], gt[:, :, :], 0.5, None, ALU.mult))
                for w, c in ((w1, 0), (w2, 1)):
                    ins = nc.vector.tensor_tensor(w[:, :, :], iota[:, :].unsqueeze(1).to_broadcast([P, 4, E8]),
                                                  idf[:, :, c:c + 1].to_broadcast([P, 4, E8]), ALU.is_equal)
                link(ins)
                for w, c in ((w1, 0), (w2, 1)):
                    ins = nc.vector.tensor_tensor(w[:, :, :], w[:, :, :], gt[:, :, c:c + 1].to_broadcast([P, 4, E8]),
                                                  ALU.mult)
                link(ins)
                link(nc.vector.tensor_tensor(w1[:, :, :], w1[:, :, :], w2[:, :, :], ALU.add))
                for t in range(4):
                    nc.vector.tensor_tensor(HW[:, t, :].rearrange("p (e r) -> p e r", e=E8),
                                            PB[4 + t][:, 0:NA].rearrange("p (e r) -> p e r", e=E8),
                                            w1[:, t, :].unsqueeze(2).to_broadcast([P, E8, R16]),
                                            ALU.mult).then_inc(s["hw"], 1)
                for t in range(4):
                    dve.wait_ge(s["hh"], i * 4 + t + 1)
                    nc.vector.tensor_tensor(HTL[:, t, :], PB[t][:, 0:NA], HTH[:, t, :].bitcast(F32),
                                            ALU.subtract).then_inc(s["hl"], 1)
                for t in range(4):
                    dve.wait_ge(s["o"], i * 4 + t + 1)
                    if t == 0:
                        dve.wait_ge(s["st"], i * 64 + 16)
                    nc.vector.tensor_tensor(Y[:, t, :], PB[4 + t][:, :], x[:, t, :], ALU.add).then_inc(s["y"], 1)

        @block.tensor
        def _(pe):
            pe.wait_ge(s["in"], 64)
            pe.wait_ge(s["bl"], 1)
            with pe.Fori(0, turns) as i:
                for t in range(4):
                    pe.wait_ge(s["xn"], i * 4 + t + 1)
                    for k in range(KT):
                        ins = nc.tensor.transpose(PB[t][:, k * P:(k + 1) * P], XN[:, t, k * P:(k + 1) * P], ident[:, :])
                    ins.then_inc(s["xp"], 1)
                for t in range(4):
                    pe.wait_ge(s["xt"], i * 4 + t + 1)
                    for k in range(KT):
                        ins = nc.tensor.matmul(PB[4 + t][:, 0:NA + E8], XT[:, t, k * P:(k + 1) * P], RA[:, k, :],
                                               start=k == 0, stop=k == KT - 1)
                    ins.then_inc(s["h"], 1)
                for t in range(4):
                    pe.wait_ge(s["hw"], i * 4 + t + 1)
                    nc.tensor.transpose(PB[t][:, 0:NA], HW[:, t, :], ident[:, :]).then_inc(s["hp"], 1)
                for t in range(4):
                    pe.wait_ge(s["hl"], i * 4 + t + 1)
                    three_pass(nc, PB[4 + t][:, :], (HTH[:, t, :], HTL[:, t, :]), (BH[:, :], BL[:, :]),
                               True, True).then_inc(s["o"], 1)
                pe.wait_ge(s["y"], i * 4 + 4)


def dump_phase(nc, X, out):
    with nc.semaphore("dump") as s, nc.Block() as block:
        @block.sync
        def _(sp):
            for j in range(NT):
                sp.dma_start(out[j], X[:, j, :]).then_inc(s, 16)
            sp.wait_ge(s, 16 * NT)


def build(nc, d, out, stop=9):
    with ExitStack() as ctx:
        X = ctx.enter_context(nc.sbuf_tensor("X", [P, NT, D], F32))
        ident = ctx.enter_context(nc.sbuf_tensor("ident", [P, P], F32))
        PB = [ctx.enter_context(nc.psum_tensor(f"PB{i}", [P, D], F32)) for i in range(8)]
        attention_phase(nc, X, PB, ident, d["x"], d["wqkvo"], d["rope"], d["mask"], d["ident"])
        if stop == 0:
            return dump_phase(nc, X, out)
        with ExitStack() as c2:
            XTH = c2.enter_context(nc.sbuf_tensor("XTH", [P, KT, TOK], F32R))
            XTL = c2.enter_context(nc.sbuf_tensor("XTL", [P, KT, TOK], F32R))
            norm_phase(nc, X, PB, ident, XTH, XTL, "a")
            swiglu_phase(nc, X, PB, XTH, XTL, F0, d["gu0"], d["d0"], d["sgu0"], d["sd0"], "a")
            if stop == 1:
                return dump_phase(nc, X, out)
            norm_phase(nc, X, PB, ident, XTH, XTL, "b")
            taylor_phase(nc, X, PB, XTH, XTL, d["ug"], d["point"], d["fuse"], d["disc"])
            swiglu_phase(nc, X, PB, XTH, XTL, F1, d["gu1"], d["d1"], None, None, "b")
            if stop == 2:
                return dump_phase(nc, X, out)
        expert_phase(nc, X, PB, ident, d["ra"], d["rb"], d["bm"], d["iota"], out)


def layouts(np, a):
    c = np.ascontiguousarray

    def rows(w):
        return c(w.reshape(KT, P, -1).transpose(1, 0, 2))

    def gate_up(g, u, F):
        def one(w):
            w = np.concatenate([w, np.zeros((F - w.shape[0], D), w.dtype)]) if w.shape[0] < F else w
            return w.T.reshape(KT, P, F // 256, 2, P).transpose(2, 3, 1, 0, 4)
        return c(np.stack([one(g), one(u)], axis=3)).reshape(F // 256, 2, P, 2 * KT * P)

    def down(w, F):
        w = w.T
        w = np.concatenate([w, np.zeros((F - w.shape[0], D), w.dtype)]) if w.shape[0] < F else w
        return c(w.reshape(F // 256, 2, P, D).transpose(0, 2, 1, 3)).reshape(F // 256, P, 2 * D)

    def scale_gu(g, u):
        def one(s):
            return s.reshape(F0 // 256, 2, P, KT).transpose(0, 1, 3, 2)
        return c(np.stack([one(g), one(u)], axis=2)).reshape(F0 // 256, 2, 2 * KT * P)

    inv = (1.0 / 10000.0 ** (np.arange(0, HD, 2)[:HD // 2].astype(np.float32) / HD))
    f = np.outer(np.arange(S), inv).astype(np.float32)
    cos, sin = np.cos(f).astype(np.float32), np.sin(f).astype(np.float32)
    cos2 = np.repeat(cos, 2, axis=1)
    sin2 = np.stack([-sin, sin], axis=-1).reshape(S, HD)
    q = np.float32(HD ** -0.5)
    rope = np.stack([cos2 * q, sin2 * q, cos2, sin2]).astype(np.float32).reshape(4, TPB, P, HD)
    mask = np.where(np.arange(P)[None, :] > np.arange(P)[:, None], np.float32(NEG), np.float32(0))
    fuse = a["L1_attn_fuse_weight"]
    return {
        "x": c(a["L0_attn_x"].reshape(B, TPB, P, D).transpose(0, 2, 1, 3)),
        "wqkvo": np.stack([rows(a[f"L0_attn_w{n}"]) for n in "qkvo"]),
        "rope": c(rope.transpose(2, 0, 1, 3)),
        "mask": mask.astype(np.float32),
        "ident": np.eye(P, dtype=np.float32),
        "gu0": gate_up(a["L0_ffn_gate_q"], a["L0_ffn_up_q"], F0),
        "d0": down(a["L0_ffn_down_q"], F0),
        "sgu0": scale_gu(a["L0_ffn_gate_s"], a["L0_ffn_up_s"]),
        "sd0": c(a["L0_ffn_down_s"].T).reshape(F0 // 256, 2 * D),
        "ug": np.stack([rows(a["L1_attn_up_w"].T).reshape(P, -1), rows(a["L1_attn_gate_w"].T).reshape(P, -1)]),
        "point": c(a["L1_attn_local_point"].reshape(P, 1)),
        "fuse": np.stack([c(a["L1_attn_local_approx_output"].T)] + [c(fuse[:, :, m].T) for m in range(G)]),
        "disc": c(a["L1_attn_discount_factor"].reshape(1, G)),
        "gu1": gate_up(a["L1_attn_ffn_gate_w"], a["L1_attn_ffn_up_w"], F1),
        "d1": down(a["L1_attn_ffn_down_w"], F1),
        "ra": np.concatenate([rows(a["L1_ffn_A"].reshape(E8 * R16, D).T), rows(a["L1_ffn_router_w"].T)], axis=2),
        "rb": c(a["L1_ffn_router_b"].reshape(1, E8)),
        "bm": c(a["L1_ffn_Bm"].transpose(0, 2, 1)).reshape(E8 * R16, D),
        "iota": np.tile(np.arange(E8, dtype=np.float32), (P, 1)),
    }


def program(nc, arrays, stop=9):
    d = {n: nc.dram_tensor(f"in_{n}", v.shape, mybir.dt.from_np(v.dtype), kind="ExternalInput").ap()
         for n, v in arrays.items()}
    out = nc.dram_tensor("out_0", (NT, P, D), F32, kind="ExternalOutput").ap()
    build(nc, d, out, stop)


def kernel(**inputs):
    import numpy as np
    import concourse.bacc as bacc
    from concourse.bass_utils import run_bass_kernel_spmd

    arrays = layouts(np, {n: np.asarray(v) for n, v in inputs.items()})
    nc = bacc.Bacc("TRN2", target_bir_lowering=False, num_devices=1)
    program(nc, arrays)
    r = run_bass_kernel_spmd(nc, [{f"in_{n}": v for n, v in arrays.items()}], core_ids=[0])
    return r.results[0]["out_0"].reshape(B, S, D)
```

```python
from contextlib import ExitStack

import concourse.bass as bass
from concourse import mybir

F32 = mybir.dt.float32
F32R = mybir.dt.float32r
BF16 = mybir.dt.bfloat16
I32 = mybir.dt.int32
U32 = mybir.dt.uint32
ALU = mybir.AluOpType
ACT = mybir.ActivationFunctionType
AXX = mybir.AxisListType.X

P = 128
D = 512
KT = D // P
B, S = 8, 256
TOK = B * S
NT = TOK // P
TPB = S // P
H, HD = 32, 16
NPAIR = H // 2
UNITS = H // 4
F0 = 1792
F1 = 1280
G = 6
E8, R16 = 8, 16
EPS = 1e-5
THD = 2.5
NEG = -3.0e38


class Chain:

    def __init__(self, eng, sem, base, tick=None):
        self.eng, self.sem, self.base, self.tick, self.n = eng, sem, base, tick, 0

    def __call__(self, ins, alone=False):
        self.n += 1
        ins.then_inc(self.sem, 1)
        self.eng.wait_ge(self.sem, self.base + self.n)
        if alone:
            self.eng.sem_inc(self.tick, 1)


def wait_alone(eng, sem, value, tick):
    eng.wait_ge(sem, value)
    eng.sem_inc(tick, 1)


def three_pass(nc, out, lhs, rhs, first, last):
    nc.tensor.matmul(out, lhs[0], rhs[0], start=first, stop=False)
    nc.tensor.matmul(out, lhs[0], rhs[1], start=False, stop=False)
    return nc.tensor.matmul(out, lhs[1], rhs[0], start=False, stop=last)


def steps(text):
    out = []
    for word in text.split():
        early = word.startswith("next-")
        kind, *args = word[5 if early else 0:].split(".")
        out.append((("early",) if early else ()) + (kind, *(int(v) for v in args)))
    return out


def alloc(nc, ctx):
    def sb(name, shape, dt=F32):
        return ctx.enter_context(nc.sbuf_tensor(name, shape, dt))

    def sem(name):
        return ctx.enter_context(nc.semaphore(name))

    return sb, sem


def attention_phase(nc, X, PB, ident, x_in, wqkvo, rope_in, mask_in, ident_in):
    HH = H // 2
    NJ = 3 * UNITS
    with ExitStack() as ctx:
        sb, sem = alloc(nc, ctx)
        WH = sb("WH", [P, 4, KT, D], F32R)
        WL = sb("WL", [P, 4, KT, D], F32R)
        XTH = sb("aXTH", [P, KT, S], F32R)
        XTL = sb("aXTL", [P, KT, S], F32R)
        ATH = sb("ATH", [P, KT, P], F32R)
        ATL = sb("ATL", [P, KT, P], F32R)
        V = sb("V", [P, 2, TPB, HH, 32])
        XN = sb("XN", [P, TPB, D])
        RA = sb("RA", [P, TPB, HH, HD])
        RB = sb("RB", [P, TPB, HH, HD])
        STK = sb("STK", [P, TPB, HH, 4, HD], F32R)
        QT = sb("QT", [P, 2, HH // 2, S], F32R)
        KTT = sb("KTT", [P, 2, HH // 2, 2, S], F32R)
        PR = sb("PR", [P, 3, D])
        PT = sb("PT", [P, 2, 4, 384])
        OT = sb("OT", [P, 2, S])
        AO = sb("AO", [P, TPB, D])
        rope = sb("rope", [P, 4, TPB, HD])
        maskf = sb("maskf", [P, P])
        maskb = sb("maskb", [P, P], BF16)
        identb = sb("identb", [P, P], BF16)
        ident_r = sb("ident_r", [P, P], F32R)
        st = sb("st", [P, TPB, 6])
        mv = sb("mv", [P, TPB, 2])
        ve = sb("ve", [P, TPB])
        half = sb("half", [P, TPB])
        rstd = sb("rstd", [P, TPB])
        nmx = sb("nmx", [P, 3, 4])
        rden = sb("rden", [P, 2, TPB, 4])
        WRAW = [X[:, 4 * w + 4:4 * w + 8, :] for w in range(3)]
        WRAW.append(V[:, :, :, :, :].rearrange("p a t h d -> p (a t h d)").rearrange("p (k n) -> p k n", k=KT))

        s_cst, s_x, s_w = sem("s_cst"), sem("s_x"), [sem(f"s_w{w}") for w in range(4)]
        s_whi, s_wlo, s_zero, s_cd, s_half = sem("s_whi"), sem("s_wlo"), sem("s_zero"), sem("s_cd"), sem("s_half")
        s_chain, s_tick, s_sptick = sem("s_chain"), sem("s_tick"), sem("s_sptick")
        s_ve, s_pow, s_xn, s_xth = sem("s_ve"), sem("s_pow"), sem("s_xn"), sem("s_xth")
        fr_full = [sem(f"fr_full{i}") for i in range(2)]
        fr_free = [sem(f"fr_free{i}") for i in range(2)]
        sc_full = [sem(f"sc_full{i}") for i in range(3)]
        sc_free = [sem(f"sc_free{i}") for i in range(3)]
        tp_full = [sem(f"tp_full{i}") for i in range(2)]
        tp_free = [sem(f"tp_free{i}") for i in range(2)]
        ou_full, ou_free = sem("ou_full"), sem("ou_free")
        tl_full, tl_free = sem("tl_full"), sem("tl_free")
        s_mx, s_rden, s_rr, s_hi, s_lo = sem("s_mx"), sem("s_rden"), sem("s_rr"), sem("s_hi"), sem("s_lo")
        s_ka, s_ath = sem("s_ka"), sem("s_ath")
        SC, TP, FR, OU = PB[0:3], PB[3:5], PB[5:7], PB[7]

        TENSOR_STEPS = steps("""
            flip.0 flip.1 score.3 at.0 flip.2 score.4 score.5 proj.0.1.0 turn.0.0.0.0 o.0.0 o.0.1 proj.0.1.1
            at.1 flip.3 score.6 flip.4 score.7 turn.0.0.0.1 flip.5 score.8 o.1.0 turn.0.0.1.0 turn.0.0.1.1
            o.1.1 proj.0.2.0 proj.0.2.1 pv.0 flip.6 score.9 turn.0.1.0.0 turn.0.1.0.1 out.0 flip.7 flip.8 pv.1
            turn.0.1.1.0 score.10 score.11 out.1 turn.0.1.1.1 flip.9 pv.2 xt.0 out.2 score.12 flip.10 xt.1
            flip.11 score.13 score.14 flip.12 score.15 proj.1.0.0 proj.1.0.1 flip.13 score.16 flip.14
            proj.1.1.0 pv.3 score.17 flip.15 score.18 flip.16 score.19 out.3 proj.1.1.1 turn.1.0.0.0 pv.4
            flip.17 score.20 flip.18 score.21 turn.1.0.0.1 turn.1.0.1.0 out.4 flip.19 score.22 turn.1.0.1.1
            pv.5 proj.1.2.0 turn.1.1.0.0 proj.1.2.1 flip.20 out.5 score.23 turn.1.1.0.1 turn.1.1.1.0 flip.21
            pv.6 flip.22 turn.1.1.1.1 out.6 next-proj.0.0.0 next-score.0 next-score.1 flip.23 next-score.2
            next-proj.0.0.1 pv.7 out.7
        """)
        VECTOR_STEPS = steps("""
            flip.1 score.3 flip.2 stack.0.0.0 at.0 score.4 score.5 o.0.1 stack.0.0.1 rope.0.1 score.6 at.1
            score.7 score.8 stats flip.4 flip.5 norm o.1.1 stack.0.1.0 stack.0.1.1 score.9 out.0 turn.0.1.0.0
            turn.0.1.0.1 flip.7 flip.8 out.1 turn.0.1.1.0 score.10 turn.0.1.1.1 score.11 score.12 flip.10 xt.0
            flip.11 xt.1 score.13 score.14 out.2 score.15 rope.1.0 score.16 flip.13 flip.14 score.17
            stack.1.0.0 score.18 stack.1.0.1 out.3 score.19 flip.16 rope.1.1 flip.17 out.4 score.20 score.21
            stack.1.1.0 stack.1.1.1 score.22 flip.19 turn.1.1.0.0 flip.20 out.5 turn.1.1.0.1 turn.1.1.1.0
            score.23 turn.1.1.1.1 flip.22 out.6 next-score.0 flip.23 next-score.1 next-score.2 next-rope.0.0
            out.7
        """)
        SCALAR_STEPS = steps("""
            flip.0 at.0 stack.0.0.0 stack.0.0.1 score.3 score.4 score.5 turn.0.0.0.0 at.1 flip.3 turn.0.0.0.1
            turn.0.0.1.0 score.6 score.7 score.8 stack.0.1.0 turn.0.0.1.1 stack.0.1.1 vals.0 pv.0 flip.6
            turn.0.1.0.0 turn.0.1.0.1 score.9 pv.1 turn.0.1.1.0 turn.0.1.1.1 flip.9 pv.2 score.10 xt.0
            score.11 score.12 xt.1 flip.12 score.13 score.14 score.15 score.16 pv.3 stack.1.0.0 stack.1.0.1
            flip.15 score.17 score.18 score.19 pv.4 turn.1.0.0.0 flip.18 turn.1.0.0.1 turn.1.0.1.0 stack.1.1.0
            turn.1.0.1.1 stack.1.1.1 score.20 score.21 turn.1.1.0.0 pv.5 vals.1 score.22 turn.1.1.0.1
            turn.1.1.1.0 pv.6 turn.1.1.1.1 flip.21 score.23 next-score.0 next-score.1 pv.7 next-score.2
        """)
        GPSIMD_STEPS = steps("""
            rope.0.1 stats rope.1.0 rope.1.1 next-rope.0.0
        """)

        def ahead(step):
            return step[0] in ("stats", "norm", "xt", "early") or \
                step[0] in ("proj", "rope", "stack", "turn", "vals") and step[1] == 1

        USES = {("proj", 0, 0): -1}
        for step in TENSOR_STEPS:
            if step[0] == "proj" and step[3] == 0:
                USES[step[:3]] = len(USES) - 1
            elif step[0] in ("turn", "xt"):
                USES[step] = len(USES) - 1
        NU = len(USES)
        assert NU == 24

        def fr(use):
            return (14 + USES[use]) % 2

        def fr_wait_full(eng, b, use):
            eng.wait_ge(fr_full[fr(use)], b * 12 + ((14 + USES[use]) // 2 + 1))

        def fr_wait_turn(eng, b, use):
            eng.wait_ge(fr_free[fr(use)], b * 12 + ((14 + USES[use]) // 2 + 1))

        def fr_wait_read(eng, b, use):
            eng.wait_ge(fr_free[fr(use)], b * 12 + ((14 + USES[use]) // 2 + 2))

        def follow(do, b, order):
            for step in order:
                if step[0] == "early":
                    do(b + 1, *step[1:])
                else:
                    do(b, *step)

        def run(eng, order, do):
            follow(do, -1, [s for s in order if ahead(s)])
            follow(do, 0, [s for s in order if s[0] not in ("at", "o")])
            with eng.Fori(1, B - 1) as i:
                follow(do, i, order)
            follow(do, B - 1, [s for s in order if not ahead(s)])
            follow(do, B, [s for s in order if s[0] in ("at", "o")])

        block = ctx.enter_context(nc.Block())

        @block.sync
        def _(sp):
            sp.dma_start(X[:, 0:TPB, :], x_in[0]).then_inc(s_x, 16)
            sp.dma_start(WRAW[0], wqkvo[0]).then_inc(s_w[0], 16)
            sp.dma_start(ident[:, :], ident_in).then_inc(s_cst, 16)
            sp.dma_start(maskf[:, :], mask_in).then_inc(s_cst, 16)
            sp.dma_start(rope[:, :, :, :], rope_in).then_inc(s_cst, 16)
            for w in range(1, 4):
                sp.dma_start(WRAW[w], wqkvo[w]).then_inc(s_w[w], 16)
            sp.wait_ge(s_x, 16)
            sp.wait_ge(s_wlo, 4)
            with sp.Fori(1, B) as i:
                sp.dma_start(X[:, bass.ds(i * TPB, TPB), :],
                             x_in[bass.ds(i, 1)].rearrange("a p t n -> p (a t) n")).then_inc(s_x, 16)
                wait_alone(sp, s_x, i * 16 + 16, s_sptick)

        @block.gpsimd
        def _(pool):
            nc.gpsimd.memset(half[:, :], -0.5).then_inc(s_half, 1)
            pool.wait_ge(s_half, 1)

            def do(b, kind, *a):
                if kind == "stats":
                    pool.wait_ge(s_ve, b + 2)
                    nc.gpsimd.tensor_tensor(rstd[:, :], ve[:, :], half[:, :], ALU.pow).then_inc(s_pow, 1)
                    if isinstance(b, int) and b == -1:
                        nc.gpsimd.memset(KTT[:, :, :, :, :].bitcast(U32), 0).then_inc(s_zero, 1)
                elif kind == "rope":
                    fr_wait_read(pool, b, ("proj", *a))
                    nc.gpsimd.tensor_tensor(RA[:, :, :, :], RA[:, :, :, :], RB[:, :, :, :], ALU.add).then_inc(s_rr, 1)
                    if isinstance(b, int) and b == -1 and a == (1, 1):
                        pool.wait_ge(s_wlo, 4)
                        nc.gpsimd.memset(V[:, :, :, :, HD:32], 1.0).then_inc(s_zero, 1)

            run(pool, GPSIMD_STEPS, do)

        @block.scalar
        def _(act):
            act.wait_ge(s_cst, 48)
            nc.scalar.copy(ident_r[:, :], ident[:, :]).then_inc(s_cd, 1)
            nc.scalar.copy(identb[:, :], ident[:, :]).then_inc(s_cd, 1)
            nc.scalar.copy(maskb[:, :], maskf[:, :]).then_inc(s_cd, 1)

            def weight(w):
                act.wait_ge(s_w[w], 16)
                nc.scalar.copy(WH[:, w, :, :], WRAW[w]).then_inc(s_whi, 1)

            weight(0)

            def do(b, kind, *a):
                if kind == "xt":
                    t, = a
                    fr_wait_full(act, b, ("xt", t))
                    nc.scalar.copy(XTH[:, :, t * P:(t + 1) * P],
                                   FR[fr(("xt", t))][:, :].rearrange("p (k n) -> p k n", k=KT)).then_inc(s_xth, 1)
                    if isinstance(b, int) and b == -1 and t == 1:
                        for w in range(1, 4):
                            weight(w)
                elif kind == "stack":
                    f, w, t = a
                    act.wait_ge(s_rr, b * 4 + (2 * f + w + 3))
                    dst = STK[:, t, :, 0:2, :] if w == 0 else STK[:, t, :, 0:4:2, :]
                    nc.scalar.copy(dst, RA[:, t, :, :].unsqueeze(2).to_broadcast([P, HH, 2, HD])).then_inc(s_hi, 1)
                elif kind == "turn":
                    f, w, t, g = a
                    use = ("turn", *a)
                    fr_wait_full(act, b, use)
                    bank = FR[fr(use)]
                    cols = slice(t * P, (t + 1) * P)
                    if w == 0:
                        nc.scalar.copy(QT[:, 1 - f, 4 * g:4 * g + 4, cols],
                                       bank[:, :].rearrange("p (a n) -> p a n", a=4)).then_inc(fr_free[fr(use)], 1)
                    else:
                        nc.scalar.copy(KTT[0:64, 1 - f, 4 * g:4 * g + 4, 0, cols],
                                       bank[0:64, :].rearrange("p (a n) -> p a n", a=4)).then_inc(s_ka, 1)
                elif kind == "vals":
                    use = ("proj", a[0], 2)
                    fr_wait_full(act, b, use)
                    if isinstance(b, int) and b == -1:
                        act.wait_ge(s_zero, 2)
                    nc.scalar.copy(V[:, 1 - a[0], :, :, 0:HD],
                                   FR[fr(use)][:, :].rearrange("p (t h d) -> p t h d", t=TPB, h=HH)
                                   ).then_inc(fr_free[fr(use)], 1)
                elif kind == "score":
                    n, = a
                    u, j = n // 3, n % 3
                    act.wait_ge(s_mx, b * NJ + (n + 1))
                    heads = 4 if j == 0 else 2
                    w = D // heads
                    for h in range(heads):
                        ins = nc.scalar.activation(PR[:, j, h * w:(h + 1) * w], SC[j][:, h * w:(h + 1) * w],
                                                   ACT.Exp, bias=nmx[:, j, h:h + 1])
                    ins.then_inc(sc_free[j], 1)
                elif kind == "flip" and a[0] % 3 == 0:
                    n, = a
                    act.wait_ge(tp_full[n % 2], b * 12 + (n // 2 + 1))
                    nc.scalar.copy(PT[:, n // 3 % 2, :, 0:P],
                                   TP[n % 2][:, :].rearrange("p (h n) -> p h n", h=4)).then_inc(tp_free[n % 2], 1)
                elif kind == "pv":
                    u, = a
                    act.wait_ge(ou_full, b * 16 + (2 * u + 1))
                    nc.scalar.copy(OT[:, u % 2, :], OU[:, 0:S]).then_inc(ou_free, 1)
                elif kind == "at":
                    t, = a
                    act.wait_ge(tl_full, b * 4 + (2 * t - 3))
                    nc.scalar.copy(ATH[:, :, :], OU[:, :].rearrange("p (k n) -> p k n", k=KT)).then_inc(s_ath, 1)

            run(act, SCALAR_STEPS, do)

        @block.vector
        def _(dve):
            def do(b, kind, *a):
                xs = [X[:, 2 * b + 2 + t, :] if isinstance(b, int) else
                      X[:, bass.ds(b * TPB + (TPB + t), 1), :].rearrange("p a n -> p (a n)") for t in range(TPB)
                      ] if kind in ("stats", "norm") else None
                if kind == "stats":
                    dve.wait_ge(s_x, b * 16 + 32)
                    for t in range(TPB):
                        ins = nc.vector.bn_stats(st[:, t, :], xs[t])
                    norm_link(b, ins, 0)
                    for t in range(TPB):
                        ins = nc.vector.bn_aggr(mv[:, t, :], st[:, t, :])
                    norm_link(b, ins, 1)
                    nc.vector.tensor_scalar(ve[:, :], mv[:, :, 1], EPS, None, ALU.add).then_inc(s_ve, 1)
                elif kind == "norm":
                    dve.wait_ge(s_pow, b + 2)
                    for t in range(TPB):
                        nc.vector.tensor_scalar(XN[:, t, :], xs[t], mv[:, t, 0:1], rstd[:, t:t + 1],
                                                ALU.subtract, ALU.mult).then_inc(s_xn, 1)
                    if isinstance(b, int) and b == -1:
                        split_weight(0)
                elif kind == "xt":
                    t, = a
                    use = ("xt", t)
                    dve.wait_ge(s_xth, b * 2 + (t + 3))
                    nc.vector.tensor_tensor(XTL[:, :, t * P:(t + 1) * P],
                                            FR[fr(use)][:, :].rearrange("p (k n) -> p k n", k=KT),
                                            XTH[:, :, t * P:(t + 1) * P].bitcast(F32),
                                            ALU.subtract).then_inc(fr_free[fr(use)], 1)
                    if isinstance(b, int) and b == -1 and t == 1:
                        split_weight(1)
                elif kind == "rope":
                    f, w = a
                    use = ("proj", f, w)
                    fr_wait_full(dve, b, use)
                    bank = FR[fr(use)]
                    cos = rope[:, 2 * w, :, :].unsqueeze(2).to_broadcast([P, TPB, HH, HD])
                    sin = rope[:, 2 * w + 1, :, :].rearrange("p t (k e) -> p t k e", e=2)
                    q4 = bank[:, :].rearrange("p (t h k e) -> p t h k e", t=TPB, h=HH, e=2)
                    b4 = RB[:, :, :, :].rearrange("p t h (k e) -> p t h k e", e=2)
                    if not (isinstance(b, int) and b == -1 and w == 0):
                        dve.wait_ge(s_lo, b * 8 + (4 * f + 2 * w + 4))
                    nc.vector.tensor_tensor(RA[:, :, :, :], bank[:, :].rearrange("p (t h d) -> p t h d", t=TPB, h=HH),
                                            cos, ALU.mult)
                    for e in range(2):
                        ins = nc.vector.tensor_tensor(b4[:, :, :, :, e], q4[:, :, :, :, 1 - e],
                                                      sin[:, :, :, e].unsqueeze(2).to_broadcast([P, TPB, HH, HD // 2]),
                                                      ALU.mult)
                    ins.then_inc(fr_free[fr(use)], 1)
                    if isinstance(b, int) and b == -1:
                        split_weight(2 + w)
                elif kind == "stack":
                    f, w, t = a
                    dve.wait_ge(s_hi, b * 8 + (4 * f + 2 * w + t + 5))
                    dst = STK[:, t, :, 2:4, :] if w == 0 else STK[:, t, :, 1:4:2, :]
                    nc.vector.tensor_tensor(dst, RA[:, t, :, :].unsqueeze(2).to_broadcast([P, HH, 2, HD]),
                                            STK[:, t, :, 0:1, :].bitcast(F32).to_broadcast([P, HH, 2, HD]),
                                            ALU.subtract).then_inc(s_lo, 1)
                elif kind == "turn" and a[1] == 1:
                    f, w, t, g = a
                    use = ("turn", *a)
                    dve.wait_ge(s_ka, b * 8 + (4 * f + 2 * t + g + 5))
                    nc.vector.tensor_copy(KTT[64:P, 1 - f, 4 * g:4 * g + 4, 1, t * P:(t + 1) * P],
                                          FR[fr(use)][64:P, :].rearrange("p (a n) -> p a n", a=4)
                                          ).then_inc(fr_free[fr(use)], 1)
                elif kind == "score":
                    n, = a
                    u, j = n // 3, n % 3
                    heads = 4 if j == 0 else 2
                    dve.wait_ge(sc_full[j], b * 8 + (u + 1))
                    nc.vector.tensor_reduce(nmx[:, j, 0:heads], SC[j][:, :].rearrange("p (h n) -> p h n", h=heads),
                                            axis=AXX, op=ALU.max, negate=True).then_inc(s_mx, 1)
                elif kind == "flip" and a[0] % 3:
                    n, = a
                    u, j = n // 3, n % 3
                    dve.wait_ge(tp_full[n % 2], b * 12 + (n // 2 + 1))
                    nc.vector.tensor_copy(PT[:, u % 2, 2 * j - 2:2 * j, P:384],
                                          TP[n % 2][:, :].rearrange("p (h n) -> p h n", h=2)
                                          ).then_inc(tp_free[n % 2], 1)
                elif kind == "out":
                    u, = a
                    dve.wait_ge(ou_full, b * 16 + (2 * u + 2))
                    v = OU[:, 0:S].rearrange("p (t h d) -> p t h d", t=TPB, h=4)
                    nc.vector.reciprocal(rden[:, u % 2, :, :], v[:, :, :, HD]).then_inc(s_rden, 1)
                    dve.wait_ge(s_rden, b * 8 + (u + 1))
                    nc.vector.tensor_tensor(
                        AO[:, :, u * 64:(u + 1) * 64].rearrange("p t (h d) -> p t h d", h=4), v[:, :, :, 0:HD],
                        rden[:, u % 2, :, :].unsqueeze(3).to_broadcast([P, TPB, 4, HD]), ALU.mult).then_inc(ou_free, 1)
                elif kind == "at":
                    t, = a
                    dve.wait_ge(s_ath, b * 2 + (t - 1))
                    nc.vector.tensor_tensor(ATL[:, :, :], OU[:, :].rearrange("p (k n) -> p k n", k=KT),
                                            ATH[:, :, :].bitcast(F32), ALU.subtract).then_inc(tl_free, 1)
                elif kind == "o" and a[1] == 1:
                    t = a[0]
                    dve.wait_ge(tl_full, b * 4 + (2 * t - 2))
                    x = X[:, 2 * b - 2 + t, :] if isinstance(b, int) else \
                        X[:, bass.ds(b * TPB + (t - TPB), 1), :].rearrange("p a n -> p (a n)")
                    nc.vector.tensor_tensor(x, x, OU[:, :], ALU.add).then_inc(tl_free, 1)

            def norm_link(b, ins, n):
                ins.then_inc(s_chain, 1)
                dve.wait_ge(s_chain, b * 2 + (n + 3))
                dve.sem_inc(s_tick, 1)

            def split_weight(w):
                dve.wait_ge(s_whi, w + 1)
                nc.vector.tensor_tensor(WL[:, w, :, :], WRAW[w], WH[:, w, :, :].bitcast(F32),
                                        ALU.subtract).then_inc(s_wlo, 1)

            run(dve, VECTOR_STEPS, do)

        @block.tensor
        def _(pe):
            for s in fr_free + sc_free + tp_free + [ou_free]:
                pe.sem_inc(s, 1)
            pe.wait_ge(s_cst, 48)
            pe.wait_ge(s_cd, 3)

            def do(b, kind, *a):
                first = isinstance(b, int) and b == -1
                if kind == "xt":
                    t, = a
                    use = ("xt", t)
                    pe.wait_ge(s_xn, b * 2 + (t + 3))
                    fr_wait_turn(pe, b, use)
                    for k in range(KT):
                        ins = nc.tensor.transpose(FR[fr(use)][:, k * P:(k + 1) * P],
                                                  XN[:, t, k * P:(k + 1) * P], ident[:, :])
                    ins.then_inc(fr_full[fr(use)], 1)
                elif kind == "proj":
                    f, w, t = a
                    use = ("proj", f, w)
                    if f == 1 and w == 0:
                        fr_wait_read(pe, b, ("xt", t))
                    if t == 0:
                        if first:
                            pe.wait_ge(s_wlo, w + 1)
                        fr_wait_turn(pe, b, use)
                    cols = slice((1 - f) * 256, (2 - f) * 256)
                    for k in range(KT):
                        ins = three_pass(nc, FR[fr(use)][:, t * 256:(t + 1) * 256],
                                         (XTH[:, k, t * P:(t + 1) * P], XTL[:, k, t * P:(t + 1) * P]),
                                         (WH[:, w, k, cols], WL[:, w, k, cols]), k == 0, k == KT - 1)
                    if t == 1:
                        ins.then_inc(fr_full[fr(use)], 1)
                elif kind == "turn":
                    f, w, t, g = a
                    use = ("turn", *a)
                    pe.wait_ge(s_lo, b * 8 + (4 * f + 2 * w + t + 5))
                    fr_wait_turn(pe, b, use)
                    for p in range(4):
                        c = g * 8 + 2 * p
                        ins = nc.tensor.transpose(
                            FR[fr(use)][:, p * P:(p + 1) * P].bitcast(F32R),
                            STK[:, t, c:c + 2, :, :].rearrange("p h a d -> p (h a d)"), ident_r[:, :])
                    ins.then_inc(fr_full[fr(use)], 1)
                elif kind == "score":
                    n, = a
                    u, j = n // 3, n % 3
                    hf = u // 4
                    bank = SC[j]
                    if n % 12 == 0:
                        for g in range(2):
                            fr_wait_read(pe, b if hf else b - 1, ("turn", 1 - hf, 1, 1, g))
                        if isinstance(b, int) and b == 0 and n == 0:
                            pe.wait_ge(s_zero, 2)
                    pe.wait_ge(sc_free[j], b * 8 + (u + 1))
                    if j == 0:
                        nc.tensor.matmul(bank[:, :].rearrange("p (h n) -> p h n", h=4), identb[:, :],
                                         maskb[:, :].unsqueeze(1).to_broadcast([P, 4, P]), start=True, stop=False)
                        for c in range(2):
                            pr = 2 * (u % 4) + c
                            ins = nc.tensor.matmul(
                                bank[:, c * 256:(c + 1) * 256].rearrange("p (h n) -> p h n", h=2),
                                QT[:, hf, pr, 0:P], KTT[:, hf, pr, :, 0:P], start=False, stop=c == 1)
                    else:
                        pr = 2 * (u % 4) + j - 1
                        nc.tensor.matmul(bank[:, :].rearrange("p (h n) -> p h n", h=2),
                                         QT[:, hf, pr, P:S], KTT[:, hf, pr, :, :], start=True, stop=False)
                        ins = nc.tensor.matmul(
                            bank[:, :].rearrange("p (h n) -> p h n", h=2)[:, :, P:S], identb[:, :],
                            maskb[:, :].unsqueeze(1).to_broadcast([P, 2, P]), start=False, stop=True)
                    ins.then_inc(sc_full[j], 1)
                elif kind == "flip":
                    n, = a
                    u, j = n // 3, n % 3
                    pe.wait_ge(sc_free[j], b * 8 + (u + 2))
                    pe.wait_ge(tp_free[n % 2], b * 12 + (n // 2 + 1))
                    for c in range(4):
                        ins = nc.tensor.transpose(TP[n % 2][:, c * P:(c + 1) * P], PR[:, j, c * P:(c + 1) * P],
                                                  ident[:, :])
                    ins.then_inc(tp_full[n % 2], 1)
                elif kind == "pv":
                    u, = a
                    hf = u // 4
                    if u % 4 == 0:
                        v = (b if hf else b - 1, ("proj", 1 - hf, 2))
                        fr_wait_read(pe, *v)
                    if u == 0 and not (isinstance(b, int) and b == 0):
                        pe.wait_ge(tl_free, b * 4)
                    for n in (3 * u + 1, 3 * u + 2):
                        pe.wait_ge(tp_free[n % 2], b * 12 + (n // 2 + 2))
                    pe.wait_ge(ou_free, b * 16 + (2 * u + 1))
                    for h in range(4):
                        nc.tensor.matmul(OU[32 * h:32 * h + 32, 0:S], V[:, hf, 0, 4 * (u % 4) + h, :],
                                         PT[:, u % 2, h, 0:S], start=True, stop=False, tile_position=(0, 32 * h))
                    for h in range(4):
                        ins = nc.tensor.matmul(OU[32 * h:32 * h + 32, P:S], V[:, hf, 1, 4 * (u % 4) + h, :],
                                               PT[:, u % 2, h, S:384], start=False, stop=True,
                                               tile_position=(0, 32 * h))
                    ins.then_inc(ou_full, 1)
                elif kind == "out":
                    u, = a
                    pe.wait_ge(ou_free, b * 16 + (2 * u + 2))
                    for t in range(TPB):
                        ins = nc.tensor.transpose(OU[:, t * P:(t + 1) * P], OT[:, u % 2, t * P:(t + 1) * P],
                                                  ident[:, :])
                    ins.then_inc(ou_full, 1)
                elif kind == "at":
                    t, = a
                    if t == 0:
                        pe.wait_ge(ou_free, b * 16 + 1)
                    else:
                        pe.wait_ge(tl_free, b * 4 - 2)
                    for k in range(KT):
                        ins = nc.tensor.transpose(OU[:, k * P:(k + 1) * P], AO[:, t, k * P:(k + 1) * P], ident[:, :])
                    ins.then_inc(tl_full, 1)
                elif kind == "o":
                    t, part = a
                    if part == 0:
                        pe.wait_ge(tl_free, b * 4 + (2 * t - 3))
                    for k in (2 * part, 2 * part + 1):
                        ins = three_pass(nc, OU[:, :], (ATH[:, k, :], ATL[:, k, :]),
                                         (WH[:, 3, k, :], WL[:, 3, k, :]), k == 0, k == KT - 1)
                    if part == 1:
                        ins.then_inc(tl_full, 1)

            run(pe, TENSOR_STEPS, do)


class BlockNorm:

    def __init__(self, nc, ctx, X, ident, XTH, XTL, banks, tag):
        sb, sem = alloc(nc, ctx)
        self.nc, self.X, self.ident, self.XTH, self.XTL, self.banks = nc, X, ident, XTH, XTL, banks
        self.XN = sb(f"nXN{tag}", [P, 4, D])
        self.st = sb(f"nst{tag}", [P, 4, 6])
        self.mv = sb(f"nmv{tag}", [P, 4, 2])
        self.ve = sb(f"nve{tag}", [P, 4])
        self.half = sb(f"nhalf{tag}", [P, 4])
        self.rstd = sb(f"nrstd{tag}", [P, 4])
        self.negm = sb(f"nnegm{tag}", [P, 4])
        self.shift = sb(f"nshift{tag}", [P, 4])
        self.s_half, self.s_chain, self.s_tick, self.s_ve, self.s_pow, self.s_shift = (
            sem(f"n{x}{tag}") for x in ("half", "chain", "tick", "ve", "pow", "shift"))
        self.s_xn = sem(f"nxn{tag}")
        self.s_xp = sem(f"nxp{tag}")
        self.s_hi = sem(f"nhi{tag}")
        self.s_lo = sem(f"nlo{tag}")

    def cols(self, i, t):
        return bass.ds(i * 512 + t * P, P)

    def pool_start(self, pool):
        self.nc.gpsimd.memset(self.half[:, :], -0.5).then_inc(self.s_half, 1)
        pool.wait_ge(self.s_half, 1)

    def pool_power(self, pool, i):
        pool.wait_ge(self.s_ve, i + 1)
        self.nc.gpsimd.tensor_tensor(self.rstd[:, :], self.ve[:, :], self.half[:, :], ALU.pow).then_inc(self.s_pow, 1)
        pool.wait_ge(self.s_pow, i + 1)
        self.nc.gpsimd.tensor_tensor(self.shift[:, :], self.negm[:, :], self.rstd[:, :], ALU.mult
                                     ).then_inc(self.s_shift, 1)

    def vector_stats(self, dve, i):
        nc, x = self.nc, self.X[:, bass.ds(i * 4, 4), :]
        link = Chain(dve, self.s_chain, i * 2, self.s_tick)
        for t in range(4):
            ins = nc.vector.bn_stats(self.st[:, t, :], x[:, t, :])
        link(ins, alone=True)
        for t in range(4):
            ins = nc.vector.bn_aggr(self.mv[:, t, :], self.st[:, t, :])
        link(ins)
        dve.wait_ge(self.s_xn, i * 4 + 4)
        nc.vector.tensor_scalar(self.negm[:, :], self.mv[:, :, 0], -1.0, None, ALU.mult)
        nc.vector.tensor_scalar(self.ve[:, :], self.mv[:, :, 1], EPS, None, ALU.add).then_inc(self.s_ve, 1)

    def scalar_norm(self, act, i):
        act.wait_ge(self.s_shift, i + 1)
        act.wait_ge(self.s_xp, i * 4 + 4)
        x = self.X[:, bass.ds(i * 4, 4), :]
        for t in range(4):
            self.nc.scalar.activation(self.XN[:, t, :], x[:, t, :], ACT.Identity, bias=self.shift[:, t:t + 1],
                                      scale=self.rstd[:, t:t + 1]).then_inc(self.s_xn, 1)

    def tensor_start(self, pe):
        pe.sem_inc(self.s_xn, 4)
        pe.sem_inc(self.s_xp, 4)
        pe.sem_inc(self.s_lo, len(self.banks))

    def tensor_turn(self, pe, i, tiles=range(4)):
        for t in tiles:
            bank = self.banks[t % len(self.banks)]
            pe.wait_ge(self.s_xn, i * 4 + t + 5)
            pe.wait_ge(self.s_lo, i * 4 + t + 1)
            for k in range(KT):
                ins = self.nc.tensor.transpose(bank[:, k * P:(k + 1) * P], self.XN[:, t, k * P:(k + 1) * P],
                                               self.ident[:, :])
            ins.then_inc(self.s_xp, 1)

    def scalar_hi(self, act, i, tiles=range(4)):
        for t in tiles:
            act.wait_ge(self.s_xp, i * 4 + t + 5)
            self.nc.scalar.copy(self.XTH[:, :, self.cols(i, t)],
                                self.banks[t % len(self.banks)][:, :].rearrange("p (k n) -> p k n", k=KT)
                                ).then_inc(self.s_hi, 1)

    def vector_lo(self, dve, i, tiles=range(4)):
        for t in tiles:
            dve.wait_ge(self.s_hi, i * 4 + t + 1)
            self.nc.vector.tensor_tensor(self.XTL[:, :, self.cols(i, t)],
                                         self.banks[t % len(self.banks)][:, :].rearrange("p (k n) -> p k n", k=KT),
                                         self.XTH[:, :, self.cols(i, t)].bitcast(F32),
                                         ALU.subtract).then_inc(self.s_lo, 1)

    def tensor_wait(self, pe, i):
        pe.wait_ge(self.s_lo, i * 4 + 4 + len(self.banks))


def coded_swiglu_phase(nc, X, PB, ident, XTH, XTL, gu_in, d_in, gu_scale, d_scale):
    C = F0 // 256
    with ExitStack() as ctx:
        sb, sem = alloc(nc, ctx)
        Q = sb("Q", [P, 2, 2, KT, P], F32R)
        DH = sb("cDH", [P, 2, D], F32R)
        DL = sb("cDL", [P, 2, D], F32R)
        raw = sb("craw", [P, 3, 1024], I32)
        w32 = sb("cw32", [P, 1024])
        scl = sb("cscl", [P, 1024])
        sgu = sb("csgu", [P, C * 16])
        HH = sb("cHH", [P, 6, D], F32R)
        HL = sb("cHL", [P, 6, D], F32R)
        T = sb("cT", [P, 2, 2, D])
        U = sb("cU", [P, 2, 2, D])
        W = sb("cW", [P, 2, D])
        SG = sb("cSG", [P, 2, D])
        HF = sb("cHF", [P, 2, D])
        turn_act = sb("cturn_act", [P, 16])
        turn_dve = sb("cturn_dve", [P, 16])
        s_act, s_dve = sem("cact"), sem("cdve")
        s_raw, s_sgu = [sem(f"craw{n}") for n in range(3)], sem("csgu")
        s_code, s_cvt, s_mul, s_whi, s_w = (sem(f"c{x}") for x in ("code", "cvt", "mul", "whi", "w"))
        s_pk = [sem(f"cpk{k}") for k in range(KT)]
        s_t = sem("ct")
        s_u = sem("cu")
        s_sum = sem("csum")
        s_silu, s_h, s_hhi, s_hlo = (sem(f"c{x}") for x in ("silu", "h", "hhi", "hlo"))
        s_dn, s_xadd, s_sptick = sem("cdn"), sem("cxadd"), sem("csptick")
        norm = BlockNorm(nc, ctx, X, ident, XTH, XTL, PB[4:8], "c")
        block = ctx.enter_context(nc.Block())
        ORDER = [("gu", 0, 0), ("gu", 0, 1), ("gu", 0, 2), ("gu", 0, 3), ("gu", 1, 0), ("gu", 1, 1), ("gu", 1, 2),
                 ("dn", 0), ("gu", 1, 3), ("dn", 1), ("finish",), ("dn", 2), ("dn", 3)]

        def looped(eng, body):
            body(0, True, True)
            with eng.Fori(1, C - 1) as i:
                body(i, True)
            body(C - 1, False)

        def scale(own, s, g, k):
            c = s // 4 * 8 + g * 4 + k
            return own[:, c:c + 1]

        @block.sync
        def _(sp):
            def fetch(c, slot):
                one = bass.ds(c, 1)
                src = gu_in[one, slot] if slot < 2 else d_in[one]
                sp.dma_start(raw[:, slot, :], src.rearrange("a p n -> (a p) n")).then_inc(s_raw[slot], 16)
                if slot == 2:
                    sp.dma_start(scl[:, :], d_scale[one].to_broadcast([P, 1024])).then_inc(s_raw[slot], 16)

            fetch(0, 0)
            sp.dma_start(sgu[:, :], gu_scale).then_inc(s_sgu, 16)
            fetch(0, 1)
            fetch(0, 2)
            with sp.Fori(0, C - 1) as i:
                wait_alone(sp, s_code, i * 2 + 1, s_sptick)
                fetch(i + 1, 0)
                wait_alone(sp, s_code, i * 2 + 2, s_sptick)
                fetch(i + 1, 1)
                wait_alone(sp, s_mul, i + 1, s_sptick)
                fetch(i + 1, 2)

        @block.gpsimd
        def _(pool):
            norm.pool_start(pool)

            def body(i, more, lead=False):
                if lead:
                    for b in range(3):
                        norm.pool_power(pool, b)
                for s in range(8):
                    for g in range(2):
                        pool.wait_ge(s_u, i * 32 + (4 * s + 2 * g + 4))
                        nc.gpsimd.tensor_tensor(U[:, s % 2, g, :], U[:, s % 2, g, :], W[:, g, :],
                                                ALU.add).then_inc(s_sum, 1)
                    if lead and s == 0:
                        norm.pool_power(pool, 3)
                    if s == 1:
                        pool.wait_ge(s_cvt, i + 1)
                        nc.gpsimd.tensor_tensor(w32[:, :], w32[:, :], scl[:, :], ALU.mult).then_inc(s_mul, 1)
                    if s == 3:
                        pool.wait_ge(s_whi, i + 1)
                        nc.gpsimd.tensor_tensor(DL[:, :, :].rearrange("p k n -> p (k n)"), w32[:, :],
                                                DH[:, :, :].rearrange("p k n -> p (k n)").bitcast(F32),
                                                ALU.subtract).then_inc(s_w, 1)
            looped(pool, body)

        @block.scalar
        def _(act):
            def take_codes(c, slot):
                act.wait_ge(s_raw[slot], c * 16 + 16)
                nc.scalar.copy(Q[:, slot].rearrange("p a k n -> p (a k n)"), raw[:, slot, :]).then_inc(s_code, 1)

            norm.scalar_norm(act, 0)
            take_codes(0, 0)
            norm.scalar_hi(act, 0)
            norm.scalar_norm(act, 1)
            act.wait_ge(s_sgu, 16)

            def leave(i, s, g):
                for k in range(2):
                    act.wait_ge(s_pk[k], i * 16 + (2 * s + g + 1))
                    nc.scalar.activation(T[:, g, k, :], PB[k][:, :], ACT.Identity,
                                         scale=scale(turn_act, s, g, k)).then_inc(s_t, 1)

            def silu(i, s):
                act.wait_ge(s_sum, i * 16 + (2 * s + 3))
                nc.scalar.activation(SG[:, s % 2, :], U[:, s % 2, 0, :], ACT.Silu).then_inc(s_silu, 1)

            def split(i, s):
                slot, t = s // 4, s % 4
                act.wait_ge(s_h, i * 8 + (s + 1))
                act.wait_ge(s_dn, i * 16 + 4 * t + (4 if slot == 0 else 12))
                nc.scalar.copy(HH[:, t if slot == 0 else 4 + t % 2, :], HF[:, s % 2, :]).then_inc(s_hhi, 1)

            def body(i, more, lead=False):
                act.wait_ge(s_t, i * 32 + 2)
                nc.scalar.copy(turn_act[:, :], sgu[:, bass.ds(i * 16, 16)]).then_inc(s_act, 1)
                act.wait_ge(s_act, i + 1)
                for s in range(8):
                    leave(i, s, 0)
                    if lead and s < 3:
                        norm.scalar_hi(act, s + 1)
                    if lead and s < 2:
                        norm.scalar_norm(act, s + 2)
                    if s > 0:
                        silu(i, s - 1)
                    leave(i, s, 1)
                    if s > 0:
                        split(i, s - 1)
                    if s == 0:
                        take_codes(i, 1)
                    if s == 1:
                        act.wait_ge(s_raw[2], i * 32 + 32)
                        if lead:
                            nc.scalar.copy(w32[:, :], raw[:, 2, :]).then_inc(s_cvt, 1)
                        else:
                            act.wait_ge(s_w, i)
                            nc.scalar.copy(w32[:, :], raw[:, 2, :]).then_inc(s_cvt, 1)
                    if s == 3:
                        act.wait_ge(s_mul, i + 1)
                        act.wait_ge(s_dn, i * 16 + 16)
                        nc.scalar.copy(DH[:, :, :].rearrange("p k n -> p (k n)"), w32[:, :]).then_inc(s_whi, 1)
                    if s == 5 and more:
                        take_codes(i + 1, 0)
                silu(i, 7)
                split(i, 7)
            looped(act, body)

        @block.vector
        def _(dve):
            norm.vector_stats(dve, 0)
            norm.vector_stats(dve, 1)
            norm.vector_lo(dve, 0)
            norm.vector_stats(dve, 2)
            dve.wait_ge(s_sgu, 16)

            def leave(i, s, g):
                for k, dst in ((2, U[:, s % 2, g, :]), (3, W[:, g, :])):
                    dve.wait_ge(s_sum, i * 16 + (2 * s + g + 1))
                    dve.wait_ge(s_t, i * 32 + (4 * s + 2 * g + k + 1))
                    dve.wait_ge(s_pk[k], i * 16 + (2 * s + g + 1))
                    nc.vector.scalar_tensor_tensor(dst, PB[k][:, :], scale(turn_dve, s, g, k), T[:, g, k - 2, :],
                                                   ALU.mult, ALU.add).then_inc(s_u, 1)

            def times_up(i, s):
                dve.wait_ge(s_silu, i * 8 + (s + 1))
                dve.wait_ge(s_sum, i * 16 + (2 * s + 4))
                nc.vector.tensor_tensor(HF[:, s % 2, :], U[:, s % 2, 1, :], SG[:, s % 2, :],
                                        ALU.mult).then_inc(s_h, 1)

            def split(i, s):
                h = s if s < 4 else 4 + s % 2
                dve.wait_ge(s_hhi, i * 8 + (s + 1))
                nc.vector.tensor_tensor(HL[:, h, :], HF[:, s % 2, :], HH[:, h, :].bitcast(F32),
                                        ALU.subtract).then_inc(s_hlo, 1)

            def body(i, more, lead=False):
                dve.wait_ge(s_u, i * 32 + 2)
                nc.vector.tensor_copy(turn_dve[:, :], sgu[:, bass.ds(i * 16, 16)]).then_inc(s_dve, 1)
                dve.wait_ge(s_dve, i + 1)
                for step in ORDER:
                    if step[0] == "gu":
                        s = 4 * step[1] + step[2]
                        leave(i, s, 0)
                        if lead and s < 3:
                            norm.vector_lo(dve, s + 1)
                        if s > 0:
                            times_up(i, s - 1)
                        leave(i, s, 1)
                        if lead and s == 0:
                            norm.vector_stats(dve, 3)
                        if s > 0:
                            split(i, s - 1)
                    elif step[0] == "finish":
                        times_up(i, 7)
                        split(i, 7)
                    else:
                        t = step[1]
                        for j in range(4):
                            dve.wait_ge(s_dn, i * 16 + t * 4 + j + 17)
                            x = X[:, 4 * t + j, :]
                            nc.vector.tensor_tensor(x, x, PB[4 + j][:, :], ALU.add).then_inc(s_xadd, 1)
            looped(dve, body)

        @block.tensor
        def _(pe):
            norm.tensor_start(pe)
            for s, n in ((s_t, 2), (s_u, 2), (s_sum, 2), (s_dn, 16), (s_xadd, 4)):
                pe.sem_inc(s, n)
            norm.tensor_turn(pe, 0)

            def body(i, more, lead=False):
                for step in ORDER:
                    if step[0] == "gu":
                        slot, t = step[1:]
                        s = 4 * slot + t
                        if lead and s < 4:
                            norm.tensor_wait(pe, s)
                        if t == 0:
                            pe.wait_ge(s_code, i * 2 + (slot + 1))
                        tok = slice(t * 512, (t + 1) * 512)
                        for g in range(2):
                            if lead and g == 1 and s < 3:
                                norm.tensor_turn(pe, s + 1)
                            for k in range(KT):
                                pe.wait_ge(s_t if k < 2 else s_u, i * 32 + (4 * s + 2 * g + k % 2 + 1))
                                nc.tensor.matmul(PB[k][:, :], Q[:, slot, g, k, :], XTH[:, k, tok],
                                                 start=True, stop=False)
                                nc.tensor.matmul(PB[k][:, :], Q[:, slot, g, k, :], XTL[:, k, tok],
                                                 start=False, stop=True).then_inc(s_pk[k], 1)
                    elif step[0] == "dn":
                        t = step[1]
                        if t == 0:
                            pe.wait_ge(s_w, i + 1)
                        pe.wait_ge(s_hlo, i * 8 + 4 + t + 1)
                        for j in range(4):
                            pe.wait_ge(s_xadd, i * 16 + t * 4 + j + 1)
                            for f in range(2):
                                h = t if f == 0 else 4 + t % 2
                                c = slice(j * P, (j + 1) * P)
                                ins = three_pass(nc, PB[4 + j][:, :], (HH[:, h, c], HL[:, h, c]),
                                                 (DH[:, f, :], DL[:, f, :]), f == 0, f == 1)
                            ins.then_inc(s_dn, 1)
            looped(pe, body)


def swiglu_phase(nc, X, PB, XTH, XTL, gu_in, d_in):
    C = F1 // 256
    with ExitStack() as ctx:
        sb, sem = alloc(nc, ctx)
        GUH = sb("GUHb", [P, 2, 2, KT, P], F32R)
        GUL = sb("GULb", [P, 2, 2, KT, P], F32R)
        DH = sb("DHb", [P, 2, D], F32R)
        DL = sb("DLb", [P, 2, D], F32R)
        raw = sb("rawb", [P, 3, 1024])
        HH = sb("HHb", [P, 6, D], F32R)
        HL = sb("HLb", [P, 6, D], F32R)
        SG = sb("SGb", [P, 2, D])
        HF = sb("HFb", [P, 2, D])
        s_raw = [sem(f"raw{n}b") for n in range(3)]
        s_whi, s_w = sem("whib"), sem("wb")
        s_gu, s_silu, s_h, s_hhi, s_hlo = (sem(f"{x}b") for x in ("gu", "silu", "h", "hhi", "hlo"))
        s_dn, s_xadd, s_sptick = sem("dnb"), sem("xaddb"), sem("sptickb")
        block = ctx.enter_context(nc.Block())
        ORDER = [("gu", 0, 0), ("gu", 0, 1), ("gu", 0, 2), ("gu", 0, 3), ("gu", 1, 0), ("gu", 1, 1), ("dn", 0),
                 ("gu", 1, 2), ("dn", 1), ("gu", 1, 3), ("dn", 2), ("dn", 3)]

        def looped(eng, body):
            with eng.Fori(0, C - 1) as i:
                body(i, True)
            body(C - 1, False)

        def fetch(sp, c, slot):
            one = bass.ds(c, 1)
            if slot < 2:
                src = gu_in[one, slot].rearrange("a p n -> (a p) n")
            else:
                src = d_in[one].rearrange("a p n -> (a p) n")
            sp.dma_start(raw[:, slot, :], src).then_inc(s_raw[slot], 16)

        @block.sync
        def _(sp):
            for slot in (0, 1, 2):
                fetch(sp, 0, slot)
            with sp.Fori(0, C - 1) as i:
                for slot in (0, 1, 2):
                    wait_alone(sp, s_w, i * 3 + slot + 1, s_sptick)
                    fetch(sp, i + 1, slot)

        @block.gpsimd
        def _(pool):
            def body(i, more):
                for slot in range(3):
                    hi = GUH[:, slot] if slot < 2 else DH[:, :, :]
                    lo = GUL[:, slot] if slot < 2 else DL[:, :, :]
                    pat = "p a k n -> p (a k n)" if slot < 2 else "p k n -> p (k n)"
                    pool.wait_ge(s_whi, i * 3 + slot + 1)
                    nc.gpsimd.tensor_tensor(lo.rearrange(pat), raw[:, slot, :], hi.rearrange(pat).bitcast(F32),
                                            ALU.subtract).then_inc(s_w, 1)
            looped(pool, body)

        @block.scalar
        def _(act):
            def to_hi(c, slot, first=False):
                hi = GUH[:, slot].rearrange("p a k n -> p (a k n)") if slot < 2 else \
                    DH[:, :, :].rearrange("p k n -> p (k n)")
                if slot == 2 and not first:
                    act.wait_ge(s_dn, c * 16 + 16)
                act.wait_ge(s_raw[slot], (c + 1) * 16)
                nc.scalar.copy(hi, raw[:, slot, :]).then_inc(s_whi, 1)

            for slot in range(3):
                to_hi(0, slot, True)

            def body(i, more):
                for s in range(8):
                    slot, t = s // 4, s % 4
                    act.wait_ge(s_gu, i * 8 + s + 1)
                    nc.scalar.activation(SG[:, s % 2, :], PB[2 * (s % 2)][:, :], ACT.Silu).then_inc(s_silu, 1)
                    h = t if slot == 0 else 4 + t % 2
                    act.wait_ge(s_h, i * 8 + s + 3)
                    act.wait_ge(s_dn, i * 16 + 4 * t + (4 if slot == 0 else 12))
                    nc.scalar.copy(HH[:, h, :], HF[:, s % 2, :]).then_inc(s_hhi, 1)
                    if more and s == 5:
                        to_hi(i + 1, 0)
                if more:
                    for slot in (1, 2):
                        to_hi(i + 1, slot)
            looped(act, body)

        @block.vector
        def _(dve):
            def body(i, more):
                s = 0
                for step in ORDER:
                    if step[0] == "gu":
                        slot, t = step[1:]
                        h = t if slot == 0 else 4 + t % 2
                        dve.wait_ge(s_silu, i * 8 + s + 1)
                        nc.vector.tensor_tensor(HF[:, s % 2, :], PB[2 * (s % 2) + 1][:, :], SG[:, s % 2, :],
                                                ALU.mult).then_inc(s_h, 1)
                        dve.wait_ge(s_hhi, i * 8 + s + 1)
                        nc.vector.tensor_tensor(HL[:, h, :], HF[:, s % 2, :], HH[:, h, :].bitcast(F32),
                                                ALU.subtract).then_inc(s_hlo, 1)
                        s += 1
                    else:
                        t = step[1]
                        for j in range(4):
                            dve.wait_ge(s_dn, i * 16 + t * 4 + j + 17)
                            x = X[:, 4 * t + j, :]
                            nc.vector.tensor_tensor(x, x, PB[4 + j][:, :], ALU.add).then_inc(s_xadd, 1)
            looped(dve, body)

        @block.tensor
        def _(pe):
            pe.sem_inc(s_h, 2)
            pe.sem_inc(s_dn, 16)
            pe.sem_inc(s_xadd, 4)

            def body(i, more):
                s = 0
                for step in ORDER:
                    if step[0] == "gu":
                        slot, t = step[1:]
                        if t == 0:
                            pe.wait_ge(s_w, i * 3 + slot + 1)
                        pe.wait_ge(s_h, i * 8 + s + 1)
                        tok = slice(t * 512, (t + 1) * 512)
                        for a in range(2):
                            for k in range(KT):
                                ins = three_pass(nc, PB[2 * (s % 2) + a][:, :],
                                                 (GUH[:, slot, a, k, :], GUL[:, slot, a, k, :]),
                                                 (XTH[:, k, tok], XTL[:, k, tok]), k == 0, k == KT - 1)
                        ins.then_inc(s_gu, 1)
                        s += 1
                    else:
                        t = step[1]
                        if t == 0:
                            pe.wait_ge(s_w, i * 3 + 3)
                        pe.wait_ge(s_hlo, i * 8 + 4 + t + 1)
                        for j in range(4):
                            pe.wait_ge(s_xadd, i * 16 + t * 4 + j + 1)
                            for f in range(2):
                                h = t if f == 0 else 4 + t % 2
                                c = slice(j * P, (j + 1) * P)
                                ins = three_pass(nc, PB[4 + j][:, :], (HH[:, h, c], HL[:, h, c]),
                                                 (DH[:, f, :], DL[:, f, :]), f == 0, f == 1)
                            ins.then_inc(s_dn, 1)
            looped(pe, body)


def taylor_phase(nc, X, PB, ident, XTH, XTL, ug_in, point_in, fuse_in, disc_in):
    with ExitStack() as ctx:
        sb, sem = alloc(nc, ctx)
        UGH = sb("UGH", [P, 2, KT, P], F32R)
        UGL = sb("UGL", [P, 2, KT, P], F32R)
        FH = sb("FH", [P, G + 1, D], F32R)
        FL = sb("FL", [P, G + 1, D], F32R)
        NRAW = 5
        rawf = sb("rawf", [P, D * NRAW])
        point = sb("point", [P, 1])
        disc = sb("disc", [P, G])
        cdis = sb("cdis", [P, G])
        DEL = sb("DEL", [P, D])
        KEEP = sb("KEEP", [P, D])
        A = sb("A", [P, 4, D])
        AH = sb("AH", [P, G + 1, D], F32R)
        AL = sb("AL", [P, G + 1, D], F32R)
        s_in, s_raw, s_c, s_whi, s_wlo = (sem(f"t{x}") for x in ("in", "raw", "c", "whi", "wlo"))
        s_ug, s_a, s_ahi, s_alo, s_out, s_xadd, s_ch, s_af, s_del = (
            sem(f"t{x}") for x in ("ug", "a", "ahi", "alo", "out", "xadd", "ch", "af", "del"))
        block = ctx.enter_context(nc.Block())
        NW = 2 + G + 1

        norm = BlockNorm(nc, ctx, X, ident, XTH, XTL, PB[2:4], "t")

        HALVES = ((0, 1), (2, 3))

        def a_of(m):
            return A[:, 3 if m == 0 else m % 3, :]

        def split_of(w, part):
            if w < 2:
                return (UGH, UGL)[part][:, w].rearrange("p k n -> p (k n)")
            return (FH, FL)[part][:, w - 2, :]

        @block.sync
        def _(sp):
            for w in range(NW):
                if w == 2:
                    sp.dma_start(point[:, :], point_in).then_inc(s_in, 16)
                    sp.dma_start(disc[:, :], disc_in.to_broadcast([P, G])).then_inc(s_in, 16)
                if w >= NRAW:
                    sp.wait_ge(s_wlo, w - NRAW + 1)
                src = ug_in[w] if w < 2 else fuse_in[w - 2]
                sp.dma_start(rawf[:, (w % NRAW) * D:(w % NRAW + 1) * D], src).then_inc(s_raw, 16)
                sp.wait_ge(s_raw, 16 * (w + 1))

        @block.gpsimd
        def _(pool):
            norm.pool_start(pool)
            norm.pool_power(pool, 0)
            with pool.Fori(1, 4) as i:
                norm.pool_power(pool, i)

        @block.scalar
        def _(act):
            def weight(w):
                act.wait_ge(s_raw, 16 * (w + 1))
                r = rawf[:, (w % NRAW) * D:(w % NRAW + 1) * D]
                if w >= 3:
                    act.wait_ge(s_c, w - 2)
                    nc.scalar.mul(r, r, cdis[:, w - 3:w - 2]).then_inc(s_c, 1)
                    act.wait_ge(s_c, w - 1)
                nc.scalar.copy(split_of(w, 0), r).then_inc(s_whi, 1)

            def body(i):
                for m in range(G + 1):
                    if i == 0:
                        weight(m + 2)
                    act.wait_ge(s_a, i * 7 + m + 1)
                    if m < G:
                        act.wait_ge(s_af, i * G + m + 1)
                    else:
                        act.wait_ge(s_out, i * 4 + 4)
                    nc.scalar.copy(AH[:, m, :], a_of(m)).then_inc(s_ahi, 1)
                    if m < 2 and i < 3:
                        norm.scalar_hi(act, i + 1, HALVES[m])
                if i < 2:
                    norm.scalar_norm(act, i + 2)

            norm.scalar_norm(act, 0)
            weight(0)
            weight(1)
            norm.scalar_hi(act, 0)
            norm.scalar_norm(act, 1)
            act.wait_ge(s_in, 32)
            nc.scalar.activation(cdis[:, :], disc[:, :], ACT.Exp, scale=-1.0).then_inc(s_c, 1)
            for i in range(4):
                body(i)

        @block.vector
        def _(dve):
            def weight(w):
                dve.wait_ge(s_whi, w + 1)
                nc.vector.tensor_tensor(split_of(w, 1), rawf[:, (w % NRAW) * D:(w % NRAW + 1) * D],
                                        split_of(w, 0).bitcast(F32), ALU.subtract).then_inc(s_wlo, 1)

            def leave_banks(i):
                dve.wait_ge(s_ug, i + 1)
                nc.vector.tensor_copy(a_of(0), PB[0][:, :]).then_inc(s_a, 1)
                if i > 0:
                    dve.wait_ge(s_a, i * 7)
                nc.vector.tensor_scalar(DEL[:, :], PB[1][:, :], point[:, 0:1], None, ALU.subtract).then_inc(s_del, 1)
                if i == 0:
                    weight(2)
                split(i, 0)

            def a_1_and_keep(i):
                dve.wait_ge(s_del, i + 1)
                if i > 0:
                    dve.wait_ge(s_alo, i * 7 - 2)
                nc.vector.tensor_tensor(a_of(1), a_of(0), DEL[:, :], ALU.mult).then_inc(s_a, 1)
                link = Chain(dve, s_ch, i * 2)
                link(nc.vector.scalar_tensor_tensor(KEEP[:, :], DEL[:, :], -THD, DEL[:, :], ALU.is_ge, ALU.mult))
                link(nc.vector.scalar_tensor_tensor(KEEP[:, :], DEL[:, :], THD, KEEP[:, :], ALU.is_le, ALU.mult))

            def split(i, m):
                dve.wait_ge(s_ahi, i * 7 + m + 1)
                nc.vector.tensor_tensor(AL[:, m, :], a_of(m), AH[:, m, :].bitcast(F32),
                                        ALU.subtract).then_inc(s_alo, 1)

            def add_out(i):
                for j in range(4):
                    dve.wait_ge(s_out, i * 4 + j + 5)
                    nc.vector.tensor_tensor(X[:, i * 4 + j, :], X[:, i * 4 + j, :], PB[4 + j][:, :],
                                            ALU.add).then_inc(s_xadd, 1)

            def body(i):
                if i > 0:
                    add_out(i - 1)
                a_1_and_keep(i)
                for m in range(G + 1):
                    if m + 2 <= G:
                        dve.wait_ge(s_a, i * 7 + m + 2)
                        if m > 0:
                            dve.wait_ge(s_alo, i * 7 + m)
                        nc.vector.tensor_tensor(a_of(m + 2), a_of(m + 1),
                                                (KEEP if m + 2 == 5 else DEL)[:, :], ALU.mult).then_inc(s_a, 1)
                    if m > 0:
                        if i == 0:
                            weight(m + 2)
                        split(i, m)
                    if m < 2 and i < 3:
                        norm.vector_lo(dve, i + 1, HALVES[m])
                if i < 2:
                    norm.vector_stats(dve, i + 2)
                if i < 3:
                    leave_banks(i + 1)

            norm.vector_stats(dve, 0)
            norm.vector_stats(dve, 1)
            weight(0)
            weight(1)
            norm.vector_lo(dve, 0)
            dve.wait_ge(s_in, 32)
            leave_banks(0)
            for i in range(4):
                body(i)
            add_out(3)

        @block.tensor
        def _(pe):
            def up_gate(i):
                norm.tensor_wait(pe, i)
                if i > 0:
                    pe.wait_ge(s_ch, i * 2)
                for a in range(2):
                    for k in range(KT):
                        ins = three_pass(nc, PB[a][:, :], (UGH[:, a, k, :], UGL[:, a, k, :]),
                                         (XTH[:, k, i * 512:(i + 1) * 512], XTL[:, k, i * 512:(i + 1) * 512]),
                                         k == 0, k == KT - 1)
                ins.then_inc(s_ug, 1)

            def body(i):
                for m in range(G + 1):
                    if i == 0:
                        pe.wait_ge(s_wlo, m + 3)
                    pe.wait_ge(s_alo, i * 7 + m + 1)
                    for j in range(4):
                        if m == 0:
                            pe.wait_ge(s_xadd, i * 4 + j + 1)
                        c = slice(j * P, (j + 1) * P)
                        ins = three_pass(nc, PB[4 + j][:, :], (AH[:, m, c], AL[:, m, c]),
                                         (FH[:, m, :], FL[:, m, :]), m == 0, m == G)
                        if m == G:
                            ins.then_inc(s_out, 1)
                    if m < G:
                        ins.then_inc(s_af, 1)
                    if m == 0 and i < 3:
                        norm.tensor_turn(pe, i + 1, HALVES[1])
                    if m == 4 and i < 3:
                        up_gate(i + 1)
                if i < 2:
                    norm.tensor_turn(pe, i + 2, HALVES[0])

            norm.tensor_start(pe)
            pe.sem_inc(s_af, G)
            pe.sem_inc(s_out, 4)
            pe.sem_inc(s_xadd, 4)
            norm.tensor_turn(pe, 0)
            norm.tensor_turn(pe, 1, HALVES[0])
            pe.wait_ge(s_wlo, 2)
            up_gate(0)
            for i in range(4):
                body(i)


def expert_phase(nc, X, PB, ident, ra_in, rb_in, bm_in, iota_in, out):
    NA = E8 * R16
    NH = NT // 2
    NB = NT // 4
    OB = 6
    with ExitStack() as ctx:
        sb, sem = alloc(nc, ctx)
        RA = sb("eRA", [P, KT, NA + E8])
        rb = sb("erb", [P, E8])
        bmr = sb("ebmr", [P, D])
        BH = sb("eBH", [P, D], F32R)
        BL = sb("eBL", [P, D], F32R)
        iota = sb("eiota", [P, E8])
        XT = sb("eXT", [P, 4, D])
        HS = sb("eHS", [P, NT, NA + E8])
        LG = sb("eLG", [P, NH, E8])
        nm = sb("enm", [P, NH])
        EX = sb("eEX", [P, NH, E8])
        sm = sb("esm", [P, NH])
        top = sb("etop", [P, NH, 8])
        idx = sb("eidx", [P, NH, 8], U32)
        idf = sb("eidf", [P, NH, 8])
        gs = sb("egs", [P, NH])
        gt = sb("egt", [P, NH, 2])
        w1 = sb("ew1", [P, 2, NH, E8])
        w2 = sb("ew2", [P, NH, E8])
        HW = sb("eHW", [P, 2, 4, NA])
        HTH = sb("eHTH", [P, 2, 4 * NA], F32R)
        HTL = sb("eHTL", [P, 2, 4 * NA], F32R)
        Y = sb("eY", [P, NT, D])
        s = {n: sem(f"e{n}") for n in ("in", "chain", "h", "ev", "lg", "ex", "hw", "hp", "hh", "hl",
                                       "o", "y", "st", "bh", "bl")}
        norm = BlockNorm(nc, ctx, X, ident, None, None, PB[0:4], "e")
        block = ctx.enter_context(nc.Block())

        @block.sync
        def _(sp):
            sp.dma_start(RA[:, :, :], ra_in).then_inc(s["in"], 16)
            sp.dma_start(rb[:, :], rb_in.to_broadcast([P, E8])).then_inc(s["in"], 16)
            sp.dma_start(bmr[:, :], bm_in).then_inc(s["in"], 16)
            sp.dma_start(iota[:, :], iota_in).then_inc(s["in"], 16)
            for j in range(0, NT, 2):
                sp.wait_ge(s["y"], j + 2)
                sp.dma_start(out[j:j + 2].rearrange("a p n -> p a n"), Y[:, j:j + 2, :]).then_inc(s["st"], 16)
            sp.wait_ge(s["st"], 16 * NT // 2)

        @block.gpsimd
        def _(pool):
            norm.pool_start(pool)
            for i in range(NB):
                norm.pool_power(pool, i)

        @block.scalar
        def _(act):
            def products(i):
                for t in range(4):
                    act.wait_ge(norm.s_xp, i * 4 + t + 5)
                    act.wait_ge(s["h"], i * 4 + t + 1)
                    nc.scalar.copy(XT[:, t, :], PB[t][:, :]).then_inc(norm.s_lo, 1)

            def keep(i):
                for t in range(4):
                    act.wait_ge(s["h"], i * 4 + t + 5)
                    nc.scalar.copy(HS[:, i * 4 + t, :], PB[4 + t][:, 0:NA + E8]).then_inc(s["ev"], 1)

            norm.scalar_norm(act, 0)
            for i in range(NB):
                if i + 1 < NB:
                    norm.scalar_norm(act, i + 1)
                products(i)
                if i > 0:
                    keep(i - 1)
            act.wait_ge(s["in"], 64)
            nc.scalar.copy(BH[:, :], bmr[:, :]).then_inc(s["bh"], 1)
            act.wait_ge(s["lg"], 1)
            nc.scalar.activation(EX[:, :, :], LG[:, :, :], ACT.Exp).then_inc(s["ex"], 1)
            keep(NB - 1)
            for i in range(NB):
                if i == 1:
                    act.wait_ge(s["hp"], 2)
                    nc.scalar.copy(HTH[:, 1, :], PB[1][:, :]).then_inc(s["hh"], 1)
                    act.wait_ge(s["lg"], 2)
                    nc.scalar.activation(EX[:, :, :], LG[:, :, :], ACT.Exp).then_inc(s["ex"], 1)
                else:
                    act.wait_ge(s["hp"], i + 1)
                    nc.scalar.copy(HTH[:, i % 2, :], PB[i % 2][:, :]).then_inc(s["hh"], 1)

        @block.vector
        def _(dve):
            def gates(half):
                link = Chain(dve, s["chain"], half * 13)
                hs = slice(half * NH, (half + 1) * NH)
                dve.wait_ge(s["ev"], (half + 1) * NH)
                link(nc.vector.tensor_tensor(LG[:, :, :], HS[:, hs, NA:NA + E8],
                                             rb[:, :].unsqueeze(1).to_broadcast([P, NH, E8]), ALU.add))
                link(nc.vector.tensor_reduce(nm[:, :], LG[:, :, :], axis=AXX, op=ALU.max))
                nc.vector.tensor_tensor(LG[:, :, :], LG[:, :, :], nm[:, :].unsqueeze(2).to_broadcast([P, NH, E8]),
                                        ALU.subtract).then_inc(s["lg"], 1)
                dve.wait_ge(s["ex"], half + 1)
                link(nc.vector.tensor_reduce(sm[:, :], EX[:, :, :], axis=AXX, op=ALU.add))
                link(nc.vector.reciprocal(sm[:, :], sm[:, :]))
                link(nc.vector.tensor_tensor(EX[:, :, :], EX[:, :, :], sm[:, :].unsqueeze(2).to_broadcast([P, NH, E8]),
                                             ALU.mult))
                for t in range(NH):
                    ins = nc.vector.max(top[:, t, :], EX[:, t, :])
                link(ins)
                for t in range(NH):
                    ins = nc.vector.max_index(idx[:, t, :], top[:, t, :], EX[:, t, :])
                link(ins)
                nc.vector.tensor_copy(idf[:, :, :], idx[:, :, :])
                link(nc.vector.tensor_tensor(gs[:, :], top[:, :, 0], top[:, :, 1], ALU.add))
                link(nc.vector.reciprocal(gs[:, :], gs[:, :]))
                link(nc.vector.scalar_tensor_tensor(gt[:, :, :], top[:, :, 0:2], 0.5,
                                                    gs[:, :].unsqueeze(2).to_broadcast([P, NH, 2]),
                                                    ALU.mult, ALU.mult))
                w = (w1[:, half, :, :], w2[:, :, :])
                for c in range(2):
                    ins = nc.vector.tensor_tensor(w[c], iota[:, :].unsqueeze(1).to_broadcast([P, NH, E8]),
                                                  idf[:, :, c:c + 1].to_broadcast([P, NH, E8]), ALU.is_equal)
                link(ins)
                for c in range(2):
                    ins = nc.vector.tensor_tensor(w[c], w[c], gt[:, :, c:c + 1].to_broadcast([P, NH, E8]), ALU.mult)
                link(ins)
                link(nc.vector.tensor_tensor(w[0], w[0], w[1], ALU.add))


            def weigh(i):
                if i >= 2:
                    dve.wait_ge(s["hp"], i - 1)
                half, t = i // 2, i % 2 * 4
                nc.vector.tensor_tensor(HW[:, i % 2, :, :].rearrange("p t (e r) -> p t e r", e=E8),
                                        HS[:, 4 * i:4 * i + 4, 0:NA].rearrange("p t (e r) -> p t e r", e=E8),
                                        w1[:, half, t:t + 4, :].unsqueeze(3).to_broadcast([P, 4, E8, R16]),
                                        ALU.mult).then_inc(s["hw"], 1)

            def split(i):
                dve.wait_ge(s["hh"], i + 1)
                nc.vector.tensor_tensor(HTL[:, i % 2, :], PB[i % 2][:, :], HTH[:, i % 2, :].bitcast(F32),
                                        ALU.subtract).then_inc(s["hl"], 1)

            def add(i):
                for j in range(4 * i, 4 * i + 4):
                    dve.wait_ge(s["o"], j + 1)
                    nc.vector.tensor_tensor(Y[:, j, :], PB[2 + j % OB][:, :], X[:, j, :], ALU.add).then_inc(s["y"], 1)

            for i in range(NB):
                norm.vector_stats(dve, i)
            dve.wait_ge(s["in"], 64)
            gates(0)
            dve.wait_ge(s["bh"], 1)
            nc.vector.tensor_tensor(BL[:, :], bmr[:, :], BH[:, :].bitcast(F32), ALU.subtract).then_inc(s["bl"], 1)
            weigh(0)
            weigh(1)
            split(0)
            split(1)
            gates(1)
            add(0)
            weigh(2)
            weigh(3)
            add(1)
            split(2)
            split(3)
            add(2)
            add(3)

        @block.tensor
        def _(pe):
            norm.tensor_start(pe)
            pe.sem_inc(s["h"], 4)
            norm.tensor_turn(pe, 0)
            pe.wait_ge(s["in"], 64)
            for i in range(NB):
                if i + 1 < NB:
                    norm.tensor_turn(pe, i + 1)
                for t in range(4):
                    pe.wait_ge(norm.s_lo, i * 4 + t + 5)
                    if i > 0:
                        pe.wait_ge(s["ev"], i * 4 + t - 3)
                    for k in range(KT):
                        ins = nc.tensor.matmul(PB[4 + t][:, 0:NA + E8], XT[:, t, k * P:(k + 1) * P], RA[:, k, :],
                                               start=k == 0, stop=k == KT - 1)
                    ins.then_inc(s["h"], 1)

            def turn(i):
                pe.wait_ge(s["hw"], i + 1)
                if i >= 2:
                    pe.wait_ge(s["hl"], i - 1)
                else:
                    pe.wait_ge(norm.s_lo, NT + 4)
                for t in range(4):
                    ins = nc.tensor.transpose(PB[i % 2][:, t * NA:(t + 1) * NA], HW[:, i % 2, t, :], ident[:, :])
                ins.then_inc(s["hp"], 1)

            def output(i):
                pe.wait_ge(s["hl"], i + 1)
                for j in range(4 * i, 4 * i + 4):
                    if j >= OB:
                        pe.wait_ge(s["y"], j - OB + 1)
                    else:
                        pe.wait_ge(s["ev"], NT)
                    c = slice(j % 4 * NA, (j % 4 + 1) * NA)
                    three_pass(nc, PB[2 + j % OB][:, :], (HTH[:, i % 2, c], HTL[:, i % 2, c]),
                               (BH[:, :], BL[:, :]), True, True).then_inc(s["o"], 1)

            turn(0)
            turn(1)
            pe.wait_ge(s["bl"], 1)
            output(0)
            output(1)
            turn(2)
            turn(3)
            output(2)
            output(3)


def build(nc, d, out):
    with ExitStack() as ctx:
        X = ctx.enter_context(nc.sbuf_tensor("X", [P, NT, D], F32))
        ident = ctx.enter_context(nc.sbuf_tensor("ident", [P, P], F32))
        PB = [ctx.enter_context(nc.psum_tensor(f"PB{i}", [P, D], F32)) for i in range(8)]
        attention_phase(nc, X, PB, ident, d["x"], d["wqkvo"], d["rope"], d["mask"], d["ident"])
        with ExitStack() as c2:
            XTH = c2.enter_context(nc.sbuf_tensor("XTH", [P, KT, TOK], F32R))
            XTL = c2.enter_context(nc.sbuf_tensor("XTL", [P, KT, TOK], F32R))
            coded_swiglu_phase(nc, X, PB, ident, XTH, XTL, d["gu0"], d["d0"], d["sgu0"], d["sd0"])
            taylor_phase(nc, X, PB, ident, XTH, XTL, d["ug"], d["point"], d["fuse"], d["disc"])
            swiglu_phase(nc, X, PB, XTH, XTL, d["gu1"], d["d1"])
        expert_phase(nc, X, PB, ident, d["ra"], d["rb"], d["bm"], d["iota"], out)


def layouts(np, a):
    c = np.ascontiguousarray

    def rows(w):
        return c(w.reshape(KT, P, -1).transpose(1, 0, 2))

    def gate_up(g, u, F):
        def one(w):
            w = np.concatenate([w, np.zeros((F - w.shape[0], D), w.dtype)]) if w.shape[0] < F else w
            return w.T.reshape(KT, P, F // 256, 2, P).transpose(2, 3, 1, 0, 4)
        return c(np.stack([one(g), one(u)], axis=3)).reshape(F // 256, 2, P, 2 * KT * P)

    def down(w, F):
        w = w.T
        w = np.concatenate([w, np.zeros((F - w.shape[0], D), w.dtype)]) if w.shape[0] < F else w
        return c(w.reshape(F // 256, 2, P, D).transpose(0, 2, 1, 3)).reshape(F // 256, P, 2 * D)

    def scale_gu(g, u):
        def one(s):
            return s.reshape(F0 // 256, 2, P, KT).transpose(2, 0, 1, 3)
        return c(np.stack([one(g), one(u)], axis=3)).reshape(P, F0 // 256 * 16)

    inv = (1.0 / 10000.0 ** (np.arange(0, HD, 2)[:HD // 2].astype(np.float32) / HD))
    f = np.outer(np.arange(S), inv).astype(np.float32)
    cos, sin = np.cos(f).astype(np.float32), np.sin(f).astype(np.float32)
    cos2 = np.repeat(cos, 2, axis=1)
    sin2 = np.stack([-sin, sin], axis=-1).reshape(S, HD)
    q = np.float32(HD ** -0.5)
    rope = np.stack([cos2 * q, sin2 * q, cos2, sin2]).astype(np.float32).reshape(4, TPB, P, HD)
    mask = np.where(np.arange(P)[None, :] > np.arange(P)[:, None], np.float32(NEG), np.float32(0))
    fuse = a["L1_attn_fuse_weight"]
    return {
        "x": c(a["L0_attn_x"].reshape(B, TPB, P, D).transpose(0, 2, 1, 3)),
        "wqkvo": np.stack([rows(a[f"L0_attn_w{n}"]) for n in "qkvo"]),
        "rope": c(rope.transpose(2, 0, 1, 3)),
        "mask": mask.astype(np.float32),
        "ident": np.eye(P, dtype=np.float32),
        "gu0": gate_up(a["L0_ffn_gate_q"], a["L0_ffn_up_q"], F0),
        "d0": down(a["L0_ffn_down_q"], F0),
        "sgu0": scale_gu(a["L0_ffn_gate_s"], a["L0_ffn_up_s"]),
        "sd0": c(a["L0_ffn_down_s"].T).reshape(F0 // 256, 2 * D),
        "ug": np.stack([rows(a["L1_attn_up_w"].T).reshape(P, -1), rows(a["L1_attn_gate_w"].T).reshape(P, -1)]),
        "point": c(a["L1_attn_local_point"].reshape(P, 1)),
        "fuse": np.stack([c(a["L1_attn_local_approx_output"].T)] + [c(fuse[:, :, m].T) for m in range(G)]),
        "disc": c(a["L1_attn_discount_factor"].reshape(1, G)),
        "gu1": gate_up(a["L1_attn_ffn_gate_w"], a["L1_attn_ffn_up_w"], F1),
        "d1": down(a["L1_attn_ffn_down_w"], F1),
        "ra": np.concatenate([rows(a["L1_ffn_A"].reshape(E8 * R16, D).T), rows(a["L1_ffn_router_w"].T)], axis=2),
        "rb": c(a["L1_ffn_router_b"].reshape(1, E8)),
        "bm": c(a["L1_ffn_Bm"].transpose(0, 2, 1)).reshape(E8 * R16, D),
        "iota": np.tile(np.arange(E8, dtype=np.float32), (P, 1)),
    }


def program(nc, arrays):
    d = {n: nc.dram_tensor(f"in_{n}", v.shape, mybir.dt.from_np(v.dtype), kind="ExternalInput").ap()
         for n, v in arrays.items()}
    out = nc.dram_tensor("out_0", (NT, P, D), F32, kind="ExternalOutput").ap()
    build(nc, d, out)


def kernel(**inputs):
    import numpy as np
    import concourse.bacc as bacc
    from concourse.bass_utils import run_bass_kernel_spmd

    arrays = layouts(np, {n: np.asarray(v) for n, v in inputs.items()})
    nc = bacc.Bacc("TRN2", target_bir_lowering=False, num_devices=1)
    program(nc, arrays)
    r = run_bass_kernel_spmd(nc, [{f"in_{n}": v for n, v in arrays.items()}], core_ids=[0])
    return r.results[0]["out_0"].reshape(B, S, D)
```
